# Optimizing a Trainium2 kernel written in Bass

```python
import numpy as np
import jax
import jax.numpy as jnp

def _softmax(x, axis=-1):
    return jax.nn.softmax(x, axis=axis)

def _gelu(x):
    return jax.nn.gelu(x, approximate=True)

def _silu(x):
    return jax.nn.silu(x)

def _sigmoid(x):
    return jax.nn.sigmoid(x)

def _layernorm(x, axis=-1, eps=1e-05):
    m = jnp.mean(x, axis=axis, keepdims=True)
    v = jnp.var(x, axis=axis, keepdims=True)
    return (x - m) / jnp.sqrt(v + eps)

def _scatter_add(tgt, idx, src, axis=0):
    return tgt.at[idx].add(src)

def _segment_sum(src, seg, n):
    return jax.ops.segment_sum(src, seg, n)
kernel_name = 'mk_decoder_postln_d1_seqx_r8_a095b8'

def setup_inputs(seed: int=0):
    np.random.seed(seed)
    _w = jnp.asarray

    def _rec_inputs():
        import jax
        import jax.numpy as jnp
        _rk = jax.random.key(seed)
        x = -0.0002928 + 1 * jax.random.normal(jax.random.fold_in(_rk, 1), (4, 512, 128), jnp.float32)
        _lenS = 512 - jax.random.randint(jax.random.fold_in(_rk, 7), (4,), 0, max(1, 512 // 4) + 1, jnp.int32)
        _lenS2 = 77 - jax.random.randint(jax.random.fold_in(_rk, 8), (4,), 0, max(1, 77 // 4) + 1, jnp.int32)
        _ctx_1024P = jax.random.normal(jax.random.fold_in(_rk, 11), (4, 16, 128), jnp.float32)
        _ctx_1024c = jax.random.dirichlet(jax.random.fold_in(_rk, 511), 0.3 * jnp.ones((16,), jnp.float32), (4, 77))
        _ctx_1024t = jnp.einsum('bsk,bkd->bsd', _ctx_1024c, _ctx_1024P)
        _ctx_1024t = _ctx_1024t * jax.lax.rsqrt(jnp.mean(jnp.square(_ctx_1024t)) + 1e-12) * 0.953939
        ctx_1024 = -1.39393e-06 + 0.999914 * (_ctx_1024t + 0.3 * jax.random.normal(jax.random.fold_in(_rk, 611), (4, 77, 128), jnp.float32))
        return (x, ctx_1024)
    x, ctx_1024 = _rec_inputs()

    def _L0_attn_setup():
        import math
        import jax, jax.numpy as jnp
        import numpy as np
        B, S, D, H = (4, 128, 128, 16)
        HD = D // H
        EPS = 1e-05

        def _sinusoidal_encodings(length, d):
            pos = jnp.arange(length, dtype=jnp.float32)
            inv_freq = 1.0 / 10000.0 ** (jnp.arange(0.0, d, 2.0) / d)
            angles = pos[:, None] * inv_freq[None, :]
            enc = jnp.zeros((length, d), dtype=jnp.float32)
            enc = enc.at[:, 0::2].set(jnp.sin(angles))
            enc = enc.at[:, 1::2].set(jnp.cos(angles))
            return enc

        def _relative_shift(emb):
            b, h, l1, l2 = emb.shape
            padded = jnp.concatenate([jnp.zeros((b, h, l1, 1), emb.dtype), emb], axis=-1)
            padded = padded.reshape(b, h, l2 + 1, l1)
            return padded[:, :, 1:, :].reshape(b, h, l1, l2)
        key = jax.random.key(seed)
        ks = jax.random.split(key, 12)
        s = 0.02
        inp = {'x': jax.random.normal(ks[0], (B, S, D), dtype=jnp.float32), 'Wq': jax.random.normal(ks[1], (D, D), dtype=jnp.float32) * s, 'bq': jnp.zeros((D,), jnp.float32), 'Wk': jax.random.normal(ks[2], (D, D), dtype=jnp.float32) * s, 'bk': jnp.zeros((D,), jnp.float32), 'Wv': jax.random.normal(ks[3], (D, D), dtype=jnp.float32) * s, 'bv': jnp.zeros((D,), jnp.float32), 'Wpos': jax.random.normal(ks[4], (D, D), dtype=jnp.float32) * s, 'Wf': jax.random.normal(ks[5], (D, D), dtype=jnp.float32) * s, 'bf': jnp.zeros((D,), jnp.float32), 'u': jax.random.normal(ks[6], (H, HD), dtype=jnp.float32) * s, 'v': jax.random.normal(ks[7], (H, HD), dtype=jnp.float32) * s, 'gamma': jnp.ones((D,), jnp.float32), 'beta': jnp.zeros((D,), jnp.float32)}
        return inp
    _L0_attn_all = _L0_attn_setup()
    _L0_attn_in = {k: v for k, v in _L0_attn_all.items() if k in ('Wq', 'bq', 'Wk', 'bk', 'Wv', 'bv', 'Wpos', 'Wf', 'bf', 'u', 'v', 'gamma', 'beta')}
    del _L0_attn_all

    def _L0_xattn_setup():
        import jax, jax.numpy as jnp
        import numpy as np
        DIM = 128
        HEADS = 16
        HEAD_DIM = DIM // HEADS
        SCALE = HEAD_DIM ** (-0.5)
        key = jax.random.key(seed)
        ks = jax.random.split(key, 7)
        b, n = (2, 256)
        x1 = jax.random.normal(ks[0], (b, n, DIM), dtype=jnp.float32)
        x2 = jax.random.normal(ks[1], (b, n, DIM), dtype=jnp.float32)
        s = DIM ** (-0.5)
        wq = jax.random.normal(ks[2], (DIM, DIM), dtype=jnp.float32) * s
        wk = jax.random.normal(ks[3], (DIM, DIM), dtype=jnp.float32) * s
        wv = jax.random.normal(ks[4], (DIM, DIM), dtype=jnp.float32) * s
        wo = jax.random.normal(ks[5], (DIM, DIM), dtype=jnp.float32) * s
        bo = jax.random.normal(ks[6], (DIM,), dtype=jnp.float32) * 0.01
        return {'x1': x1, 'x2': x2, 'wq': wq, 'wk': wk, 'wv': wv, 'wo': wo, 'bo': bo}
    _L0_xattn_all = _L0_xattn_setup()
    _L0_xattn_in = {k: v for k, v in _L0_xattn_all.items() if k in ('wq', 'wk', 'wv', 'wo', 'bo')}
    del _L0_xattn_all

    def _L0_ffn_setup():
        import jax, jax.numpy as jnp
        import numpy as np
        B, S, F, E, K = (4, 128, 128, 8, 2)
        H = 4 * F
        key = jax.random.key(seed)
        ks = jax.random.split(key, 7)

        def xavier(k, shape):
            fan_in, fan_out = (shape[-2], shape[-1])
            scale = jnp.sqrt(6.0 / (fan_in + fan_out))
            return jax.random.uniform(k, shape, jnp.float32, -scale, scale)
        return {'x': jax.random.normal(ks[0], (B, S, F), jnp.float32), 'Wg': xavier(ks[1], (F, E)), 'bg': jnp.zeros((E,), jnp.float32), 'W1': xavier(ks[2], (E, F, H)), 'b1': jnp.zeros((E, H), jnp.float32), 'W2': xavier(ks[3], (E, H, F)), 'b2': jnp.zeros((E, F), jnp.float32)}
    _L0_ffn_all = _L0_ffn_setup()
    _L0_ffn_in = {k: v for k, v in _L0_ffn_all.items() if k in ('Wg', 'bg', 'W1', 'b1', 'W2', 'b2')}
    del _L0_ffn_all
    return {'x': x, 'ctx_1024': ctx_1024, 'L0_attn_Wq': _L0_attn_in['Wq'], 'L0_attn_bq': _L0_attn_in['bq'], 'L0_attn_Wk': _L0_attn_in['Wk'], 'L0_attn_bk': _L0_attn_in['bk'], 'L0_attn_Wv': _L0_attn_in['Wv'], 'L0_attn_bv': _L0_attn_in['bv'], 'L0_attn_Wpos': _L0_attn_in['Wpos'], 'L0_attn_Wf': _L0_attn_in['Wf'], 'L0_attn_bf': _L0_attn_in['bf'], 'L0_attn_u': _L0_attn_in['u'], 'L0_attn_v': _L0_attn_in['v'], 'L0_attn_gamma': _L0_attn_in['gamma'], 'L0_attn_beta': _L0_attn_in['beta'], 'L0_xattn_wq': _L0_xattn_in['wq'], 'L0_xattn_wk': _L0_xattn_in['wk'], 'L0_xattn_wv': _L0_xattn_in['wv'], 'L0_xattn_wo': _L0_xattn_in['wo'], 'L0_xattn_bo': _L0_xattn_in['bo'], 'L0_ffn_Wg': _L0_ffn_in['Wg'], 'L0_ffn_bg': _L0_ffn_in['bg'], 'L0_ffn_W1': _L0_ffn_in['W1'], 'L0_ffn_b1': _L0_ffn_in['b1'], 'L0_ffn_W2': _L0_ffn_in['W2'], 'L0_ffn_b2': _L0_ffn_in['b2']}

def reference(x, ctx_1024, L0_attn_Wq, L0_attn_bq, L0_attn_Wk, L0_attn_bk, L0_attn_Wv, L0_attn_bv, L0_attn_Wpos, L0_attn_Wf, L0_attn_bf, L0_attn_u, L0_attn_v, L0_attn_gamma, L0_attn_beta, L0_xattn_wq, L0_xattn_wk, L0_xattn_wv, L0_xattn_wo, L0_xattn_bo, L0_ffn_Wg, L0_ffn_bg, L0_ffn_W1, L0_ffn_b1, L0_ffn_W2, L0_ffn_b2):
    import jax
    import jax.numpy as jnp

    def _L0_attn_ref(x, Wq, bq, Wk, bk, Wv, bv, Wpos, Wf, bf, u, v, gamma, beta):
        import math
        import jax, jax.numpy as jnp
        import numpy as np
        B, S, D, H = (4, 128, 128, 16)
        HD = D // H
        EPS = 1e-05

        def _sinusoidal_encodings(length, d):
            pos = jnp.arange(length, dtype=jnp.float32)
            inv_freq = 1.0 / 10000.0 ** (jnp.arange(0.0, d, 2.0) / d)
            angles = pos[:, None] * inv_freq[None, :]
            enc = jnp.zeros((length, d), dtype=jnp.float32)
            enc = enc.at[:, 0::2].set(jnp.sin(angles))
            enc = enc.at[:, 1::2].set(jnp.cos(angles))
            return enc

        def _relative_shift(emb):
            b, h, l1, l2 = emb.shape
            padded = jnp.concatenate([jnp.zeros((b, h, l1, 1), emb.dtype), emb], axis=-1)
            padded = padded.reshape(b, h, l2 + 1, l1)
            return padded[:, :, 1:, :].reshape(b, h, l1, l2)
        b, s, d = x.shape
        mu = jnp.mean(x, axis=-1, keepdims=True)
        var = jnp.mean((x - mu) ** 2, axis=-1, keepdims=True)
        xn = (x - mu) * jax.lax.rsqrt(var + EPS) * gamma + beta
        pe = _sinusoidal_encodings(s, d)
        q = (xn @ Wq + bq).reshape(b, s, H, HD)
        k = (xn @ Wk + bk).reshape(b, s, H, HD)
        val = (xn @ Wv + bv).reshape(b, s, H, HD)
        p = (pe @ Wpos).reshape(s, H, HD)
        AC = jnp.einsum('bihd,bjhd->bhij', q + u, k)
        BD = jnp.einsum('bihd,jhd->bhij', q + v, p)
        BD = _relative_shift(BD)
        attn = jax.nn.softmax((AC + BD) / math.sqrt(d), axis=-1)
        out = jnp.einsum('bhij,bjhd->bihd', attn, val).reshape(b, s, d)
        out = out @ Wf + bf
        return out

    def _L0_xattn_ref(x1, x2, wq, wk, wv, wo, bo):
        import jax, jax.numpy as jnp
        import numpy as np
        DIM = 128
        HEADS = 16
        HEAD_DIM = DIM // HEADS
        SCALE = HEAD_DIM ** (-0.5)
        b, n, _ = x1.shape
        m = x2.shape[1]
        q = (x1 @ wq.T).reshape(b, n, HEADS, HEAD_DIM).transpose(0, 2, 1, 3)
        k = (x2 @ wk.T).reshape(b, m, HEADS, HEAD_DIM).transpose(0, 2, 1, 3)
        v = (x2 @ wv.T).reshape(b, m, HEADS, HEAD_DIM).transpose(0, 2, 1, 3)
        dots = jnp.einsum('bhnd,bhmd->bhnm', q, k) * SCALE
        attn = jax.nn.softmax(dots, axis=-1)
        out = jnp.einsum('bhnm,bhmd->bhnd', attn, v)
        out = out.transpose(0, 2, 1, 3).reshape(b, n, DIM)
        return out @ wo.T + bo

    def _L0_ffn_ref(x, Wg, bg, W1, b1, W2, b2):
        import jax, jax.numpy as jnp
        import numpy as np
        B, S, F, E, K = (4, 128, 128, 8, 2)
        H = 4 * F
        gate_probs = jax.nn.softmax(x @ Wg + bg, axis=-1)
        k = K
        _, top_idx = jax.lax.top_k(gate_probs, k)
        expert_mask = jax.nn.one_hot(top_idx, gate_probs.shape[-1], dtype=gate_probs.dtype).sum(-2)
        selected = gate_probs * expert_mask
        selected = selected / (selected.sum(-1, keepdims=True) + 1e-08)
        h = jax.nn.gelu(jnp.einsum('bsf,efh->bseh', x, W1) + b1)
        expert_out = jnp.einsum('bseh,ehf->bsef', h, W2) + b2[None, None]
        return jnp.einsum('bsef,bse->bsf', expert_out, selected)
    x = _layernorm(x + _L0_attn_ref(x, L0_attn_Wq, L0_attn_bq, L0_attn_Wk, L0_attn_bk, L0_attn_Wv, L0_attn_bv, L0_attn_Wpos, L0_attn_Wf, L0_attn_bf, L0_attn_u, L0_attn_v, L0_attn_gamma, L0_attn_beta), axis=-1)
    x = _layernorm(x + _L0_xattn_ref(x, ctx_1024, L0_xattn_wq, L0_xattn_wk, L0_xattn_wv, L0_xattn_wo, L0_xattn_bo), axis=-1)
    x = _layernorm(x + _L0_ffn_ref(x, L0_ffn_Wg, L0_ffn_bg, L0_ffn_W1, L0_ffn_b1, L0_ffn_W2, L0_ffn_b2), axis=-1)
    return x

_drawn_inputs = setup_inputs


def setup_inputs(seed=0):
    import zlib

    import numpy as np

    out = dict(_drawn_inputs(seed))
    spreads = {'L0_attn_bq': (0.0, 0.8),
     'L0_attn_bk': (0.0, 2.0),
     'L0_attn_bv': (0.0, 0.1),
     'L0_attn_bf': (0.0, 0.1),
     'L0_attn_gamma': (1.0, 0.6),
     'L0_attn_beta': (0.0, 0.675),
     'L0_ffn_bg': (0.0, 0.1),
     'L0_ffn_b1': (0.0, 0.1),
     'L0_ffn_b2': (0.0, 0.1)}
    factors = {'L0_attn_Wq': 8.0,
     'L0_attn_Wk': 8.0,
     'L0_attn_Wv': 4.607,
     'L0_attn_Wpos': 8.0,
     'L0_attn_u': 8.0,
     'L0_attn_v': 41.754}
    for name, (base, spread) in spreads.items():
        noise = np.random.default_rng([zlib.crc32(name.encode()), seed]).standard_normal(out[name].shape)
        drawn = base * np.exp(spread * noise) if base else spread * noise
        out[name] = jnp.asarray(drawn.astype(out[name].dtype))
    for name, factor in factors.items():
        out[name] = (out[name] * factor).astype(out[name].dtype)
    return out
```

```python
from contextlib import ExitStack

import numpy as np

import concourse.bass as bass
from concourse import mybir

F32 = mybir.dt.float32
F32R = mybir.dt.float32r
U32 = mybir.dt.uint32
ALU = mybir.AluOpType
ACT = mybir.ActivationFunctionType
AX_X = mybir.AxisListType.X

P = 128
B, S, D = 4, 512, 128
H, HD = 16, 8
NT = B * S // P
QB = S // P
HG = 4
BAND = 32
M2 = 77
E = 8
HID = 4 * D
EPS = 1e-5
ZONE = P + 2
SCALE = float(D) ** -0.5
SCALE2 = float(HD) ** -0.5
ITS = B * HG
UPP = 2 * 4 * QB
WST = 2 * P + 4


def zone(i):
    return P * i, min(ZONE, S - P * i)


def decoder_kernel(nc, t, out):
    with ExitStack() as ctx:
        def sb(name, shape, dt=F32):
            return ctx.enter_context(nc.sbuf_tensor(name, shape, dt))

        def sem(name):
            return ctx.enter_context(nc.semaphore(name))

        ident = sb("ident", [P, P])
        epsc = sb("epsc", [P, 1])
        attn = sb("attn", [P, NT, D])
        psum = ctx.enter_context(nc.psum_tensor("psum", [P, 8, 512], F32))

        self_attention(nc, t, ident, epsc, attn, psum)
        with ExitStack() as late:
            x2 = late.enter_context(nc.sbuf_tensor("x2", [P, NT, D], F32))
            x2T = late.enter_context(nc.sbuf_tensor("x2T", [P, B * S], F32))
            cross_attention(nc, t, ident, epsc, attn, x2, x2T, psum)
            experts(nc, t, ident, epsc, x2, x2T, psum, out)


def self_attention(nc, t, ident, epsc, attn, psum):
    with ExitStack() as ctx:
        def sb(name, shape, dt=F32):
            return ctx.enter_context(nc.sbuf_tensor(name, shape, dt))

        def sem(name):
            return ctx.enter_context(nc.semaphore(name))

        xnT = sb("xnT", [P, B * S])
        v_all = sb("v_all", [P, NT, D])
        tabs = sb("tabs", [P, 2, 2, S], F32R)
        cs = sb("cs", [P, 2, S])
        wpf = sb("wpf", [P, HG, 2, P], F32R)
        psz = sb("psz", [P, HG, 4], F32R)
        negc = sb("negc", [P, 2])
        maskU = sb("maskU", [P, ZONE], U32)
        maskS = sb("maskS", [P, ZONE])
        wz = sb("wz", [P, 4, 2, P], F32R)

        with ExitStack() as ca:
            def sba(name, shape, dt=F32):
                return ca.enter_context(nc.sbuf_tensor(name, shape, dt))

            x = sba("x_in", [P, NT, D])
            xh = sba("xh", [P, NT, D])
            st = sba("ln_st", [P, NT, 6])
            mv = sba("ln_mv", [P, NT, 2])
            rstd = sba("ln_rstd", [P, NT])
            gb = sba("gb", [P, 2])
            wv = sba("wv", [P, P])
            bvb = sba("bvb", [P, P])
            wposr = sba("wposr", [P, HG, 2, P])
            wposh = sba("wposh", [P, HG, 2, P], F32R)
            wposc = sba("wposc", [P, HG, P])
            tabr = sba("tabr", [P, 2, S])
            peS = sba("peS", [P, 1])
            pSr = sba("pSr", [P, HG])
            pSh = sba("pSh", [P, HG], F32R)
            pSt = sba("pSt", [P, HG])
            bandm = sba("bandm", [P, 4])
            x_in = sem("a_x_loaded")
            c_in = sem("a_consts_loaded")
            w_in = sem("a_weights_loaded")
            stat = sem("a_stats")
            sq = sem("a_sqrt")
            rs = sem("a_rstd")
            xhs = sem("a_xhat")
            tp = sem("a_transposed")
            xe = sem("a_xnT")
            vp = sem("a_v_psum")
            ve = sem("a_v")
            sp_hi = sem("a_split_high")
            sp_lo = sem("a_split_done")
            pp = sem("a_pos_psum")
            epsm = sem("a_eps")
            with nc.Block() as block:
                @block.sync
                def _(sp):
                    for q in range(4):
                        sp.dma_start(x[:, 4 * q:4 * q + 4, :],
                                     t["x"][q].rearrange("(t p) d -> p t d", p=P)).then_inc(x_in, 16)
                    for dst, src in ((ident[:], t["ident"]), (gb[:], t["gb"]), (negc[:], t["negc"]),
                                     (bandm[:], t["bandm"]), (maskU[:], t["maskU"]), (maskS[:], t["maskS"]),
                                     (peS[:], t["peS"])):
                        sp.dma_start(dst, src).then_inc(c_in, 16)
                    sp.dma_start(cs[:], t["cs"]).then_inc(c_in, 16)

                @block.scalar
                def _(act):
                    act.dma_start(wv[:], t["wv"]).then_inc(w_in, 16)
                    act.dma_start(bvb[:], t["bv"].to_broadcast([P, P])).then_inc(w_in, 16)
                    act.dma_start(tabr[:], t["tabs"]).then_inc(w_in, 16)
                    act.dma_start(wposr[:], t["wposT"].rearrange("g v p c -> p g v c")).then_inc(w_in, 16)
                    act.dma_start(wposc[:], t["wposC"].rearrange("g c r -> c g r")).then_inc(w_in, 16)
                    act.wait_ge(epsm, 1)
                    act.wait_ge(stat, NT)
                    act.activation(rstd[:], mv[:, :, 1], ACT.Sqrt, bias=epsc[:, 0:1]).then_inc(sq, 1)
                    act.wait_ge(c_in, 16 * 8)
                    for q in range(4):
                        act.wait_ge(tp, q + 1)
                        act.activation(xnT[:, q * 512:(q + 1) * 512], psum[:, q, :], ACT.Identity,
                                       bias=gb[:, 1:2], scale=gb[:, 0:1]).then_inc(xe, 1)

                @block.gpsimd
                def _(pool):
                    pool.memset(epsc[:], EPS).then_inc(epsm, 1)

                @block.vector
                def _(v):
                    for i in range(NT):
                        if i % 4 == 0:
                            v.wait_ge(x_in, 64)
                        v.bn_stats(st[:, i, :], x[:, i, :]).then_inc(rs, 1)
                    v.wait_ge(rs, NT)
                    for i in range(NT):
                        v.bn_aggr(mv[:, i, :], st[:, i, :]).then_inc(stat, 1)
                    v.wait_ge(sq, 1)
                    v.reciprocal(rstd[:], rstd[:]).then_inc(rs, 1)
                    v.wait_ge(rs, NT + 1)
                    for i in range(NT):
                        v.tensor_scalar(xh[:, i, :], x[:, i, :], mv[:, i, 0:1], rstd[:, i:i + 1],
                                        ALU.subtract, ALU.mult).then_inc(xhs, 1)
                    v.wait_ge(w_in, 16 * 5)
                    v.wait_ge(c_in, 16 * 8)
                    v.tensor_copy(tabs[:, :, 0, :], tabr[:]).then_inc(sp_hi, 1)
                    v.tensor_copy(wposh[:], wposr[:]).then_inc(sp_hi, 1)
                    v.wait_ge(pp, 1)
                    v.tensor_copy(pSr[:], psum[:, 7, 0:HG]).then_inc(sp_hi, 1)
                    v.wait_ge(sp_hi, 3)
                    v.tensor_copy(pSh[:], pSr[:]).then_inc(sp_hi, 1)
                    v.tensor_tensor(tabs[:, :, 1, :], tabr[:], tabs[:, :, 0, :].bitcast(F32),
                                    ALU.subtract).then_inc(sp_lo, 1)
                    wf = wpf[:].rearrange("p g v c -> p (g v c)")
                    v.scalar_tensor_tensor(wf, wposh[:].rearrange("p g v c -> p (g v c)").bitcast(F32),
                                           negc[:, 1:2], wposr[:].rearrange("p g v c -> p (g v c)"),
                                           ALU.mult, ALU.add).then_inc(sp_lo, 1)
                    v.wait_ge(sp_hi, 4)
                    v.scalar_tensor_tensor(pSt[:], pSh[:].bitcast(F32), negc[:, 1:2], pSr[:],
                                           ALU.mult, ALU.add).then_inc(sp_lo, 1)
                    v.wait_ge(sp_lo, 3)
                    for g in range(HG):
                        v.tensor_scalar(psz[:, g, :], bandm[:], pSt[:, g:g + 1], None,
                                        ALU.mult).then_inc(sp_lo, 1)
                    for q in range(4):
                        v.wait_ge(vp, q + 1)
                        v.tensor_tensor(v_all[:, 4 * q:4 * q + 4, :],
                                        psum[:, q + 4, :].rearrange("p (t d) -> p t d", t=4),
                                        bvb[:].rearrange("p (a d) -> p a d", a=1).to_broadcast([P, 4, D]),
                                        ALU.add).then_inc(ve, 1)

                @block.tensor
                def _(pe):
                    pe.wait_ge(c_in, 16 * 8)
                    pe.wait_ge(w_in, 16 * 5)
                    for g in range(HG):
                        last = pe.matmul(psum[:, 7, g:g + 1], wposc[:, g, :], peS[:], start=True, stop=True)
                    last.then_inc(pp, 1)
                    for q in range(4):
                        pe.wait_ge(xhs, 4 * q + 4)
                        for k in range(4):
                            last = pe.transpose(psum[:, q, k * P:(k + 1) * P], xh[:, 4 * q + k, :], ident[:])
                        last.then_inc(tp, 1)
                    for q in range(4):
                        pe.wait_ge(xe, q + 1)
                        if q == 3:
                            pe.wait_ge(sp_hi, 3)
                        for k in range(4):
                            i = 4 * q + k
                            last = pe.matmul(psum[:, 4 + q, k * P:(k + 1) * P], xnT[:, i * P:(i + 1) * P],
                                             wv[:], start=True, stop=True)
                        last.then_inc(vp, 1)

        wst = sb("wst", [P, 2, WST])
        full = sb("full", [P, 3, S])
        high = sb("high", [P, 3, S], F32R)
        bias = sb("bias", [P, 2, 2])
        ks = sb("ks", [P, 2, S], F32R)
        qvs = sb("qvs", [P, 2, S], F32R)
        qz = sb("qz", [P, 2, 4, S], F32R)
        gh = sb("gh", [P, 2, 4, S + 2], F32R)
        gl = sb("gl", [P, 2, 4, S + 2], F32R)
        trig = sb("trig", [P, 2, 2, S])
        gsum = sb("gsum", [P, 2, S])
        negz = sb("negz", [P, 2, 16])
        vz = sb("vz", [P, 2, QB, 4, BAND])
        prob = sb("prob", [P, 2, S])
        probT = sb("probT", [P, 2, 4, QB, P])
        nmax = sb("nmax", [P, 2])
        rsum = sb("rsum", [P, 2, 16])
        rinv = sb("rinv", [P, 2, 4])
        oT = sb("oT", [P, 2, P])

        psS = [psum[:, 0, :], psum[:, 1, :]]
        psU = [psum[:, 2, :], psum[:, 3, :]]
        psT = psum[:, 4, :]
        psO = psum[:, 5, :]
        psG = psum[:, 6:8, :]

        zeroed = sem("zeroed")
        w_in = [sem("wst_in0"), sem("wst_in1")]
        s_bias = sem("s_bias")
        s_proj = sem("s_proj")
        s_full = sem("s_full")
        s_high = sem("s_high")
        s_stack = sem("s_stack")
        s_wz = sem("s_wz")
        s_vz = sem("s_vz")
        s_g = sem("s_g")
        s_rot = sem("s_rot")
        s_gsum = sem("s_gsum")
        s_gh = sem("s_gh")
        s_gl = sem("s_gl")
        s_z = sem("s_z")
        s_negz = sem("s_negz")
        s_score = sem("s_score")
        s_pred = sem("s_pred")
        s_zfix = sem("s_zfix")
        s_max = sem("s_max")
        s_exp = sem("s_exp")
        s_tr = sem("s_tr")
        s_evac = sem("s_evac")
        s_pv = sem("s_pv")
        s_oT = sem("s_oT")
        s_trO = sem("s_trO")
        s_rinv = sem("s_rinv")
        s_norm = sem("s_norm")
        NSTK = 6

        with nc.Block() as block:
            @block.sync
            def _(sp):
                for it in range(ITS + 1):
                    if it >= 2:
                        sp.wait_ge(s_full, 3 * (it - 1))
                    sp.dma_start(wst[:, it % 2, :], t["wst"][it // 4 % HG]).then_inc(w_in[it % 2], 16)

            @block.gpsimd
            def _(pool):
                def weights(it, par, first):
                    g = (it >> 2) & 3
                    if not first:
                        pool.wait_ge(s_g, 4 * it)
                        pool.wait_ge(s_gl, 4 * it)
                    for r in range(4):
                        b = slice(BAND * r, BAND * r + BAND)
                        pool.tensor_copy(wz[b, r, :, :], wpf[b, bass.ds(g, 1), :, :]
                                         .rearrange("p a v c -> p (a v) c")).then_inc(s_wz, 1)
                        pool.wait_ge(s_wz, 4 * it + r + 1)

                def values(it, par, first):
                    g, b = (it >> 2) & 3, it & 3
                    if not first:
                        pool.wait_ge(s_pv, 4 * (it - 1) + 1)
                    for j in range(QB):
                        src = v_all[:, bass.ds(4 * b + j, 1), bass.ds(BAND * g, BAND)]
                        pool.tensor_copy(vz[:, par, j, :, 0:HD],
                                         src.rearrange("p a (r d) -> p (a r) d", r=4)).then_inc(s_vz, 1)

                def table(it, par, r):
                    pool.wait_ge(s_rot, 4 * it + r + 1)
                    if r >= 2:
                        pool.wait_ge(s_gl, 4 * it + r - 1)
                    pool.tensor_tensor(gsum[:, r % 2, :], trig[:, r % 2, 0, :], trig[:, r % 2, 1, :],
                                       ALU.add).then_inc(s_gsum, 1)
                    pool.wait_ge(s_gh, 4 * it + r + 1)
                    pool.tensor_tensor(gl[:, par, r, 0:S], gsum[:, r % 2, :],
                                       gh[:, par, r, 0:S].bitcast(F32), ALU.subtract).then_inc(s_gl, 1)

                def prep(it, par, first=False):
                    weights(it, par, first)
                    for r in range(4):
                        table(it, par, r)
                    values(it, par, first)

                pool.memset(wz[:].bitcast(F32), 0.0).then_inc(zeroed, 1)
                pool.memset(vz[:], 0.0).then_inc(zeroed, 1)
                pool.memset(gh[:, :, :, S:S + 2].bitcast(F32), 0.0).then_inc(zeroed, 1)
                pool.memset(gl[:, :, :, S:S + 2].bitcast(F32), 0.0).then_inc(zeroed, 1)
                pool.memset(qz[:].bitcast(F32), 0.0).then_inc(zeroed, 1)
                pool.wait_ge(zeroed, 5)
                prep(0, 0, True)
                with pool.Fori(0, ITS // 2) as p:
                    prep(2 * p + 1, 1)
                    prep(2 * p + 2, 0)

            @block.scalar
            def _(act):
                def full_rows(it, par, turn):
                    act.wait_ge(s_proj, it + 1)
                    act.wait_ge(s_bias, it + 1)
                    if turn is not None:
                        act.wait_ge(s_stack, NSTK * it)
                    act.activation(full[:, 0, :], psG[:, 0, :], ACT.Identity, bias=bias[:, par, 0:1],
                                   scale=SCALE).then_inc(s_full, 1)
                    act.activation(full[:, 1, :], psG[:, 0, :], ACT.Identity, bias=bias[:, par, 1:2],
                                   scale=SCALE).then_inc(s_full, 1)
                    act.activation(full[:, 2, :], psG[:, 1, :], ACT.Identity,
                                   bias=wst[:, par, 2 * P + 1:2 * P + 2]).then_inc(s_full, 1)

                def exp(p, u):
                    act.wait_ge(s_max, UPP * p + u + 1)
                    if u >= 2:
                        act.wait_ge(s_tr, UPP * p + u - 1)
                    act.activation(prob[:, u % 2, :], psS[u % 2], ACT.Exp, bias=nmax[:, u % 2:u % 2 + 1],
                                   accum_out=rsum[:, u // 16, u % 16:u % 16 + 1]).then_inc(s_exp, 1)

                def evac(p, u):
                    blk = u // 4
                    act.wait_ge(s_tr, UPP * p + u + 1)
                    if blk >= 2:
                        act.wait_ge(s_pv, 8 * p + blk - 1)
                    act.activation(probT[:, blk % 2, u % 4, :, :], psT.rearrange("p (j i) -> p j i", j=QB),
                                   ACT.Copy).then_inc(s_evac, 1)

                full_rows(0, 0, None)
                with act.Fori(0, ITS // 2) as p:
                    for s in range(UPP + 1):
                        if s >= 1:
                            evac(p, s - 1)
                        if s < UPP:
                            exp(p, s)
                            if s % 16 == 2:
                                full_rows(2 * p + s // 16 + 1, (s // 16 + 1) % 2, p)

            @block.vector
            def _(v):
                def biases(it, par, turn):
                    v.wait_ge(w_in[par], 16 * (turn + 1))
                    v.tensor_scalar(bias[:, par, :], wst[:, par, 2 * P + 2:2 * P + 4],
                                    wst[:, par, 2 * P:2 * P + 1], SCALE, ALU.add, ALU.mult).then_inc(s_bias, 1)

                def stacks(it, par):
                    v.wait_ge(s_full, 3 * it + 3)
                    v.tensor_copy(high[:], full[:]).then_inc(s_high, 1)
                    v.wait_ge(s_high, it + 1)

                    def stack(dst, k, c, b=slice(0, P)):
                        v.scalar_tensor_tensor(dst, high[b, k, :].bitcast(F32), negc[b, c:c + 1],
                                               full[b, k, :], ALU.mult, ALU.add).then_inc(s_stack, 1)
                    stack(qvs[:, par, :], 1, 0)
                    stack(ks[:, par, :], 2, 1)
                    for r in range(4):
                        b = slice(BAND * r, BAND * r + BAND)
                        stack(qz[b, par, r, :], 0, 0, b)

                def rotate(it, par, r):
                    v.wait_ge(s_g, 4 * it + r + 1)
                    if r >= 2:
                        v.wait_ge(s_gsum, 4 * it + r - 1)
                    v.tensor_tensor(trig[:, r % 2, :, :], psG, cs[:], ALU.mult).then_inc(s_rot, 1)

                def high_part(it, par, r):
                    v.wait_ge(s_gsum, 4 * it + r + 1)
                    v.tensor_copy(gh[:, par, r, 0:S], gsum[:, r % 2, :]).then_inc(s_gh, 1)

                def neg_z(it, par):
                    v.wait_ge(s_z, it + 1)
                    v.tensor_scalar(negz[:, par, :], psG[:, 0, 0:16], -1.0, None, ALU.mult).then_inc(s_negz, 1)

                def fix(p, u):
                    par, i, r = u // 16, u % 16 // 4, u % 4
                    z0, zw = zone(i)
                    sc, up = psS[u % 2], psU[u % 2]
                    v.reg_add(scored, scored, 1)
                    v.wait_ge(zeroed, 5)
                    v.wait_ge(s_score, scored)
                    v.copy_predicated(sc[:, z0:z0 + zw], maskU[:, 0:zw], up[:, 0:zw]).then_inc(s_pred, 1)
                    if u % 16 == 0:
                        v.wait_ge(s_negz, 2 * p + par + 1)
                    v.wait_ge(s_pred, UPP * p + u + 1)
                    v.scalar_tensor_tensor(sc[:, z0:z0 + zw], maskS[:, 0:zw],
                                           negz[:, par, 4 * i + r:4 * i + r + 1], sc[:, z0:z0 + zw],
                                           ALU.mult, ALU.add).then_inc(s_zfix, 1)
                    v.wait_ge(s_zfix, UPP * p + u + 1)
                    v.tensor_reduce(nmax[:, u % 2:u % 2 + 1], sc, AX_X, ALU.max, negate=True).then_inc(s_max, 1)

                def out_T(p, blk):
                    v.wait_ge(s_pv, 8 * p + blk + 1)
                    v.tensor_copy(oT[:, blk % 2, :], psO[:, 0:P]).then_inc(s_oT, 1)

                def norm(p, blk):
                    par, i = blk // 4, blk % 4
                    it = 2 * p + par
                    v.wait_ge(s_exp, UPP * p + 4 * blk + 4)
                    v.reciprocal(rinv[:, blk % 2, :], rsum[:, par, 4 * i:4 * i + 4]).then_inc(s_rinv, 1)
                    v.wait_ge(s_trO, 8 * p + blk + 1)
                    v.wait_ge(s_rinv, 8 * p + blk + 1)
                    dst = attn[:, bass.ds(4 * (it & 3) + i, 1), bass.ds(BAND * ((it >> 2) & 3), BAND)]
                    v.tensor_tensor(dst.rearrange("p a (r d) -> p (a r) d", r=4),
                                    psO[:, P:2 * P].rearrange("p (r c) -> p r c", r=4)[:, :, 0:HD],
                                    rinv[:, blk % 2, :].rearrange("p (r a) -> p r a", a=1)
                                    .to_broadcast([P, 4, HD]), ALU.mult).then_inc(s_norm, 1)

                scored = v.alloc_register("scored")
                v.reg_mov(scored, 0)
                biases(0, 0, 0)
                v.wait_ge(zeroed, 5)
                stacks(0, 0)
                for r in range(4):
                    rotate(0, 0, r)
                    high_part(0, 0, r)
                neg_z(0, 0)
                with v.Fori(0, ITS // 2) as p:
                    for s in range(UPP + 5):
                        if s < UPP:
                            fix(p, s)
                            nxt, par, q = 2 * p + s // 16 + 1, (s // 16 + 1) % 2, s % 16
                            if q == 0:
                                biases(nxt, par, p + s // 16)
                            if q == 3:
                                stacks(nxt, par)
                            if q in (6, 8, 10, 12):
                                high_part(nxt, par, (q - 6) // 2)
                            if q in (5, 7, 9, 11):
                                rotate(nxt, par, (q - 5) // 2)
                            if q == 13:
                                neg_z(nxt, par)
                        if s >= 6 and (s - 6) % 4 == 0 and (s - 6) // 4 < 8:
                            out_T(p, (s - 6) // 4)
                        if s >= 8 and (s - 8) % 4 == 0 and (s - 8) // 4 < 7:
                            norm(p, (s - 8) // 4)
                    norm(p, 7)

            @block.tensor
            def _(pe):
                def project(it, par, turn):
                    pe.wait_ge(w_in[par], 16 if turn is None else 16 * (turn + 1))
                    if turn is not None:
                        pe.wait_ge(s_negz, it)
                    xb = xnT[:, bass.ds(S * (it & 3), S)]
                    pe.matmul(psG[:, 0, :], wst[:, par, 0:P], xb, start=True, stop=True)
                    pe.matmul(psG[:, 1, :], wst[:, par, P:2 * P], xb, start=True, stop=True).then_inc(s_proj, 1)

                def positions(it, par, r):
                    pe.wait_ge(s_wz, 4 * it + 4)
                    pe.wait_ge(s_stack, NSTK * it + 1)
                    if r == 0:
                        pe.wait_ge(s_full, 3 * it + 3)
                    else:
                        pe.wait_ge(s_rot, 4 * it + r)
                    pe.matmul(psG[:, 0, :], wz[:, r, 0, :], qvs[:, par, :], start=True, stop=True)
                    pe.matmul(psG[:, 1, :], wz[:, r, 1, :], qvs[:, par, :], start=True,
                              stop=True).then_inc(s_g, 1)

                def beside(it, par):
                    pe.wait_ge(s_rot, 4 * it + 4)
                    g = (it >> 2) & 3
                    for i in range(QB):
                        last = pe.matmul(psG[:, 0, 4 * i:4 * i + 4], qvs[:, par, i * P:(i + 1) * P],
                                         psz[:, bass.ds(g, 1), :].rearrange("p a r -> p (a r)"),
                                         start=True, stop=True)
                    last.then_inc(s_z, 1)

                def scores(p, u):
                    par, i, r = u // 16, u % 16 // 4, u % 4
                    it = 2 * p + par
                    z0, zw = zone(i)
                    nl = z0 + zw
                    sc, up = psS[u % 2], psU[u % 2][:, 0:zw]
                    if u % 16 == 0:
                        pe.wait_ge(s_gl, 4 * it + 4)
                        pe.wait_ge(s_gh, 4 * it + 4)
                        pe.wait_ge(s_stack, NSTK * it + NSTK)
                    if u >= 2:
                        pe.wait_ge(s_exp, UPP * p + u - 1)
                    q = qz[:, par, r, i * P:(i + 1) * P]
                    low = gh[:, par, r, i * P:(i + 1) * P], gl[:, par, r, i * P:(i + 1) * P]
                    upp = gh[:, par, r, i * P + 1:(i + 1) * P + 1], gl[:, par, r, i * P + 1:(i + 1) * P + 1]
                    pe.matmul(sc, q, ks[:, par, :], start=True, stop=False)
                    pe.matmul(up, q, ks[:, par, z0:nl], start=True, stop=False)
                    pe.matmul(sc[:, 0:nl], low[0], tabs[:, 0, 0, 0:nl], start=False, stop=False)
                    pe.matmul(sc[:, 0:nl], low[0], tabs[:, 0, 1, 0:nl], start=False, stop=False)
                    pe.matmul(sc[:, 0:nl], low[1], tabs[:, 0, 0, 0:nl], start=False, stop=nl == S)
                    for a, k in ((0, 0), (0, 1), (1, 0)):
                        if nl < S:
                            pe.matmul(sc[:, nl:S], upp[a], tabs[:, 1, k, nl:S], start=False, stop=a == 1)
                        last = pe.matmul(up, upp[a], tabs[:, 1, k, z0:nl], start=False, stop=a == 1)
                    last.then_inc(s_score, 1)

                def turn_probs(p, u):
                    pe.wait_ge(s_exp, UPP * p + u + 1)
                    if u:
                        pe.wait_ge(s_evac, UPP * p + u)
                    for j in range(QB):
                        last = pe.transpose(psT[:, j * P:(j + 1) * P], prob[:, u % 2, j * P:(j + 1) * P],
                                            ident[:])
                    last.then_inc(s_tr, 1)

                def weigh(p, blk):
                    par = blk // 4
                    pe.wait_ge(s_evac, UPP * p + 4 * blk + 4)
                    if blk:
                        pe.wait_ge(s_norm, 8 * p + blk)
                    if blk % 4 == 0:
                        pe.wait_ge(s_vz, 4 * (2 * p + par) + 4)
                    for j in range(QB):
                        for r in range(4):
                            last = pe.matmul(psO[BAND * r:BAND * r + BAND, 0:P], vz[:, par, j, r, :],
                                             probT[:, blk % 2, r, j, :], start=j == 0, stop=j == QB - 1)
                    last.then_inc(s_pv, 1)

                def turn_out(p, blk):
                    pe.wait_ge(s_oT, 8 * p + blk + 1)
                    pe.transpose(psO[:, P:2 * P], oT[:, blk % 2, :], ident[:]).then_inc(s_trO, 1)

                project(0, 0, None)
                for r in range(4):
                    positions(0, 0, r)
                beside(0, 0)
                with pe.Fori(0, ITS // 2) as p:
                    for s in range(UPP + 4):
                        if s < UPP:
                            scores(p, s)
                        if 1 <= s <= UPP:
                            turn_probs(p, s - 1)
                        if s >= 5 and (s - 5) % 4 == 0 and (s - 5) // 4 < 8:
                            weigh(p, (s - 5) // 4)
                        if s >= 7 and (s - 7) % 4 == 0 and (s - 7) // 4 < 8:
                            turn_out(p, (s - 7) // 4)
                        if s < UPP:
                            nxt, par, q = 2 * p + s // 16 + 1, (s // 16 + 1) % 2, s % 16
                            if q == 1:
                                project(nxt, par, p + s // 16)
                            if q in (4, 6, 8, 10):
                                positions(nxt, par, (q - 4) // 2)
                            if q == 12:
                                beside(nxt, par)


def layer_norm(v, x, st, mv, done_st, done_mv, base, n, seen=None):
    for i in range(n):
        v.bn_stats(st[:, i, :], x[:, i, :]).then_inc(done_st, 1)
    if seen is not None:
        v.reg_add(seen, seen, n)
        v.wait_ge(done_st, n)
    v.wait_ge(done_st, base + n if seen is None else seen)
    for i in range(n):
        v.bn_aggr(mv[:, i, :], st[:, i, :]).then_inc(done_mv, 1)


def cross_attention(nc, t, ident, epsc, attn, x2, x2T, psum):
    with ExitStack() as ctx:
        def sb(name, shape, dt=F32):
            return ctx.enter_context(nc.sbuf_tensor(name, shape, dt))

        def sem(name):
            return ctx.enter_context(nc.semaphore(name))

        T = QB
        wf = sb("wf", [P, D])
        bfb = sb("bfb", [P, D])
        bob = sb("bob", [P, D])
        wq2 = sb("wq2", [P, HG, P])
        wk2 = sb("wk2", [P, HG, P])
        wv2 = sb("wv2", [P, D])
        wo2 = sb("wo2", [P, D])
        negc = sb("negc2", [P, 2])
        xb = sb("xb", [P, T, D])
        cb = sb("cb", [M2, D])
        att = sb("att", [P, T, D])
        attT = sb("attT", [P, S])
        y = sb("y1", [P, T, D])
        st = sb("st2", [P, T, 6])
        mv = sb("mv2", [P, T, 2])
        rstd = sb("rstd2", [P, T])
        x1 = sb("x1", [P, T, D])
        x1T = sb("x1T", [P, S])
        cT = sb("cT", [P, M2])
        q2f = sb("q2f", [P, HG, S])
        q2h = sb("q2h", [P, HG, S], F32R)
        q2s = sb("q2s", [P, HG, S], F32R)
        k2f = sb("k2f", [P, HG, M2])
        k2h = sb("k2h", [P, HG, M2], F32R)
        k2z = sb("k2z", [P, HG, 4, M2], F32R)
        v2z = sb("v2z", [M2, HG, 4, BAND])
        pr = sb("pr2", [P, 2, H, M2])
        mx = sb("mx2", [P, 2, H])
        rs2 = sb("rs2", [P, T, H])
        pT = sb("pT2", [M2, H, T, P])
        o2T = sb("o2T", [P, HG, S])
        at2 = sb("at2", [P, T, D])
        at2T = sb("at2T", [P, S])

        w_in = sem("c_w_in")
        x_in = sem("c_x_in")
        ctx_in = sem("c_ctx_in")
        zeroed = sem("c_zeroed")
        names = ["att", "attT_ps", "attT", "y_ps", "res", "res_b", "st", "mv", "sq", "rstd", "x1",
                 "x1T_ps", "x1T", "cT_ps", "cT", "q_ps", "q_full", "q_high", "q_stack", "k_ps", "k_full",
                 "k_high", "k_stack", "v_ps", "v2", "score", "max", "sub", "exp", "sum", "inv", "pT_ps",
                 "pT", "o_ps", "oT", "oN_ps", "at2", "at2T_ps", "at2T", "y2_ps", "res2", "res2b", "st2",
                 "mv2", "sq2", "rstd2", "x2", "x2T_ps", "x2T", "x2keep"]
        s = {n: sem("c_" + n) for n in names}
        bA, bB, bD, bE = 4, 5, 6, 7
        four = psum[:, 0:4, :]

        with nc.Block() as block:
            @block.sync
            def _(sp):
                for dst, src in ((wf[:], t["wf"]), (bfb[:], t["bf"].to_broadcast([P, D])),
                                 (bob[:], t["bo"].to_broadcast([P, D])),
                                 (wq2[:], t["wq2"].rearrange("g e r -> e g r")),
                                 (wk2[:], t["wk2"].rearrange("g e r -> e g r")),
                                 (wv2[:], t["wv2"]), (wo2[:], t["wo2"]), (negc[:], t["negc"])):
                    sp.dma_start(dst, src).then_inc(w_in, 16)
                for b in range(B):
                    if b:
                        sp.wait_ge(s["res"], b)
                    sp.dma_start(xb[:], t["x"][b].rearrange("(t p) d -> p t d", p=P)).then_inc(x_in, 16)
                    if b:
                        sp.wait_ge(s["cT_ps"], b)
                    sp.dma_start(cb[:], t["ctx"][b]).then_inc(ctx_in, 16)

            @block.gpsimd
            def _(pool):
                pool.memset(k2z[:].bitcast(F32), 0.0).then_inc(zeroed, 1)
                pool.memset(v2z[:], 0.0).then_inc(zeroed, 1)

            @block.scalar
            def _(act):
                act.wait_ge(w_in, 16 * 8)
                with act.Fori(0, B) as b:
                    act.wait_ge(s["cT_ps"], b + 1)
                    act.activation(cT[:], psum[:, bB, 0:M2], ACT.Copy).then_inc(s["cT"], 1)
                    act.wait_ge(s["attT_ps"], b + 1)
                    act.activation(attT[:], psum[:, bA, :], ACT.Copy).then_inc(s["attT"], 1)
                    act.wait_ge(s["k_ps"], b + 1)
                    act.activation(k2f[:], psum[:, bD, 0:HG * M2].rearrange("p (g m) -> p g m", g=HG),
                                   ACT.Copy).then_inc(s["k_full"], 1)
                    act.wait_ge(s["mv"], T * (b + 1))
                    act.activation(rstd[:], mv[:, :, 1], ACT.Sqrt, bias=epsc[:, 0:1]).then_inc(s["sq"], 1)
                    act.wait_ge(s["x1T_ps"], b + 1)
                    act.activation(x1T[:], psum[:, bA, :], ACT.Copy).then_inc(s["x1T"], 1)
                    act.wait_ge(s["q_ps"], b + 1)
                    act.activation(q2f[:], four, ACT.Copy, scale=SCALE2).then_inc(s["q_full"], 1)
                    for k in range(T):
                        act.wait_ge(s["sub"], T * b + k + 1)
                        act.activation(pr[:, k % 2, :, :], pr[:, k % 2, :, :], ACT.Exp).then_inc(s["exp"], 1)
                        act.wait_ge(s["pT_ps"], T * b + k + 1)
                        act.activation(pT[:, :, k, :], psum[0:M2, 4:8, :].rearrange("m g (r i) -> m (g r) i", r=4),
                                       ACT.Copy).then_inc(s["pT"], 1)
                    act.wait_ge(s["o_ps"], b + 1)
                    act.activation(o2T[:], four, ACT.Copy).then_inc(s["oT"], 1)
                    act.wait_ge(s["at2T_ps"], b + 1)
                    act.activation(at2T[:], psum[:, 0, :], ACT.Copy).then_inc(s["at2T"], 1)
                    act.wait_ge(s["mv2"], T * (b + 1))
                    act.activation(rstd[:], mv[:, :, 1], ACT.Sqrt, bias=epsc[:, 0:1]).then_inc(s["sq2"], 1)
                    act.wait_ge(s["x2T_ps"], b + 1)
                    act.activation(x2T[:, bass.ds(S * b, S)], psum[:, 2, :], ACT.Copy).then_inc(s["x2T"], 1)

            @block.vector
            def _(v):
                seen1 = v.alloc_register("seen1")
                seen2 = v.alloc_register("seen2")
                v.reg_mov(seen1, 0)
                v.reg_mov(seen2, 0)
                v.wait_ge(w_in, 16 * 8)
                v.wait_ge(zeroed, 2)

                def bcast(a):
                    return a.rearrange("p (a d) -> p a d", a=1).to_broadcast([P, T, D])

                def tiles(bank):
                    return psum[:, bank, :].rearrange("p (t d) -> p t d", t=T)

                with v.Fori(0, B) as b:
                    v.tensor_copy(att[:], attn[:, bass.ds(T * b, T), :]).then_inc(s["att"], 1)
                    v.wait_ge(s["k_full"], b + 1)
                    v.tensor_copy(k2h[:], k2f[:]).then_inc(s["k_high"], 1)
                    v.wait_ge(s["k_high"], b + 1)
                    for r in range(4):
                        c = slice(BAND * r, BAND * r + BAND)
                        v.scalar_tensor_tensor(k2z[c, :, r, :], k2h[c, :, :].bitcast(F32), negc[c, 1:2],
                                               k2f[c, :, :], ALU.mult, ALU.add).then_inc(s["k_stack"], 1)
                    v.wait_ge(s["v_ps"], b + 1)
                    v.tensor_copy(v2z[:, :, :, 0:HD], psum[0:M2, bE, 0:D]
                                  .rearrange("m (g r d) -> m g r d", g=HG, r=4)).then_inc(s["v2"], 1)
                    v.wait_ge(s["y_ps"], b + 1)
                    v.wait_ge(x_in, 16 * (b + 1))
                    v.tensor_tensor(y[:], tiles(bB), xb[:], ALU.add).then_inc(s["res"], 1)
                    v.wait_ge(s["res"], b + 1)
                    v.tensor_tensor(y[:], y[:], bcast(bfb[:]), ALU.add).then_inc(s["res_b"], 1)
                    v.wait_ge(s["res_b"], b + 1)
                    layer_norm(v, y, st, mv, s["st"], s["mv"], T * b, T, seen1)
                    v.wait_ge(s["sq"], b + 1)
                    v.reciprocal(rstd[:], rstd[:]).then_inc(s["rstd"], 1)
                    v.wait_ge(s["rstd"], b + 1)
                    for k in range(T):
                        v.tensor_scalar(x1[:, k, :], y[:, k, :], mv[:, k, 0:1], rstd[:, k:k + 1],
                                        ALU.subtract, ALU.mult).then_inc(s["x1"], 1)
                    v.wait_ge(s["q_full"], b + 1)
                    v.tensor_copy(q2h[:], q2f[:]).then_inc(s["q_high"], 1)
                    v.wait_ge(s["q_high"], b + 1)
                    v.scalar_tensor_tensor(q2s[:].rearrange("p g i -> p (g i)"),
                                           q2h[:].rearrange("p g i -> p (g i)").bitcast(F32), negc[:, 0:1],
                                           q2f[:].rearrange("p g i -> p (g i)"), ALU.mult,
                                           ALU.add).then_inc(s["q_stack"], 1)

                    def sums(k):
                        v.wait_ge(s["exp"], T * b + k + 1)
                        v.tensor_reduce(rs2[:, k, :], pr[:, k % 2, :, :], AX_X, ALU.add).then_inc(s["sum"], 1)

                    for k in range(T):
                        v.wait_ge(s["score"], T * b + k + 1)
                        sc = psum[:, 0:4, 0:4 * M2].rearrange("p g (r m) -> p g r m", r=4)
                        v.tensor_reduce(mx[:, k % 2, :].rearrange("p (g r) -> p g r", g=HG), sc, AX_X,
                                        ALU.max).then_inc(s["max"], 1)
                        v.wait_ge(s["max"], T * b + k + 1)
                        if k >= 2:
                            v.wait_ge(s["pT_ps"], T * b + k - 1)
                            v.wait_ge(s["sum"], T * b + k - 1)
                        v.tensor_tensor(pr[:, k % 2, :, :].rearrange("p (g r) m -> p g r m", g=HG), sc,
                                        mx[:, k % 2, :].rearrange("p (g r a) -> p g r a", g=HG, a=1)
                                        .to_broadcast([P, HG, 4, M2]), ALU.subtract).then_inc(s["sub"], 1)
                        sums(k)
                    v.wait_ge(s["sum"], T * (b + 1))
                    v.reciprocal(rs2[:], rs2[:]).then_inc(s["inv"], 1)
                    v.wait_ge(s["oN_ps"], b + 1)
                    v.wait_ge(s["inv"], b + 1)
                    v.tensor_tensor(at2[:].rearrange("p t (h d) -> p t h d", h=H),
                                    psum[:, 4:8, :].rearrange("p t (h c) -> p t h c", h=H)[:, :, :, 0:HD],
                                    rs2[:].rearrange("p t (h a) -> p t h a", a=1).to_broadcast([P, T, H, HD]),
                                    ALU.mult).then_inc(s["at2"], 1)
                    v.wait_ge(s["y2_ps"], b + 1)
                    v.tensor_tensor(y[:], tiles(1), x1[:], ALU.add).then_inc(s["res2"], 1)
                    v.wait_ge(s["res2"], b + 1)
                    v.tensor_tensor(y[:], y[:], bcast(bob[:]), ALU.add).then_inc(s["res2b"], 1)
                    v.wait_ge(s["res2b"], b + 1)
                    layer_norm(v, y, st, mv, s["st2"], s["mv2"], T * b, T, seen2)
                    v.wait_ge(s["sq2"], b + 1)
                    v.reciprocal(rstd[:], rstd[:]).then_inc(s["rstd2"], 1)
                    v.wait_ge(s["rstd2"], b + 1)
                    for k in range(T):
                        v.tensor_scalar(at2[:, k, :], y[:, k, :], mv[:, k, 0:1], rstd[:, k:k + 1],
                                        ALU.subtract, ALU.mult).then_inc(s["x2"], 1)
                    v.wait_ge(s["x2"], T * (b + 1))
                    v.tensor_copy(x2[:, bass.ds(T * b, T), :], at2[:]).then_inc(s["x2keep"], 1)

            @block.tensor
            def _(pe):
                pe.wait_ge(w_in, 16 * 8)

                def turn(bank, src, done):
                    for k in range(T):
                        last = pe.transpose(psum[:, bank, k * P:(k + 1) * P], src[:, k, :], ident[:])
                    last.then_inc(done, 1)

                def times(bank, src, w, done):
                    for k in range(T):
                        last = pe.matmul(psum[:, bank, k * P:(k + 1) * P], src[:, k * P:(k + 1) * P], w,
                                         start=True, stop=True)
                    last.then_inc(done, 1)

                with pe.Fori(0, B) as b:
                    pe.wait_ge(ctx_in, 16 * (b + 1))
                    pe.transpose(psum[:, bB, 0:M2], cb[:], ident[0:M2, 0:M2]).then_inc(s["cT_ps"], 1)
                    pe.wait_ge(s["att"], b + 1)
                    turn(bA, att, s["attT_ps"])
                    pe.wait_ge(s["cT"], b + 1)
                    for g in range(HG):
                        last = pe.matmul(psum[:, bD, g * M2:(g + 1) * M2], wk2[:, g, :], cT[:], start=True,
                                         stop=True)
                    last.then_inc(s["k_ps"], 1)
                    pe.matmul(psum[0:M2, bE, 0:D], cT[:], wv2[:], start=True, stop=True).then_inc(s["v_ps"], 1)
                    pe.wait_ge(s["attT"], b + 1)
                    times(bB, attT, wf[:], s["y_ps"])
                    pe.wait_ge(s["x1"], T * (b + 1))
                    turn(bA, x1, s["x1T_ps"])
                    pe.wait_ge(s["x1T"], b + 1)
                    for g in range(HG):
                        last = pe.matmul(psum[:, g, :], wq2[:, g, :], x1T[:], start=True, stop=True)
                    last.then_inc(s["q_ps"], 1)
                    pe.wait_ge(s["q_stack"], b + 1)
                    pe.wait_ge(s["k_stack"], 4 * (b + 1))
                    pe.wait_ge(s["v2"], b + 1)
                    for k in range(T):
                        if k:
                            pe.wait_ge(s["sub"], T * b + k)
                        for g in range(HG):
                            last = pe.matmul(psum[:, g, 0:4 * M2], q2s[:, g, k * P:(k + 1) * P],
                                             k2z[:, g, :, :].rearrange("p r m -> p (r m)"), start=True,
                                             stop=True)
                        last.then_inc(s["score"], 1)
                        pe.wait_ge(s["exp"], T * b + k + 1)
                        if k:
                            pe.wait_ge(s["pT"], T * b + k)
                        for h in range(H):
                            last = pe.transpose(psum[0:M2, 4 + h // 4, (h % 4) * P:(h % 4 + 1) * P],
                                                pr[:, k % 2, h, :], ident[:])
                        last.then_inc(s["pT_ps"], 1)
                    pe.wait_ge(s["sub"], T * (b + 1))
                    pe.wait_ge(s["pT"], T * (b + 1))
                    for g in range(HG):
                        for r in range(4):
                            last = pe.matmul(psum[BAND * r:BAND * r + BAND, g, :], v2z[:, g, r, :],
                                             pT[:, 4 * g + r, :, :].rearrange("m t i -> m (t i)"), start=True,
                                             stop=True)
                    last.then_inc(s["o_ps"], 1)
                    pe.wait_ge(s["oT"], b + 1)
                    for k in range(T):
                        for g in range(HG):
                            last = pe.transpose(psum[:, 4 + k, g * P:(g + 1) * P],
                                                o2T[:, g, k * P:(k + 1) * P], ident[:])
                    last.then_inc(s["oN_ps"], 1)
                    pe.wait_ge(s["at2"], b + 1)
                    turn(0, at2, s["at2T_ps"])
                    pe.wait_ge(s["at2T"], b + 1)
                    times(1, at2T, wo2[:], s["y2_ps"])
                    pe.wait_ge(s["x2"], T * (b + 1))
                    turn(2, at2, s["x2T_ps"])


def experts(nc, t, ident, epsc, x2, x2T, psum, out):
    with ExitStack() as ctx:
        def sb(name, shape, dt=F32):
            return ctx.enter_context(nc.sbuf_tensor(name, shape, dt))

        def sem(name):
            return ctx.enter_context(nc.semaphore(name))

        C = HID // P
        wg = sb("wg", [P, E])
        bgb = sb("bgb", [P, E])
        b2 = sb("b2", [E, D])
        order = sb("order", [P, E])
        w1 = sb("w1", [P, 2, HID])
        w2 = sb("w2", [P, 2, C, D])
        b1 = sb("b1", [P, 2, C])
        pr = sb("gate_p", [P, NT, E])
        left = sb("gate_left", [P, NT, E])
        hit = sb("gate_hit", [P, NT, E])
        sel = sb("gate_sel", [P, NT, E])
        m = sb("gate_m", [P, NT])
        selT = sb("selT", [E, B * S])
        acc = sb("acc", [P, NT, D])
        hT = sb("hT", [P, 2, C, S])
        st = sb("st3", [P, NT, 6])
        mv = sb("mv3", [P, NT, 2])
        rstd = sb("rstd3", [P, NT])

        c_in = sem("e_consts_in")
        w_in = [sem("e_w_in0"), sem("e_w_in1")]
        logit = sem("e_logit")
        gate = sem("e_gate_step")
        gexp = sem("e_gate_exp")
        selt = sem("e_selT_ps")
        seltd = sem("e_selT")
        accp = sem("e_b2_ps")
        s_h = sem("e_hidden_ps")
        s_ge = sem("e_gelu")
        s_y = sem("e_out_ps")
        s_acc = sem("e_acc")
        st_d = sem("e_st")
        mv_d = sem("e_mv")
        sq = sem("e_sq")
        rs_d = sem("e_rstd")
        fin = sem("e_final")
        stored = sem("e_stored")
        NB = B * C

        with nc.Block() as block:
            @block.sync
            def _(sp):
                for dst, src in ((wg[:], t["wg"]), (bgb[:], t["bg"].to_broadcast([P, E])), (b2[:], t["b2"]),
                                 (order[:], t["order"])):
                    sp.dma_start(dst, src).then_inc(c_in, 16)

                def load(e, par):
                    sp.dma_start(w1[:, par, :], t["w1"][bass.ds(e, 1)].rearrange("a p n -> p (a n)")
                                 ).then_inc(w_in[par], 16)
                    sp.dma_start(w2[:, par, :, :], t["w2"][bass.ds(e, 1)].rearrange("a (c p) n -> p (a c) n", p=P)
                                 ).then_inc(w_in[par], 16)
                    sp.dma_start(b1[:, par, :], t["b1"][bass.ds(e, 1)].rearrange("a p c -> p (a c)")
                                 ).then_inc(w_in[par], 16)
                load(0, 0)
                load(1, 1)
                with sp.Fori(1, E // 2) as p:
                    for par in range(2):
                        sp.wait_ge(w_in[par], 48)
                        sp.wait_ge(s_y, B * (2 * p + par - 1))
                        load(2 * p + par, par)
                for q in range(4):
                    sp.wait_ge(fin, 4 * q + 4)
                    sp.dma_start(out[q].rearrange("(t p) d -> p t d", p=P),
                                 acc[:, 4 * q:4 * q + 4, :]).then_inc(stored, 16)
                sp.wait_ge(stored, 64)

            @block.scalar
            def _(act):
                act.wait_ge(gate, 3)
                act.activation(pr[:], pr[:], ACT.Exp).then_inc(gexp, 1)
                act.wait_ge(selt, 1)
                act.activation(selT[:], psum[0:E, 4:8, :].rearrange("e q n -> e (q n)"), ACT.Copy).then_inc(seltd, 1)
                with act.Fori(0, E // 2) as p:
                    for k in range(2 * B):
                        par, b = k // B, k % B
                        n0 = 2 * NB * p + C * k
                        if k >= 2:
                            act.wait_ge(s_y, 2 * B * p + k - 1)
                        for c in range(C):
                            act.wait_ge(s_h, n0 + c + 1)
                            act.activation(hT[:, k % 2, c, :], psum[:, c, :], ACT.Gelu_apprx_tanh,
                                           bias=b1[:, par, c:c + 1]).then_inc(s_ge, 1)
                act.wait_ge(mv_d, NT)
                act.activation(rstd[:], mv[:, :, 1], ACT.Sqrt, bias=epsc[:, 0:1]).then_inc(sq, 1)

            @block.vector
            def _(v):
                step = [0]

                def link(ins):
                    step[0] += 1
                    ins.then_inc(gate, 1)
                    v.wait_ge(gate, step[0])

                def per_tile(a):
                    return a.rearrange("p (t a) -> p t a", a=1).to_broadcast([P, NT, E])

                def all_tiles(a):
                    return a.rearrange("p (a e) -> p a e", a=1).to_broadcast([P, NT, E])

                v.wait_ge(c_in, 64)
                v.wait_ge(logit, 1)
                link(v.tensor_tensor(pr[:], psum[:, 3, 0:NT * E].rearrange("p (t e) -> p t e", e=E),
                                     all_tiles(bgb[:]), ALU.add))
                link(v.tensor_reduce(m[:], pr[:], AX_X, ALU.max))
                link(v.tensor_tensor(pr[:], pr[:], per_tile(m[:]), ALU.subtract))
                choose(v, link, gexp, pr, left, hit, sel, m, order, per_tile, all_tiles)
                v.wait_ge(accp, 1)
                v.tensor_tensor(acc[:], psum[:, 4:8, :].rearrange("p q (k d) -> p (q k) d", k=4), x2[:],
                                ALU.add).then_inc(s_acc, 1)
                v.wait_ge(s_acc, 1)
                with v.Fori(0, E // 2) as p:
                    for k in range(2 * B):
                        par, b = k // B, k % B
                        v.wait_ge(s_y, 2 * B * p + k + 1)
                        v.wait_ge(s_acc, 1 + 2 * NT * p + 4 * max(0, k - B + 1))
                        for q in range(4):
                            i = 4 * b + q
                            v.scalar_tensor_tensor(acc[:, i, :], psum[:, 4 + k % 2, q * P:(q + 1) * P],
                                                   sel[:, i, bass.ds(2 * p + par, 1)], acc[:, i, :],
                                                   ALU.mult, ALU.add).then_inc(s_acc, 1)
                v.wait_ge(s_acc, 1 + NT * E)
                layer_norm(v, acc, st, mv, st_d, mv_d, 0, NT)
                v.wait_ge(sq, 1)
                v.reciprocal(rstd[:], rstd[:]).then_inc(rs_d, 1)
                v.wait_ge(rs_d, 1)
                for i in range(NT):
                    v.tensor_scalar(acc[:, i, :], acc[:, i, :], mv[:, i, 0:1], rstd[:, i:i + 1],
                                    ALU.subtract, ALU.mult).then_inc(fin, 1)

            @block.tensor
            def _(pe):
                pe.wait_ge(c_in, 64)
                for i in range(NT):
                    last = pe.matmul(psum[:, 3, i * E:(i + 1) * E], x2T[:, i * P:(i + 1) * P], wg[:],
                                     start=True, stop=True)
                last.then_inc(logit, 1)
                pe.wait_ge(gate, GATE_STEPS)
                for i in range(NT):
                    last = pe.transpose(psum[0:E, 4 + i // 4, (i % 4) * P:(i % 4 + 1) * P], sel[:, i, :], ident[:])
                last.then_inc(selt, 1)
                pe.wait_ge(seltd, 1)
                for i in range(NT):
                    last = pe.matmul(psum[:, 4 + i // 4, (i % 4) * P:(i % 4 + 1) * P], selT[:, i * P:(i + 1) * P],
                                     b2[:], start=True, stop=True)
                last.then_inc(accp, 1)
                pe.wait_ge(s_acc, 1)

                def hidden(p, k):
                    par, b = k // B, k % B
                    n0 = 2 * NB * p + C * k
                    if b == 0:
                        pe.wait_ge(w_in[par], 48 * (p + 1))
                    for c in range(C):
                        if k:
                            pe.wait_ge(s_ge, n0 + c + 1 - C)
                        pe.matmul(psum[:, c, :], w1[:, par, c * P:(c + 1) * P], x2T[:, b * S:(b + 1) * S],
                                  start=True, stop=True).then_inc(s_h, 1)

                def down(p, k):
                    par, b = k // B, k % B
                    pe.wait_ge(s_ge, 2 * NB * p + C * k + C)
                    if k >= 2:
                        pe.wait_ge(s_acc, 1 + 2 * NT * p + 4 * (k - 1))
                    else:
                        pe.wait_ge(s_acc, 1 + 2 * NT * p)
                    for q in range(4):
                        for c in range(C):
                            last = pe.matmul(psum[:, 4 + k % 2, q * P:(q + 1) * P],
                                             hT[:, k % 2, c, q * P:(q + 1) * P], w2[:, par, c, :],
                                             start=c == 0, stop=c == C - 1)
                    last.then_inc(s_y, 1)

                with pe.Fori(0, E // 2) as p:
                    for k in range(2 * B + 1):
                        if k < 2 * B:
                            hidden(p, k)
                        if k:
                            down(p, k - 1)


GATE_STEPS = 25


def choose(v, link, gexp, pr, left, hit, sel, m, order, per_tile, all_tiles):
    v.wait_ge(gexp, 1)
    link(v.tensor_reduce(m[:], pr[:], AX_X, ALU.add))
    link(v.reciprocal(m[:], m[:]))
    link(v.tensor_tensor(pr[:], pr[:], per_tile(m[:]), ALU.mult))
    link(v.tensor_copy(left[:], pr[:]))
    for n in range(2):
        link(v.tensor_reduce(m[:], left[:], AX_X, ALU.max))
        link(v.tensor_tensor(hit[:], left[:], per_tile(m[:]), ALU.is_ge))
        link(v.tensor_tensor(hit[:], hit[:], all_tiles(order[:]), ALU.mult))
        link(v.tensor_reduce(m[:], hit[:], AX_X, ALU.max))
        link(v.tensor_tensor(hit[:], all_tiles(order[:]), per_tile(m[:]), ALU.is_equal))
        link(v.scalar_tensor_tensor(left[:], hit[:], -2.0, left[:], ALU.mult, ALU.add))
    link(v.tensor_scalar(hit[:], left[:], 0.0, None, ALU.is_lt))
    link(v.tensor_tensor(sel[:], pr[:], hit[:], ALU.mult))
    link(v.tensor_reduce(m[:], sel[:], AX_X, ALU.add))
    link(v.tensor_scalar(m[:], m[:], 1e-8, None, ALU.add))
    link(v.reciprocal(m[:], m[:]))
    link(v.tensor_tensor(sel[:], sel[:], per_tile(m[:]), ALU.mult))


def in_bands(a):
    a = np.asarray(a)
    out = np.zeros(a.shape[:-1] + (HG, 4, BAND), a.dtype)
    src = a.reshape(a.shape[:-1] + (HG, 4, HD))
    for k in range(3):
        out[..., k * HD:(k + 1) * HD] = src
    return out.reshape(a.shape[:-1] + (HG, P))


def shape_constants():
    f32 = np.float32
    inv = f32(1.0) / np.power(f32(10000.0), np.arange(0, D, 2, dtype=f32) / f32(D))
    w = np.repeat(inv.astype(f32).astype(np.float64), 2)[:, None]
    odd = (np.arange(D) % 2 == 1)[:, None]
    j = np.arange(S)[None, :]

    def table(pos):
        return np.where(odd, np.cos(pos * w), np.sin(pos * w))
    turn = (S - 1 - j) * w
    tabs = np.stack([table(j), table(j - S)], axis=1)
    cs = np.stack([np.cos(turn), np.where(odd, np.sin(turn), -np.sin(turn))], axis=1)
    row = np.arange(P)[:, None]
    in_band = row % BAND // HD
    negc = np.concatenate([-(in_band == 2).astype(f32), -(in_band == 1).astype(f32)], axis=1)
    col = np.arange(ZONE)[None, :]
    return {
        "ident": np.eye(P, dtype=f32), "negc": negc, "tabs": tabs.astype(f32), "cs": cs.astype(f32),
        "peS": table(np.array([[S]])).astype(f32), "bandm": (row // BAND == np.arange(4)[None, :]).astype(f32),
        "maskU": (col >= row + 2).astype(np.uint32), "maskS": (col == row + 1).astype(f32),
        "order": np.tile(np.arange(E, 0, -1, dtype=f32), (P, 1)),
    }


def kernel(x, ctx_1024, L0_attn_Wq, L0_attn_bq, L0_attn_Wk, L0_attn_bk, L0_attn_Wv, L0_attn_bv, L0_attn_Wpos,
           L0_attn_Wf, L0_attn_bf, L0_attn_u, L0_attn_v, L0_attn_gamma, L0_attn_beta, L0_xattn_wq, L0_xattn_wk,
           L0_xattn_wv, L0_xattn_wo, L0_xattn_bo, L0_ffn_Wg, L0_ffn_bg, L0_ffn_W1, L0_ffn_b1, L0_ffn_W2,
           L0_ffn_b2):
    import concourse.bacc as bacc
    from concourse.bass_utils import run_bass_kernel_spmd

    A = np.asarray
    wq, wk = (in_bands(w).transpose(1, 0, 2) for w in (L0_attn_Wq, L0_attn_Wk))
    cols = [in_bands(A(c).reshape(D))[:, :, None] for c in (L0_attn_bq, L0_attn_bk, L0_attn_u, L0_attn_v)]
    posC = in_bands(L0_attn_Wpos).transpose(1, 0, 2)
    posT = posC.transpose(0, 2, 1)
    swapped = posT.reshape(HG, P, D // 2, 2)[..., ::-1].reshape(HG, P, D)
    arrays = {
        "x": x, "ctx": ctx_1024, "wst": np.concatenate([wq, wk] + cols, axis=2),
        "wposT": np.stack([posT, swapped], axis=1), "wposC": posC,
        "gb": np.stack([A(L0_attn_gamma), A(L0_attn_beta)], axis=1),
        "wv": L0_attn_Wv, "bv": A(L0_attn_bv).reshape(1, D), "wf": L0_attn_Wf, "bf": A(L0_attn_bf).reshape(1, D),
        "wq2": in_bands(A(L0_xattn_wq).T).transpose(1, 0, 2), "wk2": in_bands(A(L0_xattn_wk).T).transpose(1, 0, 2),
        "wv2": A(L0_xattn_wv).T, "wo2": A(L0_xattn_wo).T, "bo": A(L0_xattn_bo).reshape(1, D),
        "wg": L0_ffn_Wg, "bg": A(L0_ffn_bg).reshape(1, E), "w1": L0_ffn_W1,
        "b1": A(L0_ffn_b1).reshape(E, HID // P, P).transpose(0, 2, 1), "w2": L0_ffn_W2, "b2": L0_ffn_b2,
    }
    arrays.update(shape_constants())
    nc = bacc.Bacc("TRN2", target_bir_lowering=False, num_devices=1)
    feed, t = {}, {}
    for name, a in arrays.items():
        a = np.ascontiguousarray(a)
        feed[f"in_{name}"] = a
        t[name] = nc.dram_tensor(f"in_{name}", a.shape, mybir.dt.from_np(a.dtype), kind="ExternalInput").ap()
    out = nc.dram_tensor("out_0", (B, S, D), F32, kind="ExternalOutput").ap()
    decoder_kernel(nc, t, out)
    r = run_bass_kernel_spmd(nc, [feed], core_ids=[0])
    return r.results[0]["out_0"]
```

```python
from contextlib import ExitStack

import numpy as np

import concourse.bass as bass
from concourse import mybir

F32 = mybir.dt.float32
F32R = mybir.dt.float32r
U32 = mybir.dt.uint32
ALU = mybir.AluOpType
ACT = mybir.ActivationFunctionType
AX_X = mybir.AxisListType.X

P = 128
B, S, D = 4, 512, 128
H, HD = 16, 8
NT = B * S // P
QB = S // P
HG = 4
BAND = 32
M2 = 77
E = 8
HID = 4 * D
EPS = 1e-5
PASSES = (0, 0), (0, 1), (1, 0)
ZONE = P + 2
SCALE = float(D) ** -0.5
SCALE2 = float(HD) ** -0.5
ITS = B * HG
UPP = 2 * 4 * QB
WST = 2 * P + 4


LAG = 3
LEAD = 7


def zone(i):
    return P * i, min(ZONE, S - P * i)


def first(p):
    return isinstance(p, int) and p == 0


def decoder_kernel(nc, t, out):
    with ExitStack() as ctx:
        def sb(name, shape, dt=F32):
            return ctx.enter_context(nc.sbuf_tensor(name, shape, dt))

        def sem(name):
            return ctx.enter_context(nc.semaphore(name))

        ident = sb("ident", [P, P])
        epsc = sb("epsc", [P, 1])
        attn = sb("attn", [P, NT, D])
        psum = ctx.enter_context(nc.psum_tensor("psum", [P, 8, 512], F32))

        self_attention(nc, t, ident, epsc, attn, psum)
        with ExitStack() as late:
            x2 = late.enter_context(nc.sbuf_tensor("x2", [P, NT, D], F32))
            x2T = late.enter_context(nc.sbuf_tensor("x2T", [P, B * S], F32))
            cross_attention(nc, t, ident, epsc, attn, x2, x2T, psum)
            experts(nc, t, ident, epsc, x2, x2T, psum, out)


def self_attention(nc, t, ident, epsc, attn, psum):
    with ExitStack() as ctx:
        def sb(name, shape, dt=F32):
            return ctx.enter_context(nc.sbuf_tensor(name, shape, dt))

        def sem(name):
            return ctx.enter_context(nc.semaphore(name))

        xnT = sb("xnT", [P, B * S])
        v_all = sb("v_all", [P, NT, D])
        tabs = sb("tabs", [P, 2, 2, S], F32R)
        cs = sb("cs", [P, 2, S])
        wpf = sb("wpf", [P, HG, 2, P], F32R)
        psz = sb("psz", [P, HG, 4], F32R)
        negc = sb("negc", [P, 2])
        bandm = sb("bandm", [P, 4])
        maskU = sb("maskU", [P, S], U32)
        maskS = sb("maskS", [P, ZONE])
        wz = sb("wz", [P, 4, 2, P], F32R)

        with ExitStack() as ca:
            def sba(name, shape, dt=F32):
                return ca.enter_context(nc.sbuf_tensor(name, shape, dt))

            x = sba("x_in", [P, NT, D])
            xh = sba("xh", [P, NT, D])
            st = sba("ln_st", [P, NT, 6])
            mv = sba("ln_mv", [P, NT, 2])
            rstd = sba("ln_rstd", [P, NT])
            gb = sba("gb", [P, 2])
            wv = sba("wv", [P, P])
            bvb = sba("bvb", [P, P])
            wposr = sba("wposr", [P, HG, 2, P])
            wposh = sba("wposh", [P, HG, 2, P], F32R)
            wposc = sba("wposc", [P, HG, P])
            tabr = sba("tabr", [P, 2, S])
            peS = sba("peS", [P, 1])
            pSr = sba("pSr", [P, HG])
            pSh = sba("pSh", [P, HG], F32R)
            pSt = sba("pSt", [P, HG])
            x_in = sem("a_x_loaded")
            c_in = sem("a_consts_loaded")
            w_in = sem("a_weights_loaded")
            stat = sem("a_stats")
            sq = sem("a_sqrt")
            rs = sem("a_rstd")
            xhs = sem("a_xhat")
            tp = sem("a_transposed")
            xe = sem("a_xnT")
            vp = sem("a_v_psum")
            ve = sem("a_v")
            sp_hi = sem("a_split_high")
            sp_lo = sem("a_split_done")
            pp = sem("a_pos_psum")
            epsm = sem("a_eps")
            with nc.Block() as block:
                @block.sync
                def _(sp):
                    for q in range(4):
                        sp.dma_start(x[:, 4 * q:4 * q + 4, :],
                                     t["x"][q].rearrange("(t p) d -> p t d", p=P)).then_inc(x_in, 16)
                    for dst, src in ((ident[:], t["ident"]), (gb[:], t["gb"]), (negc[:], t["negc"]),
                                     (bandm[:], t["bandm"]), (maskU[:], t["maskU"]), (maskS[:], t["maskS"]),
                                     (peS[:], t["peS"])):
                        sp.dma_start(dst, src).then_inc(c_in, 16)
                    sp.dma_start(cs[:], t["cs"]).then_inc(c_in, 16)

                @block.scalar
                def _(act):
                    act.dma_start(wv[:], t["wv"]).then_inc(w_in, 16)
                    act.dma_start(bvb[:], t["bv"].to_broadcast([P, P])).then_inc(w_in, 16)
                    act.dma_start(tabr[:], t["tabs"]).then_inc(w_in, 16)
                    act.dma_start(wposr[:], t["wposT"].rearrange("g v p c -> p g v c")).then_inc(w_in, 16)
                    act.dma_start(wposc[:], t["wposC"].rearrange("g c r -> c g r")).then_inc(w_in, 16)
                    act.wait_ge(epsm, 1)
                    act.wait_ge(stat, NT)
                    act.activation(rstd[:], mv[:, :, 1], ACT.Sqrt, bias=epsc[:, 0:1]).then_inc(sq, 1)
                    act.wait_ge(c_in, 16 * 8)
                    for q in range(4):
                        act.wait_ge(tp, q + 1)
                        act.activation(xnT[:, q * 512:(q + 1) * 512], psum[:, q, :], ACT.Identity,
                                       bias=gb[:, 1:2], scale=gb[:, 0:1]).then_inc(xe, 1)

                @block.gpsimd
                def _(pool):
                    pool.memset(epsc[:], EPS).then_inc(epsm, 1)

                @block.vector
                def _(v):
                    for i in range(NT):
                        if i % 4 == 0:
                            v.wait_ge(x_in, 64)
                        v.bn_stats(st[:, i, :], x[:, i, :]).then_inc(rs, 1)
                    v.wait_ge(rs, NT)
                    for i in range(NT):
                        v.bn_aggr(mv[:, i, :], st[:, i, :]).then_inc(stat, 1)
                    v.wait_ge(sq, 1)
                    v.reciprocal(rstd[:], rstd[:]).then_inc(rs, 1)
                    v.wait_ge(rs, NT + 1)
                    for i in range(NT):
                        v.tensor_scalar(xh[:, i, :], x[:, i, :], mv[:, i, 0:1], rstd[:, i:i + 1],
                                        ALU.subtract, ALU.mult).then_inc(xhs, 1)
                    v.wait_ge(w_in, 16 * 5)
                    v.wait_ge(c_in, 16 * 8)
                    v.tensor_copy(tabs[:, :, 0, :], tabr[:]).then_inc(sp_hi, 1)
                    v.tensor_copy(wposh[:], wposr[:]).then_inc(sp_hi, 1)
                    v.wait_ge(pp, 1)
                    v.tensor_copy(pSr[:], psum[:, 7, 0:HG]).then_inc(sp_hi, 1)
                    v.wait_ge(sp_hi, 3)
                    v.tensor_copy(pSh[:], pSr[:]).then_inc(sp_hi, 1)
                    v.tensor_tensor(tabs[:, :, 1, :], tabr[:], tabs[:, :, 0, :].bitcast(F32),
                                    ALU.subtract).then_inc(sp_lo, 1)
                    wf = wpf[:].rearrange("p g v c -> p (g v c)")
                    v.scalar_tensor_tensor(wf, wposh[:].rearrange("p g v c -> p (g v c)").bitcast(F32),
                                           negc[:, 1:2], wposr[:].rearrange("p g v c -> p (g v c)"),
                                           ALU.mult, ALU.add).then_inc(sp_lo, 1)
                    v.wait_ge(sp_hi, 4)
                    v.scalar_tensor_tensor(pSt[:], pSh[:].bitcast(F32), negc[:, 1:2], pSr[:],
                                           ALU.mult, ALU.add).then_inc(sp_lo, 1)
                    v.wait_ge(sp_lo, 3)
                    for g in range(HG):
                        v.tensor_scalar(psz[:, g, :], bandm[:], pSt[:, g:g + 1], None,
                                        ALU.mult).then_inc(sp_lo, 1)
                    for q in range(4):
                        v.wait_ge(vp, q + 1)
                        v.tensor_tensor(v_all[:, 4 * q:4 * q + 4, :],
                                        psum[:, q + 4, :].rearrange("p (t d) -> p t d", t=4),
                                        bvb[:].rearrange("p (a d) -> p a d", a=1).to_broadcast([P, 4, D]),
                                        ALU.add).then_inc(ve, 1)

                @block.tensor
                def _(pe):
                    pe.wait_ge(c_in, 16 * 8)
                    pe.wait_ge(w_in, 16 * 5)
                    for g in range(HG):
                        last = pe.matmul(psum[:, 7, g:g + 1], wposc[:, g, :], peS[:], start=True, stop=True)
                    last.then_inc(pp, 1)
                    for q in range(4):
                        pe.wait_ge(xhs, 4 * q + 4)
                        for k in range(4):
                            last = pe.transpose(psum[:, q, k * P:(k + 1) * P], xh[:, 4 * q + k, :], ident[:])
                        last.then_inc(tp, 1)
                    for q in range(4):
                        pe.wait_ge(xe, q + 1)
                        if q == 3:
                            pe.wait_ge(sp_hi, 3)
                        for k in range(4):
                            i = 4 * q + k
                            last = pe.matmul(psum[:, 4 + q, k * P:(k + 1) * P], xnT[:, i * P:(i + 1) * P],
                                             wv[:], start=True, stop=True)
                        last.then_inc(vp, 1)

        wst = sb("wst", [P, 2, WST])
        full = sb("full", [P, 3, S])
        high = sb("high", [P, 3, S], F32R)
        bias = sb("bias", [P, 2, 2])
        ks = sb("ks", [P, 2, S], F32R)
        qvs = sb("qvs", [P, 2, S], F32R)
        qs = sb("qs", [P, S], F32R)
        qz = sb("qz", [P, 2, 4, S], F32R)
        gh = sb("gh", [P, 2, 4, S + 2], F32R)
        gl = sb("gl", [P, 2, 4, S + 2], F32R)
        trig = sb("trig", [P, 2, 2, S])
        gsum = sb("gsum", [P, 2, S])
        negz = sb("negz", [P, 2, 16])
        vz = sb("vz", [P, 2, QB, 4, BAND])
        prob = sb("prob", [P, 4, S])
        probT = sb("probT", [P, 2, 4, QB, P])
        nmax = sb("nmax", [P, 4])
        rsum = sb("rsum", [P, 2, 16])
        rinv = sb("rinv", [P, 2, 4])
        oT = sb("oT", [P, 2, P])

        psS = [psum[:, k, :] for k in range(4)]
        psU = psum[:, 4, :]
        TURNS = (6, 7, 8, 10, 11, 12, 14, 15)
        psT = psum[:, 5, :]
        psO = psum[:, 6, :]
        psG = psum[:, 7, :]
        psG2 = psG.rearrange("p (v j) -> p v j", v=2)
        HS = S // 2

        zeroed = sem("zeroed")
        w_in = [sem("wst_in0"), sem("wst_in1")]
        s_bias = sem("s_bias")
        s_proj = sem("s_proj")
        s_full = sem("s_full")
        s_high = sem("s_high")
        s_stack = sem("s_stack")
        s_qz = sem("s_qz")
        s_wz = sem("s_wz")
        s_vz = sem("s_vz")
        s_g = sem("s_g")
        s_rot = sem("s_rot")
        s_gsum = sem("s_gsum")
        s_gh = sem("s_gh")
        s_gl = sem("s_gl")
        s_z = sem("s_z")
        s_negz = sem("s_negz")
        s_score = sem("s_score")
        s_pred = sem("s_pred")
        s_zfix = sem("s_zfix")
        s_max = sem("s_max")
        s_exp = sem("s_exp")
        s_tr = sem("s_tr")
        s_evac = sem("s_evac")
        s_pv = sem("s_pv")
        s_oT = sem("s_oT")
        s_trO = sem("s_trO")
        s_rinv = sem("s_rinv")
        s_norm = sem("s_norm")
        SPLIT_AT = {1: 1, 2: 2, 0: 3}
        NSTK = 3

        with nc.Block() as block:
            @block.sync
            def _(sp):
                for it in range(ITS):
                    if it >= 2:
                        sp.wait_ge(s_full, 3 * (it - 1))
                    sp.dma_start(wst[:, it % 2, :], t["wst"][it // 4 % HG]).then_inc(w_in[it % 2], 16)

            @block.gpsimd
            def _(pool):
                def weights(it, par, first):
                    g = (it >> 2) & 3
                    if not first:
                        pool.wait_ge(s_g, 8 * it)
                        pool.wait_ge(s_gl, 4 * it)
                    for r in range(4):
                        b = slice(BAND * r, BAND * r + BAND)
                        pool.tensor_copy(wz[b, r, :, :], wpf[b, bass.ds(g, 1), :, :]
                                         .rearrange("p a v c -> p (a v) c")).then_inc(s_wz, 1)
                        pool.wait_ge(s_wz, 4 * it + r + 1)

                def values(it, par, first):
                    g, b = (it >> 2) & 3, it & 3
                    if not first:
                        pool.wait_ge(s_pv, 4 * (it - 1) + 1)
                    for j in range(QB):
                        src = v_all[:, bass.ds(4 * b + j, 1), bass.ds(BAND * g, BAND)]
                        pool.tensor_copy(vz[:, par, j, :, 0:HD],
                                         src.rearrange("p a (r d) -> p (a r) d", r=4)).then_inc(s_vz, 1)

                def table(it, par, r):
                    pool.wait_ge(s_rot, 8 * it + 2 * r + 2)
                    if r >= 2:
                        pool.wait_ge(s_gl, 4 * it + r - 1)
                    pool.tensor_tensor(gsum[:, r % 2, :], trig[:, r % 2, 0, :], trig[:, r % 2, 1, :],
                                       ALU.add).then_inc(s_gsum, 1)
                    pool.wait_ge(s_gh, 4 * it + r + 1)
                    pool.tensor_tensor(gl[:, par, r, 0:S], gsum[:, r % 2, :],
                                       gh[:, par, r, 0:S].bitcast(F32), ALU.subtract).then_inc(s_gl, 1)

                def prep(it, par, first=False):
                    weights(it, par, first)
                    for r in range(4):
                        table(it, par, r)
                    values(it, par, first)

                pool.memset(wz[:].bitcast(F32), 0.0).then_inc(zeroed, 1)
                pool.memset(vz[:], 0.0).then_inc(zeroed, 1)
                pool.memset(gh[:, :, :, S:S + 2].bitcast(F32), 0.0).then_inc(zeroed, 1)
                pool.memset(gl[:, :, :, S:S + 2].bitcast(F32), 0.0).then_inc(zeroed, 1)
                pool.wait_ge(zeroed, 4)
                prep(0, 0, True)
                with pool.Fori(0, ITS // 2 - 1) as p:
                    prep(2 * p + 1, 1)
                    prep(2 * p + 2, 0)
                prep(ITS - 1, 1)

            @block.scalar
            def _(act):
                def full_queries(it, par, turn):
                    act.wait_ge(s_proj, 2 * it + 1)
                    act.wait_ge(s_bias, it + 1)
                    if turn is not None:
                        act.wait_ge(s_stack, NSTK * it)
                    for k in range(2):
                        act.activation(full[:, k, :], psG, ACT.Identity, bias=bias[:, par, k:k + 1],
                                       scale=SCALE).then_inc(s_full, 1)

                def full_keys(it, par):
                    act.wait_ge(s_proj, 2 * it + 2)
                    act.activation(full[:, 2, :], psG, ACT.Identity,
                                   bias=wst[:, par, 2 * P + 1:2 * P + 2]).then_inc(s_full, 1)

                def split(it, k):
                    act.wait_ge(s_full, 3 * it + 2 + k // 2)
                    act.activation(high[:, k, :], full[:, k, :], ACT.Copy).then_inc(s_high, 1)

                def one_head(it, par, r):
                    act.wait_ge(s_stack, NSTK * it + 3)
                    act.activation(qz[:, par, r, :], qs[:], ACT.Copy, scale=bandm[:, r:r + 1]).then_inc(s_qz, 1)

                def high_part(it, par, r):
                    act.wait_ge(s_gsum, 4 * it + r + 1)
                    act.activation(gh[:, par, r, 0:S], gsum[:, r % 2, :], ACT.Copy).then_inc(s_gh, 1)

                def exp(p, u):
                    act.wait_ge(s_max, UPP * p + u + 1)
                    if u >= 4 or not first(p):
                        act.wait_ge(s_tr, UPP * p + u - 3)
                    act.activation(prob[:, u % 4, :], psS[u % 4], ACT.Exp, bias=nmax[:, u % 4:u % 4 + 1],
                                   accum_out=rsum[:, u // 16, u % 16:u % 16 + 1]).then_inc(s_exp, 1)

                def evac(p, u):
                    blk = u // 4
                    act.wait_ge(s_tr, UPP * p + u + 1)
                    if blk >= 2 or not first(p):
                        act.wait_ge(s_pv, 8 * p + blk - 1)
                    act.activation(probT[:, blk % 2, u % 4, :, :], psT.rearrange("p (j i) -> p j i", j=QB),
                                   ACT.Copy).then_inc(s_evac, 1)

                def slot(p, s, prep=True):
                    nxt, par, q = 2 * p + s // 16 + 1, (s // 16 + 1) % 2, s % 16
                    if prep and q == 0:
                        full_queries(nxt, par, p)
                    if prep and q == 3:
                        full_keys(nxt, par)
                    if s:
                        evac(p, s - 1)
                    elif not first(p):
                        evac(p - 1, UPP - 1)
                    exp(p, s)
                    if not prep:
                        return
                    if q in (0, 3, 4):
                        split(nxt, {0: 1, 3: 2, 4: 0}[q])
                    if q in (6, 9, 11, 14):
                        high_part(nxt, par, (6, 9, 11, 14).index(q))
                    if q in (10, 12, 13, 15):
                        one_head(nxt, par, (10, 12, 13, 15).index(q))

                full_queries(0, 0, None)
                full_keys(0, 0)
                for k in (1, 2, 0):
                    split(0, k)
                for r in range(4):
                    one_head(0, 0, r)
                for r in range(4):
                    high_part(0, 0, r)
                for s in range(LEAD):
                    slot(0, s)
                with act.Fori(0, ITS // 2 - 1) as p:
                    for s in range(LEAD, UPP):
                        slot(p, s)
                    for s in range(LEAD):
                        slot(p + 1, s)
                for s in range(LEAD, UPP):
                    slot(ITS // 2 - 1, s, prep=s < UPP // 2)
                evac(ITS // 2 - 1, UPP - 1)

            @block.vector
            def _(v):
                def biases(it, par, turn):
                    v.wait_ge(w_in[par], 16 * (turn + 1))
                    v.tensor_scalar(bias[:, par, :], wst[:, par, 2 * P + 2:2 * P + 4],
                                    wst[:, par, 2 * P:2 * P + 1], SCALE, ALU.add, ALU.mult).then_inc(s_bias, 1)

                def stack(it, dst, k, c, b=slice(0, P)):
                    v.wait_ge(s_high, 3 * it + SPLIT_AT[k])
                    v.scalar_tensor_tensor(dst, high[b, k, :].bitcast(F32), negc[b, c:c + 1],
                                           full[b, k, :], ALU.mult, ALU.add).then_inc(s_stack, 1)

                def rotate(it, par, h):
                    r, c = h // 2, slice(h % 2 * HS, h % 2 * HS + HS)
                    v.wait_ge(s_g, 8 * it + h + 1)
                    if r >= 2:
                        v.wait_ge(s_gsum, 4 * it + r - 1)
                    v.tensor_tensor(trig[:, r % 2, :, c], psG2, cs[:, :, c], ALU.mult).then_inc(s_rot, 1)

                def neg_z(it, par):
                    v.wait_ge(s_z, it + 1)
                    v.tensor_scalar(negz[:, par, :], psG[:, 0:16], -1.0, None, ALU.mult).then_inc(s_negz, 1)

                def take_upper(p, u):
                    z0, _ = zone(u % 16 // 4)
                    v.reg_add(scored, scored, 1)
                    v.wait_ge(zeroed, 4)
                    v.wait_ge(s_score, scored)
                    v.copy_predicated(psS[u % 4][:, z0:S], maskU[:, 0:S - z0], psU[:, z0:S]).then_inc(s_pred, 1)

                def fix(p, u):
                    par, i, r = u // 16, u % 16 // 4, u % 4
                    z0, zw = zone(i)
                    sc = psS[u % 4][:, z0:z0 + zw]
                    if u % 16 == 0:
                        v.wait_ge(s_negz, 2 * p + par + 1)
                    v.wait_ge(s_pred, UPP * p + u + 1)
                    v.scalar_tensor_tensor(sc, maskS[:, 0:zw], negz[:, par, 4 * i + r:4 * i + r + 1], sc,
                                           ALU.mult, ALU.add).then_inc(s_zfix, 1)

                def maximum(p, u):
                    v.wait_ge(s_zfix, UPP * p + u + 1)
                    v.tensor_reduce(nmax[:, u % 4:u % 4 + 1], psS[u % 4], AX_X, ALU.max,
                                    negate=True).then_inc(s_max, 1)

                def out_T(p, blk):
                    v.wait_ge(s_pv, 8 * p + blk + 1)
                    v.tensor_copy(oT[:, blk % 2, :], psO[:, 0:P]).then_inc(s_oT, 1)

                def norm(p, blk):
                    par, i = blk // 4, blk % 4
                    it = 2 * p + par
                    v.wait_ge(s_exp, UPP * p + 4 * blk + 4)
                    v.reciprocal(rinv[:, blk % 2, :], rsum[:, par, 4 * i:4 * i + 4]).then_inc(s_rinv, 1)
                    v.wait_ge(s_trO, 8 * p + blk + 1)
                    v.wait_ge(s_rinv, 8 * p + blk + 1)
                    dst = attn[:, bass.ds(4 * (it & 3) + i, 1), bass.ds(BAND * ((it >> 2) & 3), BAND)]
                    v.tensor_tensor(dst.rearrange("p a (r d) -> p (a r) d", r=4),
                                    psO[:, P:2 * P].rearrange("p (r c) -> p r c", r=4)[:, :, 0:HD],
                                    rinv[:, blk % 2, :].rearrange("p (r a) -> p r a", a=1)
                                    .to_broadcast([P, 4, HD]), ALU.mult).then_inc(s_norm, 1)

                scored = v.alloc_register("scored")
                v.reg_mov(scored, 0)
                biases(0, 0, 0)
                v.wait_ge(zeroed, 4)
                stack(0, qvs[:, 0, :], 1, 0)
                stack(0, ks[:, 0, :], 2, 1)
                stack(0, qs[:], 0, 0)
                neg_z(0, 0)
                for h in range(8):
                    rotate(0, 0, h)

                def slot(p, s, prep=True):
                    nxt, par, q = 2 * p + s // 16 + 1, (s // 16 + 1) % 2, s % 16
                    if prep and q == 0:
                        biases(nxt, par, p + s // 16)
                    if prep and q in TURNS:
                        rotate(nxt, par, TURNS.index(q))
                    if prep and q == 5:
                        neg_z(nxt, par)
                    finish(p, s)
                    if s < LEAD and not first(p):
                        finish(p - 1, s + UPP)
                    take_upper(p, s)
                    if s:
                        maximum(p, s - 1)
                    elif not first(p):
                        maximum(p - 1, UPP - 1)
                    fix(p, s)
                    if prep and q == 2:
                        stack(nxt, qvs[:, par, :], 1, 0)
                    if prep and q == 6:
                        stack(nxt, ks[:, par, :], 2, 1)
                    if prep and q == 9:
                        v.wait_ge(s_qz, 4 * nxt)
                        stack(nxt, qs[:], 0, 0)

                def finish(p, s):
                    if s >= 8 and s % 4 == 0:
                        out_T(p, (s - 8) // 4)
                    if s >= 10 and s % 4 == 2:
                        norm(p, (s - 10) // 4)

                for s in range(LEAD):
                    slot(0, s)
                with v.Fori(0, ITS // 2 - 1) as p:
                    for s in range(LEAD, UPP):
                        slot(p, s)
                    for s in range(LEAD):
                        slot(p + 1, s)
                for s in range(LEAD, UPP):
                    slot(ITS // 2 - 1, s, prep=s < UPP // 2)
                maximum(ITS // 2 - 1, UPP - 1)
                for s in range(UPP, UPP + LEAD):
                    finish(ITS // 2 - 1, s)

            @block.tensor
            def _(pe):
                def project_q(it, par, turn):
                    pe.wait_ge(w_in[par], 16 if turn is None else 16 * (turn + 1))
                    if turn is not None:
                        pe.wait_ge(s_rot, 8 * it)
                    pe.matmul(psG, wst[:, par, 0:P], xnT[:, bass.ds(S * (it & 3), S)], start=True,
                              stop=True).then_inc(s_proj, 1)

                def project_k(it, par):
                    pe.wait_ge(s_full, 3 * it + 2)
                    pe.matmul(psG, wst[:, par, P:2 * P], xnT[:, bass.ds(S * (it & 3), S)], start=True,
                              stop=True).then_inc(s_proj, 1)

                def positions(it, par, h):
                    r, c = h // 2, slice(h % 2 * HS, h % 2 * HS + HS)
                    if h == 0:
                        pe.wait_ge(s_negz, it + 1)
                    else:
                        pe.wait_ge(s_rot, 8 * it + h)
                    pe.wait_ge(s_wz, 4 * it + r + 1)
                    pe.matmul(psG2[:, 0, :], wz[:, r, 0, :], qvs[:, par, c], start=True, stop=True)
                    pe.matmul(psG2[:, 1, :], wz[:, r, 1, :], qvs[:, par, c], start=True,
                              stop=True).then_inc(s_g, 1)

                def beside(it, par):
                    pe.wait_ge(s_stack, NSTK * it + 1)
                    pe.wait_ge(s_full, 3 * it + 3)
                    g = (it >> 2) & 3
                    for i in range(QB):
                        last = pe.matmul(psG[:, 4 * i:4 * i + 4], qvs[:, par, i * P:(i + 1) * P],
                                         psz[:, bass.ds(g, 1), :].rearrange("p a r -> p (a r)"),
                                         start=True, stop=True)
                    last.then_inc(s_z, 1)

                def scores_lower(p, u):
                    par, i, r = u // 16, u % 16 // 4, u % 4
                    it = 2 * p + par
                    nl = sum(zone(i))
                    if i == 0:
                        pe.wait_ge(s_gl, 4 * it + r + 1)
                        pe.wait_ge(s_gh, 4 * it + r + 1)
                        pe.wait_ge(s_qz, 4 * it + r + 1)
                    if u >= 4 or not first(p):
                        pe.wait_ge(s_exp, UPP * p + u - 3)
                    g = gh[:, par, r, i * P:(i + 1) * P], gl[:, par, r, i * P:(i + 1) * P]
                    pe.matmul(psS[u % 4][:, 0:nl], qz[:, par, r, i * P:(i + 1) * P], ks[:, par, 0:nl],
                              start=True, stop=False)
                    for a, k in PASSES:
                        pe.matmul(psS[u % 4][:, 0:nl], g[a], tabs[:, 0, k, 0:nl], start=False, stop=a == 1)

                def scores_upper(p, u):
                    par, i, r = u // 16, u % 16 // 4, u % 4
                    z0, _ = zone(i)
                    if u or not first(p):
                        pe.wait_ge(s_pred, UPP * p + u)
                    g = gh[:, par, r, i * P + 1:(i + 1) * P + 1], gl[:, par, r, i * P + 1:(i + 1) * P + 1]
                    pe.matmul(psU[:, z0:S], qz[:, par, r, i * P:(i + 1) * P], ks[:, par, z0:S],
                              start=True, stop=False)
                    for a, k in PASSES:
                        last = pe.matmul(psU[:, z0:S], g[a], tabs[:, 1, k, z0:S], start=False, stop=a == 1)
                    last.then_inc(s_score, 1)

                def turn_probs(p, u):
                    pe.wait_ge(s_exp, UPP * p + u + 1)
                    if u or not first(p):
                        pe.wait_ge(s_evac, UPP * p + u)
                    for j in range(QB):
                        last = pe.transpose(psT[:, j * P:(j + 1) * P], prob[:, u % 4, j * P:(j + 1) * P],
                                            ident[:])
                    last.then_inc(s_tr, 1)

                def weigh(p, blk):
                    par = blk // 4
                    pe.wait_ge(s_evac, UPP * p + 4 * blk + 4)
                    if blk or not first(p):
                        pe.wait_ge(s_norm, 8 * p + blk)
                    if blk % 4 == 0:
                        pe.wait_ge(s_vz, 4 * (2 * p + par) + 4)
                    for j in range(QB):
                        for r in range(4):
                            last = pe.matmul(psO[BAND * r:BAND * r + BAND, 0:P], vz[:, par, j, r, :],
                                             probT[:, blk % 2, r, j, :], start=j == 0, stop=j == QB - 1)
                    last.then_inc(s_pv, 1)

                def turn_out(p, blk):
                    pe.wait_ge(s_oT, 8 * p + blk + 1)
                    pe.transpose(psO[:, P:2 * P], oT[:, blk % 2, :], ident[:]).then_inc(s_trO, 1)

                project_q(0, 0, None)
                project_k(0, 0)
                beside(0, 0)
                for h in range(8):
                    positions(0, 0, h)
                def finish(p, s):
                    if LAG <= s < UPP + LAG:
                        turn_probs(p, s - LAG)
                    if s >= 7 and s % 4 == 3:
                        weigh(p, (s - 7) // 4)
                    if s >= 9 and s % 4 == 1:
                        turn_out(p, (s - 9) // 4)

                def slot(p, s, prep=True):
                    scores_lower(p, s)
                    finish(p, s)
                    if s < LEAD and not first(p):
                        finish(p - 1, s + UPP)
                    nxt, par, q = 2 * p + s // 16 + 1, (s // 16 + 1) % 2, s % 16
                    if prep:
                        if q == 0:
                            project_q(nxt, par, p + s // 16)
                        if q == 4:
                            project_k(nxt, par)
                        if q in TURNS:
                            positions(nxt, par, TURNS.index(q))
                        if q == 5:
                            beside(nxt, par)
                    scores_upper(p, s)

                for s in range(LEAD):
                    slot(0, s)
                with pe.Fori(0, ITS // 2 - 1) as p:
                    for s in range(LEAD, UPP):
                        slot(p, s)
                    for s in range(LEAD):
                        slot(p + 1, s)
                for s in range(LEAD, UPP):
                    slot(ITS // 2 - 1, s, prep=s < UPP // 2)
                for s in range(UPP, UPP + LEAD):
                    finish(ITS // 2 - 1, s)


def layer_norm(v, x, st, mv, done_st, done_mv, base, n, seen=None):
    for i in range(n):
        v.bn_stats(st[:, i, :], x[:, i, :]).then_inc(done_st, 1)
    if seen is not None:
        v.reg_add(seen, seen, n)
        v.wait_ge(done_st, n)
    v.wait_ge(done_st, base + n if seen is None else seen)
    for i in range(n):
        v.bn_aggr(mv[:, i, :], st[:, i, :]).then_inc(done_mv, 1)


def cross_attention(nc, t, ident, epsc, attn, x2, x2T, psum):
    with ExitStack() as ctx:
        def sb(name, shape, dt=F32):
            return ctx.enter_context(nc.sbuf_tensor(name, shape, dt))

        def sem(name):
            return ctx.enter_context(nc.semaphore(name))

        T = QB
        wf = sb("wf", [P, D])
        bfb = sb("bfb", [P, D])
        bob = sb("bob", [P, D])
        wq2 = sb("wq2", [P, HG, P])
        wk2 = sb("wk2", [P, HG, P])
        wv2 = sb("wv2", [P, D])
        wo2 = sb("wo2", [P, D])
        negc = sb("negc2", [P, 2])
        xb = sb("xb", [P, T, D])
        cb = sb("cb", [M2, D])
        att = sb("att", [P, T, D])
        attT = sb("attT", [P, S])
        y = sb("y1", [P, T, D])
        st = sb("st2", [P, T, 6])
        mv = sb("mv2", [P, T, 2])
        rstd = sb("rstd2", [P, T])
        x1 = sb("x1", [P, T, D])
        x1T = sb("x1T", [P, S])
        cT = sb("cT", [P, M2])
        q2f = sb("q2f", [P, HG, S])
        q2h = sb("q2h", [P, HG, S], F32R)
        q2s = sb("q2s", [P, HG, S], F32R)
        k2f = sb("k2f", [P, HG, M2])
        k2h = sb("k2h", [P, HG, M2], F32R)
        k2z = sb("k2z", [P, HG, 4, M2], F32R)
        v2z = sb("v2z", [M2, HG, 4, BAND])
        pr = sb("pr2", [P, 2, H, M2])
        mx = sb("mx2", [P, 2, H])
        rs2 = sb("rs2", [P, T, H])
        pT = sb("pT2", [M2, H, T, P])
        o2T = sb("o2T", [P, HG, S])
        at2 = sb("at2", [P, T, D])
        at2T = sb("at2T", [P, S])

        w_in = sem("c_w_in")
        x_in = sem("c_x_in")
        ctx_in = sem("c_ctx_in")
        zeroed = sem("c_zeroed")
        names = ["att", "attT_ps", "attT", "y_ps", "res", "res_b", "st", "mv", "sq", "rstd", "x1",
                 "x1T_ps", "x1T", "cT_ps", "cT", "q_ps", "q_full", "q_high", "q_stack", "k_ps", "k_full",
                 "k_high", "k_stack", "v_ps", "v2", "score", "max", "sub", "exp", "sum", "inv", "pT_ps",
                 "pT", "o_ps", "oT", "oN_ps", "at2", "at2T_ps", "at2T", "y2_ps", "res2", "res2b", "st2",
                 "mv2", "sq2", "rstd2", "x2", "x2T_ps", "x2T", "x2keep"]
        s = {n: sem("c_" + n) for n in names}
        bA, bB, bD, bE = 4, 5, 6, 7
        four = psum[:, 0:4, :]

        with nc.Block() as block:
            @block.sync
            def _(sp):
                for dst, src in ((wf[:], t["wf"]), (bfb[:], t["bf"].to_broadcast([P, D])),
                                 (bob[:], t["bo"].to_broadcast([P, D])),
                                 (wq2[:], t["wq2"].rearrange("g e r -> e g r")),
                                 (wk2[:], t["wk2"].rearrange("g e r -> e g r")),
                                 (wv2[:], t["wv2"]), (wo2[:], t["wo2"]), (negc[:], t["negc"])):
                    sp.dma_start(dst, src).then_inc(w_in, 16)
                for b in range(B):
                    if b:
                        sp.wait_ge(s["res"], b)
                    sp.dma_start(xb[:], t["x"][b].rearrange("(t p) d -> p t d", p=P)).then_inc(x_in, 16)
                    if b:
                        sp.wait_ge(s["cT_ps"], b)
                    sp.dma_start(cb[:], t["ctx"][b]).then_inc(ctx_in, 16)

            @block.gpsimd
            def _(pool):
                pool.memset(k2z[:].bitcast(F32), 0.0).then_inc(zeroed, 1)
                pool.memset(v2z[:], 0.0).then_inc(zeroed, 1)

            @block.scalar
            def _(act):
                act.wait_ge(w_in, 16 * 8)
                with act.Fori(0, B) as b:
                    act.wait_ge(s["cT_ps"], b + 1)
                    act.activation(cT[:], psum[:, bB, 0:M2], ACT.Copy).then_inc(s["cT"], 1)
                    act.wait_ge(s["attT_ps"], b + 1)
                    act.activation(attT[:], psum[:, bA, :], ACT.Copy).then_inc(s["attT"], 1)
                    act.wait_ge(s["k_ps"], b + 1)
                    act.activation(k2f[:], psum[:, bD, 0:HG * M2].rearrange("p (g m) -> p g m", g=HG),
                                   ACT.Copy).then_inc(s["k_full"], 1)
                    act.wait_ge(s["mv"], T * (b + 1))
                    act.activation(rstd[:], mv[:, :, 1], ACT.Sqrt, bias=epsc[:, 0:1]).then_inc(s["sq"], 1)
                    act.wait_ge(s["x1T_ps"], b + 1)
                    act.activation(x1T[:], psum[:, bA, :], ACT.Copy).then_inc(s["x1T"], 1)
                    act.wait_ge(s["q_ps"], b + 1)
                    act.activation(q2f[:], four, ACT.Copy, scale=SCALE2).then_inc(s["q_full"], 1)
                    for k in range(T):
                        act.wait_ge(s["sub"], T * b + k + 1)
                        act.activation(pr[:, k % 2, :, :], pr[:, k % 2, :, :], ACT.Exp).then_inc(s["exp"], 1)
                        act.wait_ge(s["pT_ps"], T * b + k + 1)
                        act.activation(pT[:, :, k, :], psum[0:M2, 4:8, :].rearrange("m g (r i) -> m (g r) i", r=4),
                                       ACT.Copy).then_inc(s["pT"], 1)
                    act.wait_ge(s["o_ps"], b + 1)
                    act.activation(o2T[:], four, ACT.Copy).then_inc(s["oT"], 1)
                    act.wait_ge(s["at2T_ps"], b + 1)
                    act.activation(at2T[:], psum[:, 0, :], ACT.Copy).then_inc(s["at2T"], 1)
                    act.wait_ge(s["mv2"], T * (b + 1))
                    act.activation(rstd[:], mv[:, :, 1], ACT.Sqrt, bias=epsc[:, 0:1]).then_inc(s["sq2"], 1)
                    act.wait_ge(s["x2T_ps"], b + 1)
                    act.activation(x2T[:, bass.ds(S * b, S)], psum[:, 2, :], ACT.Copy).then_inc(s["x2T"], 1)

            @block.vector
            def _(v):
                seen1 = v.alloc_register("seen1")
                seen2 = v.alloc_register("seen2")
                v.reg_mov(seen1, 0)
                v.reg_mov(seen2, 0)
                v.wait_ge(w_in, 16 * 8)
                v.wait_ge(zeroed, 2)

                def bcast(a):
                    return a.rearrange("p (a d) -> p a d", a=1).to_broadcast([P, T, D])

                def tiles(bank):
                    return psum[:, bank, :].rearrange("p (t d) -> p t d", t=T)

                with v.Fori(0, B) as b:
                    v.tensor_copy(att[:], attn[:, bass.ds(T * b, T), :]).then_inc(s["att"], 1)
                    v.wait_ge(s["k_full"], b + 1)
                    v.tensor_copy(k2h[:], k2f[:]).then_inc(s["k_high"], 1)
                    v.wait_ge(s["k_high"], b + 1)
                    for r in range(4):
                        c = slice(BAND * r, BAND * r + BAND)
                        v.scalar_tensor_tensor(k2z[c, :, r, :], k2h[c, :, :].bitcast(F32), negc[c, 1:2],
                                               k2f[c, :, :], ALU.mult, ALU.add).then_inc(s["k_stack"], 1)
                    v.wait_ge(s["v_ps"], b + 1)
                    v.tensor_copy(v2z[:, :, :, 0:HD], psum[0:M2, bE, 0:D]
                                  .rearrange("m (g r d) -> m g r d", g=HG, r=4)).then_inc(s["v2"], 1)
                    v.wait_ge(s["y_ps"], b + 1)
                    v.wait_ge(x_in, 16 * (b + 1))
                    v.tensor_tensor(y[:], tiles(bB), xb[:], ALU.add).then_inc(s["res"], 1)
                    v.wait_ge(s["res"], b + 1)
                    v.tensor_tensor(y[:], y[:], bcast(bfb[:]), ALU.add).then_inc(s["res_b"], 1)
                    v.wait_ge(s["res_b"], b + 1)
                    layer_norm(v, y, st, mv, s["st"], s["mv"], T * b, T, seen1)
                    v.wait_ge(s["sq"], b + 1)
                    v.reciprocal(rstd[:], rstd[:]).then_inc(s["rstd"], 1)
                    v.wait_ge(s["rstd"], b + 1)
                    for k in range(T):
                        v.tensor_scalar(x1[:, k, :], y[:, k, :], mv[:, k, 0:1], rstd[:, k:k + 1],
                                        ALU.subtract, ALU.mult).then_inc(s["x1"], 1)
                    v.wait_ge(s["q_full"], b + 1)
                    v.tensor_copy(q2h[:], q2f[:]).then_inc(s["q_high"], 1)
                    v.wait_ge(s["q_high"], b + 1)
                    v.scalar_tensor_tensor(q2s[:].rearrange("p g i -> p (g i)"),
                                           q2h[:].rearrange("p g i -> p (g i)").bitcast(F32), negc[:, 0:1],
                                           q2f[:].rearrange("p g i -> p (g i)"), ALU.mult,
                                           ALU.add).then_inc(s["q_stack"], 1)

                    def sums(k):
                        v.wait_ge(s["exp"], T * b + k + 1)
                        v.tensor_reduce(rs2[:, k, :], pr[:, k % 2, :, :], AX_X, ALU.add).then_inc(s["sum"], 1)

                    for k in range(T):
                        v.wait_ge(s["score"], T * b + k + 1)
                        sc = psum[:, 0:4, 0:4 * M2].rearrange("p g (r m) -> p g r m", r=4)
                        v.tensor_reduce(mx[:, k % 2, :].rearrange("p (g r) -> p g r", g=HG), sc, AX_X,
                                        ALU.max).then_inc(s["max"], 1)
                        v.wait_ge(s["max"], T * b + k + 1)
                        if k >= 2:
                            v.wait_ge(s["pT_ps"], T * b + k - 1)
                            v.wait_ge(s["sum"], T * b + k - 1)
                        v.tensor_tensor(pr[:, k % 2, :, :].rearrange("p (g r) m -> p g r m", g=HG), sc,
                                        mx[:, k % 2, :].rearrange("p (g r a) -> p g r a", g=HG, a=1)
                                        .to_broadcast([P, HG, 4, M2]), ALU.subtract).then_inc(s["sub"], 1)
                        sums(k)
                    v.wait_ge(s["sum"], T * (b + 1))
                    v.reciprocal(rs2[:], rs2[:]).then_inc(s["inv"], 1)
                    v.wait_ge(s["oN_ps"], b + 1)
                    v.wait_ge(s["inv"], b + 1)
                    v.tensor_tensor(at2[:].rearrange("p t (h d) -> p t h d", h=H),
                                    psum[:, 4:8, :].rearrange("p t (h c) -> p t h c", h=H)[:, :, :, 0:HD],
                                    rs2[:].rearrange("p t (h a) -> p t h a", a=1).to_broadcast([P, T, H, HD]),
                                    ALU.mult).then_inc(s["at2"], 1)
                    v.wait_ge(s["y2_ps"], b + 1)
                    v.tensor_tensor(y[:], tiles(1), x1[:], ALU.add).then_inc(s["res2"], 1)
                    v.wait_ge(s["res2"], b + 1)
                    v.tensor_tensor(y[:], y[:], bcast(bob[:]), ALU.add).then_inc(s["res2b"], 1)
                    v.wait_ge(s["res2b"], b + 1)
                    layer_norm(v, y, st, mv, s["st2"], s["mv2"], T * b, T, seen2)
                    v.wait_ge(s["sq2"], b + 1)
                    v.reciprocal(rstd[:], rstd[:]).then_inc(s["rstd2"], 1)
                    v.wait_ge(s["rstd2"], b + 1)
                    for k in range(T):
                        v.tensor_scalar(at2[:, k, :], y[:, k, :], mv[:, k, 0:1], rstd[:, k:k + 1],
                                        ALU.subtract, ALU.mult).then_inc(s["x2"], 1)
                    v.wait_ge(s["x2"], T * (b + 1))
                    v.tensor_copy(x2[:, bass.ds(T * b, T), :], at2[:]).then_inc(s["x2keep"], 1)

            @block.tensor
            def _(pe):
                pe.wait_ge(w_in, 16 * 8)

                def turn(bank, src, done):
                    for k in range(T):
                        last = pe.transpose(psum[:, bank, k * P:(k + 1) * P], src[:, k, :], ident[:])
                    last.then_inc(done, 1)

                def times(bank, src, w, done):
                    for k in range(T):
                        last = pe.matmul(psum[:, bank, k * P:(k + 1) * P], src[:, k * P:(k + 1) * P], w,
                                         start=True, stop=True)
                    last.then_inc(done, 1)

                with pe.Fori(0, B) as b:
                    pe.wait_ge(ctx_in, 16 * (b + 1))
                    pe.transpose(psum[:, bB, 0:M2], cb[:], ident[0:M2, 0:M2]).then_inc(s["cT_ps"], 1)
                    pe.wait_ge(s["att"], b + 1)
                    turn(bA, att, s["attT_ps"])
                    pe.wait_ge(s["cT"], b + 1)
                    for g in range(HG):
                        last = pe.matmul(psum[:, bD, g * M2:(g + 1) * M2], wk2[:, g, :], cT[:], start=True,
                                         stop=True)
                    last.then_inc(s["k_ps"], 1)
                    pe.matmul(psum[0:M2, bE, 0:D], cT[:], wv2[:], start=True, stop=True).then_inc(s["v_ps"], 1)
                    pe.wait_ge(s["attT"], b + 1)
                    times(bB, attT, wf[:], s["y_ps"])
                    pe.wait_ge(s["x1"], T * (b + 1))
                    turn(bA, x1, s["x1T_ps"])
                    pe.wait_ge(s["x1T"], b + 1)
                    for g in range(HG):
                        last = pe.matmul(psum[:, g, :], wq2[:, g, :], x1T[:], start=True, stop=True)
                    last.then_inc(s["q_ps"], 1)
                    pe.wait_ge(s["q_stack"], b + 1)
                    pe.wait_ge(s["k_stack"], 4 * (b + 1))
                    pe.wait_ge(s["v2"], b + 1)
                    for k in range(T):
                        if k:
                            pe.wait_ge(s["sub"], T * b + k)
                        for g in range(HG):
                            last = pe.matmul(psum[:, g, 0:4 * M2], q2s[:, g, k * P:(k + 1) * P],
                                             k2z[:, g, :, :].rearrange("p r m -> p (r m)"), start=True,
                                             stop=True)
                        last.then_inc(s["score"], 1)
                        pe.wait_ge(s["exp"], T * b + k + 1)
                        if k:
                            pe.wait_ge(s["pT"], T * b + k)
                        for h in range(H):
                            last = pe.transpose(psum[0:M2, 4 + h // 4, (h % 4) * P:(h % 4 + 1) * P],
                                                pr[:, k % 2, h, :], ident[:])
                        last.then_inc(s["pT_ps"], 1)
                    pe.wait_ge(s["sub"], T * (b + 1))
                    pe.wait_ge(s["pT"], T * (b + 1))
                    for g in range(HG):
                        for r in range(4):
                            last = pe.matmul(psum[BAND * r:BAND * r + BAND, g, :], v2z[:, g, r, :],
                                             pT[:, 4 * g + r, :, :].rearrange("m t i -> m (t i)"), start=True,
                                             stop=True)
                    last.then_inc(s["o_ps"], 1)
                    pe.wait_ge(s["oT"], b + 1)
                    for k in range(T):
                        for g in range(HG):
                            last = pe.transpose(psum[:, 4 + k, g * P:(g + 1) * P],
                                                o2T[:, g, k * P:(k + 1) * P], ident[:])
                    last.then_inc(s["oN_ps"], 1)
                    pe.wait_ge(s["at2"], b + 1)
                    turn(0, at2, s["at2T_ps"])
                    pe.wait_ge(s["at2T"], b + 1)
                    times(1, at2T, wo2[:], s["y2_ps"])
                    pe.wait_ge(s["x2"], T * (b + 1))
                    turn(2, at2, s["x2T_ps"])


def experts(nc, t, ident, epsc, x2, x2T, psum, out):
    with ExitStack() as ctx:
        def sb(name, shape, dt=F32):
            return ctx.enter_context(nc.sbuf_tensor(name, shape, dt))

        def sem(name):
            return ctx.enter_context(nc.semaphore(name))

        C = HID // P
        wg = sb("wg", [P, E])
        bgb = sb("bgb", [P, E])
        b2 = sb("b2", [E, D])
        order = sb("order", [P, E])
        w1 = sb("w1", [P, 2, HID])
        w2 = sb("w2", [P, 2, C, D])
        b1 = sb("b1", [P, 2, C])
        pr = sb("gate_p", [P, NT, E])
        left = sb("gate_left", [P, NT, E])
        hit = sb("gate_hit", [P, NT, E])
        sel = sb("gate_sel", [P, NT, E])
        m = sb("gate_m", [P, NT])
        selT = sb("selT", [E, B * S])
        acc = sb("acc", [P, NT, D])
        hT = sb("hT", [P, 2, C, S])
        st = sb("st3", [P, NT, 6])
        mv = sb("mv3", [P, NT, 2])
        rstd = sb("rstd3", [P, NT])

        c_in = sem("e_consts_in")
        w_in = [sem("e_w_in0"), sem("e_w_in1")]
        logit = sem("e_logit")
        gate = sem("e_gate_step")
        gexp = sem("e_gate_exp")
        selt = sem("e_selT_ps")
        seltd = sem("e_selT")
        accp = sem("e_b2_ps")
        s_h = sem("e_hidden_ps")
        s_ge = sem("e_gelu")
        s_y = sem("e_out_ps")
        s_acc = sem("e_acc")
        st_d = sem("e_st")
        mv_d = sem("e_mv")
        sq = sem("e_sq")
        rs_d = sem("e_rstd")
        fin = sem("e_final")
        stored = sem("e_stored")
        NB = B * C

        with nc.Block() as block:
            @block.sync
            def _(sp):
                for dst, src in ((wg[:], t["wg"]), (bgb[:], t["bg"].to_broadcast([P, E])), (b2[:], t["b2"]),
                                 (order[:], t["order"])):
                    sp.dma_start(dst, src).then_inc(c_in, 16)

                def load(e, par):
                    sp.dma_start(w1[:, par, :], t["w1"][bass.ds(e, 1)].rearrange("a p n -> p (a n)")
                                 ).then_inc(w_in[par], 16)
                    sp.dma_start(w2[:, par, :, :], t["w2"][bass.ds(e, 1)].rearrange("a (c p) n -> p (a c) n", p=P)
                                 ).then_inc(w_in[par], 16)
                    sp.dma_start(b1[:, par, :], t["b1"][bass.ds(e, 1)].rearrange("a p c -> p (a c)")
                                 ).then_inc(w_in[par], 16)
                load(0, 0)
                load(1, 1)
                with sp.Fori(1, E // 2) as p:
                    for par in range(2):
                        sp.wait_ge(w_in[par], 48)
                        sp.wait_ge(s_y, B * (2 * p + par - 1))
                        load(2 * p + par, par)
                for q in range(4):
                    sp.wait_ge(fin, 4 * q + 4)
                    sp.dma_start(out[q].rearrange("(t p) d -> p t d", p=P),
                                 acc[:, 4 * q:4 * q + 4, :]).then_inc(stored, 16)
                sp.wait_ge(stored, 64)

            @block.scalar
            def _(act):
                act.wait_ge(gate, 3)
                act.activation(pr[:], pr[:], ACT.Exp).then_inc(gexp, 1)
                act.wait_ge(selt, 1)
                act.activation(selT[:], psum[0:E, 4:8, :].rearrange("e q n -> e (q n)"), ACT.Copy).then_inc(seltd, 1)
                with act.Fori(0, E // 2) as p:
                    for k in range(2 * B):
                        par, b = k // B, k % B
                        n0 = 2 * NB * p + C * k
                        if k >= 2:
                            act.wait_ge(s_y, 2 * B * p + k - 1)
                        for c in range(C):
                            act.wait_ge(s_h, n0 + c + 1)
                            act.activation(hT[:, k % 2, c, :], psum[:, c, :], ACT.Gelu_apprx_tanh,
                                           bias=b1[:, par, c:c + 1]).then_inc(s_ge, 1)
                act.wait_ge(mv_d, NT)
                act.activation(rstd[:], mv[:, :, 1], ACT.Sqrt, bias=epsc[:, 0:1]).then_inc(sq, 1)

            @block.vector
            def _(v):
                step = [0]

                def link(ins):
                    step[0] += 1
                    ins.then_inc(gate, 1)
                    v.wait_ge(gate, step[0])

                def per_tile(a):
                    return a.rearrange("p (t a) -> p t a", a=1).to_broadcast([P, NT, E])

                def all_tiles(a):
                    return a.rearrange("p (a e) -> p a e", a=1).to_broadcast([P, NT, E])

                v.wait_ge(c_in, 64)
                v.wait_ge(logit, 1)
                link(v.tensor_tensor(pr[:], psum[:, 3, 0:NT * E].rearrange("p (t e) -> p t e", e=E),
                                     all_tiles(bgb[:]), ALU.add))
                link(v.tensor_reduce(m[:], pr[:], AX_X, ALU.max))
                link(v.tensor_tensor(pr[:], pr[:], per_tile(m[:]), ALU.subtract))
                choose(v, link, gexp, pr, left, hit, sel, m, order, per_tile, all_tiles)
                v.wait_ge(accp, 1)
                v.tensor_tensor(acc[:], psum[:, 4:8, :].rearrange("p q (k d) -> p (q k) d", k=4), x2[:],
                                ALU.add).then_inc(s_acc, 1)
                v.wait_ge(s_acc, 1)
                with v.Fori(0, E // 2) as p:
                    for k in range(2 * B):
                        par, b = k // B, k % B
                        v.wait_ge(s_y, 2 * B * p + k + 1)
                        v.wait_ge(s_acc, 1 + 2 * NT * p + 4 * max(0, k - B + 1))
                        for q in range(4):
                            i = 4 * b + q
                            v.scalar_tensor_tensor(acc[:, i, :], psum[:, 4 + k % 2, q * P:(q + 1) * P],
                                                   sel[:, i, bass.ds(2 * p + par, 1)], acc[:, i, :],
                                                   ALU.mult, ALU.add).then_inc(s_acc, 1)
                v.wait_ge(s_acc, 1 + NT * E)
                layer_norm(v, acc, st, mv, st_d, mv_d, 0, NT)
                v.wait_ge(sq, 1)
                v.reciprocal(rstd[:], rstd[:]).then_inc(rs_d, 1)
                v.wait_ge(rs_d, 1)
                for i in range(NT):
                    v.tensor_scalar(acc[:, i, :], acc[:, i, :], mv[:, i, 0:1], rstd[:, i:i + 1],
                                    ALU.subtract, ALU.mult).then_inc(fin, 1)

            @block.tensor
            def _(pe):
                pe.wait_ge(c_in, 64)
                for i in range(NT):
                    last = pe.matmul(psum[:, 3, i * E:(i + 1) * E], x2T[:, i * P:(i + 1) * P], wg[:],
                                     start=True, stop=True)
                last.then_inc(logit, 1)
                pe.wait_ge(gate, GATE_STEPS)
                for i in range(NT):
                    last = pe.transpose(psum[0:E, 4 + i // 4, (i % 4) * P:(i % 4 + 1) * P], sel[:, i, :], ident[:])
                last.then_inc(selt, 1)
                pe.wait_ge(seltd, 1)
                for i in range(NT):
                    last = pe.matmul(psum[:, 4 + i // 4, (i % 4) * P:(i % 4 + 1) * P], selT[:, i * P:(i + 1) * P],
                                     b2[:], start=True, stop=True)
                last.then_inc(accp, 1)
                pe.wait_ge(s_acc, 1)

                def hidden(p, k):
                    par, b = k // B, k % B
                    n0 = 2 * NB * p + C * k
                    if b == 0:
                        pe.wait_ge(w_in[par], 48 * (p + 1))
                    for c in range(C):
                        if k:
                            pe.wait_ge(s_ge, n0 + c + 1 - C)
                        pe.matmul(psum[:, c, :], w1[:, par, c * P:(c + 1) * P], x2T[:, b * S:(b + 1) * S],
                                  start=True, stop=True).then_inc(s_h, 1)

                def down(p, k):
                    par, b = k // B, k % B
                    pe.wait_ge(s_ge, 2 * NB * p + C * k + C)
                    if k >= 2:
                        pe.wait_ge(s_acc, 1 + 2 * NT * p + 4 * (k - 1))
                    else:
                        pe.wait_ge(s_acc, 1 + 2 * NT * p)
                    for q in range(4):
                        for c in range(C):
                            last = pe.matmul(psum[:, 4 + k % 2, q * P:(q + 1) * P],
                                             hT[:, k % 2, c, q * P:(q + 1) * P], w2[:, par, c, :],
                                             start=c == 0, stop=c == C - 1)
                    last.then_inc(s_y, 1)

                with pe.Fori(0, E // 2) as p:
                    for k in range(2 * B + 1):
                        if k < 2 * B:
                            hidden(p, k)
                        if k:
                            down(p, k - 1)


GATE_STEPS = 25


def choose(v, link, gexp, pr, left, hit, sel, m, order, per_tile, all_tiles):
    v.wait_ge(gexp, 1)
    link(v.tensor_reduce(m[:], pr[:], AX_X, ALU.add))
    link(v.reciprocal(m[:], m[:]))
    link(v.tensor_tensor(pr[:], pr[:], per_tile(m[:]), ALU.mult))
    link(v.tensor_copy(left[:], pr[:]))
    for n in range(2):
        link(v.tensor_reduce(m[:], left[:], AX_X, ALU.max))
        link(v.tensor_tensor(hit[:], left[:], per_tile(m[:]), ALU.is_ge))
        link(v.tensor_tensor(hit[:], hit[:], all_tiles(order[:]), ALU.mult))
        link(v.tensor_reduce(m[:], hit[:], AX_X, ALU.max))
        link(v.tensor_tensor(hit[:], all_tiles(order[:]), per_tile(m[:]), ALU.is_equal))
        link(v.scalar_tensor_tensor(left[:], hit[:], -2.0, left[:], ALU.mult, ALU.add))
    link(v.tensor_scalar(hit[:], left[:], 0.0, None, ALU.is_lt))
    link(v.tensor_tensor(sel[:], pr[:], hit[:], ALU.mult))
    link(v.tensor_reduce(m[:], sel[:], AX_X, ALU.add))
    link(v.tensor_scalar(m[:], m[:], 1e-8, None, ALU.add))
    link(v.reciprocal(m[:], m[:]))
    link(v.tensor_tensor(sel[:], sel[:], per_tile(m[:]), ALU.mult))


def in_bands(a):
    a = np.asarray(a)
    out = np.zeros(a.shape[:-1] + (HG, 4, BAND), a.dtype)
    src = a.reshape(a.shape[:-1] + (HG, 4, HD))
    for k in range(3):
        out[..., k * HD:(k + 1) * HD] = src
    return out.reshape(a.shape[:-1] + (HG, P))


def shape_constants():
    f32 = np.float32
    inv = f32(1.0) / np.power(f32(10000.0), np.arange(0, D, 2, dtype=f32) / f32(D))
    w = np.repeat(inv.astype(f32).astype(np.float64), 2)[:, None]
    odd = (np.arange(D) % 2 == 1)[:, None]
    j = np.arange(S)[None, :]

    def table(pos):
        return np.where(odd, np.cos(pos * w), np.sin(pos * w))
    turn = (S - 1 - j) * w
    tabs = np.stack([table(j), table(j - S)], axis=1)
    cs = np.stack([np.cos(turn), np.where(odd, np.sin(turn), -np.sin(turn))], axis=1)
    row = np.arange(P)[:, None]
    in_band = row % BAND // HD
    negc = np.concatenate([-(in_band == 2).astype(f32), -(in_band == 1).astype(f32)], axis=1)
    col = np.arange(S)[None, :]
    return {
        "ident": np.eye(P, dtype=f32), "negc": negc, "tabs": tabs.astype(f32), "cs": cs.astype(f32),
        "peS": table(np.array([[S]])).astype(f32), "bandm": (row // BAND == np.arange(4)[None, :]).astype(f32),
        "maskU": (col >= row + 2).astype(np.uint32), "maskS": (col == row + 1)[:, 0:ZONE].astype(f32),
        "order": np.tile(np.arange(E, 0, -1, dtype=f32), (P, 1)),
    }


def kernel(x, ctx_1024, L0_attn_Wq, L0_attn_bq, L0_attn_Wk, L0_attn_bk, L0_attn_Wv, L0_attn_bv, L0_attn_Wpos,
           L0_attn_Wf, L0_attn_bf, L0_attn_u, L0_attn_v, L0_attn_gamma, L0_attn_beta, L0_xattn_wq, L0_xattn_wk,
           L0_xattn_wv, L0_xattn_wo, L0_xattn_bo, L0_ffn_Wg, L0_ffn_bg, L0_ffn_W1, L0_ffn_b1, L0_ffn_W2,
           L0_ffn_b2):
    import concourse.bacc as bacc
    from concourse.bass_utils import run_bass_kernel_spmd

    A = np.asarray
    wq, wk = (in_bands(w).transpose(1, 0, 2) for w in (L0_attn_Wq, L0_attn_Wk))
    cols = [in_bands(A(c).reshape(D))[:, :, None] for c in (L0_attn_bq, L0_attn_bk, L0_attn_u, L0_attn_v)]
    posC = in_bands(L0_attn_Wpos).transpose(1, 0, 2)
    posT = posC.transpose(0, 2, 1)
    swapped = posT.reshape(HG, P, D // 2, 2)[..., ::-1].reshape(HG, P, D)
    arrays = {
        "x": x, "ctx": ctx_1024, "wst": np.concatenate([wq, wk] + cols, axis=2),
        "wposT": np.stack([posT, swapped], axis=1), "wposC": posC,
        "gb": np.stack([A(L0_attn_gamma), A(L0_attn_beta)], axis=1),
        "wv": L0_attn_Wv, "bv": A(L0_attn_bv).reshape(1, D), "wf": L0_attn_Wf, "bf": A(L0_attn_bf).reshape(1, D),
        "wq2": in_bands(A(L0_xattn_wq).T).transpose(1, 0, 2), "wk2": in_bands(A(L0_xattn_wk).T).transpose(1, 0, 2),
        "wv2": A(L0_xattn_wv).T, "wo2": A(L0_xattn_wo).T, "bo": A(L0_xattn_bo).reshape(1, D),
        "wg": L0_ffn_Wg, "bg": A(L0_ffn_bg).reshape(1, E), "w1": L0_ffn_W1,
        "b1": A(L0_ffn_b1).reshape(E, HID // P, P).transpose(0, 2, 1), "w2": L0_ffn_W2, "b2": L0_ffn_b2,
    }
    arrays.update(shape_constants())
    nc = bacc.Bacc("TRN2", target_bir_lowering=False, num_devices=1)
    feed, t = {}, {}
    for name, a in arrays.items():
        a = np.ascontiguousarray(a)
        feed[f"in_{name}"] = a
        t[name] = nc.dram_tensor(f"in_{name}", a.shape, mybir.dt.from_np(a.dtype), kind="ExternalInput").ap()
    out = nc.dram_tensor("out_0", (B, S, D), F32, kind="ExternalOutput").ap()
    decoder_kernel(nc, t, out)
    r = run_bass_kernel_spmd(nc, [feed], core_ids=[0])
    return r.results[0]["out_0"]
```

```python
from contextlib import ExitStack

import numpy as np

import concourse.bass as bass
from concourse import mybir

F32 = mybir.dt.float32
F32R = mybir.dt.float32r
U32 = mybir.dt.uint32
ALU = mybir.AluOpType
ACT = mybir.ActivationFunctionType
AX_X = mybir.AxisListType.X

P = 128
B, S, D = 4, 512, 128
H, HD = 16, 8
NT = B * S // P
QB = S // P
HG = 4
BAND = 32
M2 = 77
E = 8
HID = 4 * D
EPS = 1e-5
PASSES = (0, 0), (0, 1), (1, 0)
ZONE = P + 2
SCALE = float(D) ** -0.5
SCALE2 = float(HD) ** -0.5
ITS = B * HG
UPP = 2 * 4 * QB
WST = 2 * P + 4
LAG = 3
LEAD = 7


def zone(i):
    return P * i, min(ZONE, S - P * i)


def first(p):
    return isinstance(p, int) and p == 0


def decoder_kernel(nc, t, out):
    with ExitStack() as ctx:
        def sb(name, shape, dt=F32):
            return ctx.enter_context(nc.sbuf_tensor(name, shape, dt))

        def sem(name):
            return ctx.enter_context(nc.semaphore(name))

        ident = sb("ident", [P, P])
        epsc = sb("epsc", [P, 1])
        attn = sb("attn", [P, NT, D])
        psum = ctx.enter_context(nc.psum_tensor("psum", [P, 8, 512], F32))
        xr = sb("xr", [P, NT, D])
        c = {"ctx": sb("c_ctx", [M2, B, D]), "wf": sb("c_wf", [P, D]), "bf": sb("c_bf", [P, D]),
             "bo": sb("c_bo", [P, D]), "wq2": sb("c_wq2", [P, HG, P]), "wk2": sb("c_wk2", [P, HG, P]),
             "wv2": sb("c_wv2", [P, D]), "wo2": sb("c_wo2", [P, D]), "negc": sb("c_negc", [P, 2])}
        c_loaded = sem("cross_inputs_loaded")

        self_attention(nc, t, ident, epsc, attn, psum, xr, c, c_loaded)
        with ExitStack() as late:
            def lsb(name, shape, dt=F32):
                return late.enter_context(nc.sbuf_tensor(name, shape, dt))

            x2T = lsb("x2T", [P, B * S])
            x2Th = lsb("x2Th", [P, B * S], F32R)
            x2Tl = lsb("x2Tl", [P, B * S], F32R)
            w = ExpertWeights(lsb, sem)
            cross_attention(nc, t, ident, epsc, attn, xr, c, x2T, x2Th, x2Tl, w, psum)
            experts(nc, t, ident, epsc, x2T, x2Th, x2Tl, w, psum, out)


def self_attention(nc, t, ident, epsc, attn, psum, xr, c, c_loaded):
    with ExitStack() as ctx:
        def sb(name, shape, dt=F32):
            return ctx.enter_context(nc.sbuf_tensor(name, shape, dt))

        def sem(name):
            return ctx.enter_context(nc.semaphore(name))

        xnT = sb("xnT", [P, B * S])
        v_all = sb("v_all", [P, NT, D])
        tabs = sb("tabs", [P, 2, 2, S], F32R)
        cs = sb("cs", [P, 2, S])
        wpf = sb("wpf", [P, HG, 2, P], F32R)
        psz = sb("psz", [P, HG, 4], F32R)
        negc = sb("negc", [P, 2])
        bandm = sb("bandm", [P, 4])
        maskU = sb("maskU", [P, S], U32)
        maskS = sb("maskS", [P, ZONE])
        wz = sb("wz", [P, 4, 2, P], F32R)

        wst = sb("wst", [P, 2, WST])
        w_in = [sem("wst_in0"), sem("wst_in1")]
        zeroed = sem("zeroed")
        s_wz = sem("s_wz")

        with ExitStack() as ca:
            def sba(name, shape, dt=F32):
                return ca.enter_context(nc.sbuf_tensor(name, shape, dt))

            x = xr
            xh = sba("xh", [P, NT, D])
            st = sba("ln_st", [P, NT, 6])
            mv = sba("ln_mv", [P, NT, 2])
            rstd = sba("ln_rstd", [P, NT])
            gb = sba("gb", [P, 2])
            wv = sba("wv", [P, P])
            bvb = sba("bvb", [P, P])
            wposr = sba("wposr", [P, HG, 2, P])
            wposh = sba("wposh", [P, HG, 2, P], F32R)
            wposc = sba("wposc", [P, HG, P])
            tabr = sba("tabr", [P, 2, S])
            peS = sba("peS", [P, 1])
            pSr = sba("pSr", [P, HG])
            pSh = sba("pSh", [P, HG], F32R)
            pSt = sba("pSt", [P, HG])
            x_in = [sem(f"a_x_loaded{q}") for q in range(B)]
            id_in = sem("a_ident_loaded")
            c_in = sem("a_consts_loaded")
            wa_in = sem("a_weights_loaded")
            tab_hi = sem("a_tables_high")
            tab_lo = sem("a_tables_low")
            stat = sem("a_stats")
            sq = sem("a_sqrt")
            rs = sem("a_rstd")
            xhs = sem("a_xhat")
            tp = sem("a_transposed")
            xe = sem("a_xnT")
            vp = sem("a_v_psum")
            ve = sem("a_v")
            sp_hi = sem("a_split_high")
            sp_lo = sem("a_split_done")
            pp = sem("a_pos_psum")
            epsm = sem("a_eps")
            warm = sem("a_warm")
            with nc.Block() as block:
                @block.sync
                def _(sp):
                    for q in (0, 2):
                        sp.dma_start(x[:, 4 * q:4 * q + 4, :],
                                     t["x"][q].rearrange("(t p) d -> p t d", p=P)).then_inc(x_in[q], 16)
                    for dst, src in ((ident[:], t["ident"]), (gb[:], t["gb"])):
                        sp.dma_start(dst, src).then_inc(id_in, 16)
                    for dst, src in ((negc[:], t["negc"]),
                                     (bandm[:], t["bandm"]), (maskU[:], t["maskU"]), (maskS[:], t["maskS"]),
                                     (peS[:], t["peS"])):
                        sp.dma_start(dst, src).then_inc(c_in, 16)
                    sp.dma_start(wst[:, 0, :], t["wst"][0]).then_inc(w_in[0], 16)
                    sp.dma_start(cs[:], t["cs"]).then_inc(c_in, 16)
                    sp.dma_start(wst[:, 1, :], t["wst"][0]).then_inc(w_in[1], 16)

                @block.scalar
                def _(act):
                    for q in (1, 3):
                        act.dma_start(x[:, 4 * q:4 * q + 4, :],
                                      t["x"][q].rearrange("(t p) d -> p t d", p=P)).then_inc(x_in[q], 16)
                    act.dma_start(tabr[:], t["tabs"]).then_inc(wa_in, 16)
                    act.dma_start(wposr[:], t["wposT"].rearrange("g v p c -> p g v c")).then_inc(wa_in, 16)
                    act.dma_start(wposc[:], t["wposC"].rearrange("g c r -> c g r")).then_inc(wa_in, 16)
                    act.dma_start(wv[:], t["wv"]).then_inc(wa_in, 16)
                    act.dma_start(bvb[:], t["bv"].to_broadcast([P, P])).then_inc(wa_in, 16)
                    act.wait_ge(epsm, 1)
                    act.activation(rstd[:, 0:1], epsc[:], ACT.Sqrt).then_inc(warm, 1)
                    act.wait_ge(warm, 1)
                    act.wait_ge(stat, NT)
                    act.activation(rstd[:], mv[:, :, 1], ACT.Sqrt, bias=epsc[:, 0:1]).then_inc(sq, 1)
                    act.wait_ge(id_in, 32)
                    for q in range(4):
                        act.wait_ge(tp, q + 1)
                        act.activation(xnT[:, q * 512:(q + 1) * 512], psum[:, q, :], ACT.Identity,
                                       bias=gb[:, 1:2], scale=gb[:, 0:1]).then_inc(xe, 1)

                @block.gpsimd
                def _(pool):
                    pool.memset(epsc[:], EPS).then_inc(epsm, 1)
                    pool.memset(wz[:].bitcast(F32), 0.0).then_inc(zeroed, 1)
                    pool.wait_ge(wa_in, 16 * 5)
                    pool.tensor_copy(tabs[:, :, 0, :], tabr[:]).then_inc(tab_hi, 1)
                    pool.wait_ge(tab_hi, 1)
                    pool.tensor_tensor(tabs[:, :, 1, :], tabr[:], tabs[:, :, 0, :].bitcast(F32),
                                       ALU.subtract).then_inc(tab_lo, 1)
                    pool.wait_ge(sp_lo, 1)
                    pool.wait_ge(zeroed, 1)
                    for r in range(4):
                        rows = slice(BAND * r, BAND * r + BAND)
                        pool.tensor_copy(wz[rows, r, :, :], wpf[rows, 0, :, :]).then_inc(s_wz, 1)
                        pool.wait_ge(s_wz, r + 1)

                @block.vector
                def _(v):
                    for i in range(NT):
                        if i % 4 == 0:
                            v.wait_ge(x_in[i // 4], 16)
                        v.bn_stats(st[:, i, :], x[:, i, :]).then_inc(rs, 1)
                    v.wait_ge(rs, NT)
                    for i in range(NT):
                        v.bn_aggr(mv[:, i, :], st[:, i, :]).then_inc(stat, 1)
                    v.wait_ge(sq, 1)
                    v.reciprocal(rstd[:], rstd[:]).then_inc(rs, 1)
                    v.wait_ge(rs, NT + 1)
                    for i in range(NT):
                        v.tensor_scalar(xh[:, i, :], x[:, i, :], mv[:, i, 0:1], rstd[:, i:i + 1],
                                        ALU.subtract, ALU.mult).then_inc(xhs, 1)
                    v.wait_ge(wa_in, 16 * 5)
                    v.wait_ge(c_in, 16 * 6)
                    v.tensor_copy(wposh[:], wposr[:]).then_inc(sp_hi, 1)
                    v.wait_ge(sp_hi, 1)
                    wf = wpf[:].rearrange("p g v c -> p (g v c)")
                    v.scalar_tensor_tensor(wf, wposh[:].rearrange("p g v c -> p (g v c)").bitcast(F32),
                                           negc[:, 1:2], wposr[:].rearrange("p g v c -> p (g v c)"),
                                           ALU.mult, ALU.add).then_inc(sp_lo, 1)
                    v.wait_ge(pp, 1)
                    v.tensor_copy(pSr[:], psum[:, 7, 0:HG]).then_inc(sp_hi, 1)
                    v.wait_ge(sp_hi, 2)
                    v.tensor_copy(pSh[:], pSr[:]).then_inc(sp_hi, 1)
                    v.wait_ge(sp_hi, 3)
                    v.scalar_tensor_tensor(pSt[:], pSh[:].bitcast(F32), negc[:, 1:2], pSr[:],
                                           ALU.mult, ALU.add).then_inc(sp_lo, 1)
                    v.wait_ge(sp_lo, 2)
                    for g in range(HG):
                        v.tensor_scalar(psz[:, g, :], bandm[:], pSt[:, g:g + 1], None,
                                        ALU.mult).then_inc(sp_lo, 1)
                    for q in range(4):
                        v.wait_ge(vp, q + 1)
                        v.tensor_tensor(v_all[:, 4 * q:4 * q + 4, :],
                                        psum[:, q + 4, :].rearrange("p (t d) -> p t d", t=4),
                                        bvb[:].rearrange("p (a d) -> p a d", a=1).to_broadcast([P, 4, D]),
                                        ALU.add).then_inc(ve, 1)

                @block.tensor
                def _(pe):
                    pe.wait_ge(id_in, 32)
                    for q in range(4):
                        pe.wait_ge(xhs, 4 * q + 4)
                        for k in range(4):
                            last = pe.transpose(psum[:, q, k * P:(k + 1) * P], xh[:, 4 * q + k, :], ident[:])
                        last.then_inc(tp, 1)
                    pe.wait_ge(c_in, 16 * 6)
                    pe.wait_ge(wa_in, 16 * 5)
                    for g in range(HG):
                        last = pe.matmul(psum[:, 7, g:g + 1], wposc[:, g, :], peS[:], start=True, stop=True)
                    last.then_inc(pp, 1)
                    for q in range(4):
                        pe.wait_ge(xe, q + 1)
                        if q == 3:
                            pe.wait_ge(sp_hi, 2)
                        for k in range(4):
                            i = 4 * q + k
                            last = pe.matmul(psum[:, 4 + q, k * P:(k + 1) * P], xnT[:, i * P:(i + 1) * P],
                                             wv[:], start=True, stop=True)
                        last.then_inc(vp, 1)

        full = sb("full", [P, 3, S])
        high = sb("high", [P, 3, S], F32R)
        bias = sb("bias", [P, 2, 2])
        ks = sb("ks", [P, 2, S], F32R)
        qvs = sb("qvs", [P, 2, S], F32R)
        qs = sb("qs", [P, S], F32R)
        qz = sb("qz", [P, 2, 4, S], F32R)
        gh = sb("gh", [P, 2, 4, S + 2], F32R)
        gl = sb("gl", [P, 2, 4, S + 2], F32R)
        trig = sb("trig", [P, 2, 2, S])
        gsum = sb("gsum", [P, 2, S])
        negz = sb("negz", [P, 2, 16])
        vz = sb("vz", [P, 2, QB, 4, BAND])
        prob = sb("prob", [P, 4, S])
        probT = sb("probT", [P, 2, 4, QB, P])
        nmax = sb("nmax", [P, 4])
        rsum = sb("rsum", [P, 2, 16])
        rinv = sb("rinv", [P, 2, 4])
        oT = sb("oT", [P, 2, P])

        psS = [psum[:, k, :] for k in range(4)]
        psU = psum[:, 4, :]
        TURNS = (7, 8, 9, 10, 12, 13, 14, 15)
        psT = psum[:, 5, :]
        psO = psum[:, 6, :]
        psG = psum[:, 7, :]
        HS = S // 2
        early = psG, psT

        s_bias = sem("s_bias")
        s_proj = sem("s_proj")
        s_full = sem("s_full")
        s_high = sem("s_high")
        s_stack = sem("s_stack")
        s_xbf = sem("s_xbf")
        s_qz = sem("s_qz")
        s_vz = sem("s_vz")
        s_g = sem("s_g")
        s_rot = sem("s_rot")
        s_gsum = sem("s_gsum")
        s_gh = sem("s_gh")
        s_gl = sem("s_gl")
        s_z = sem("s_z")
        s_negz = sem("s_negz")
        s_score = sem("s_score")
        s_pred = sem("s_pred")
        s_zfix = sem("s_zfix")
        s_max = sem("s_max")
        s_exp = sem("s_exp")
        s_tr = sem("s_tr")
        s_evac = sem("s_evac")
        s_pv = sem("s_pv")
        s_oT = sem("s_oT")
        s_trO = sem("s_trO")
        s_rinv = sem("s_rinv")
        s_norm = sem("s_norm")
        SPLIT_AT = {1: 1, 2: 2, 0: 3}
        NSTK = 3

        with nc.Block() as block:
            @block.sync
            def _(sp):
                for dst, src in ((c["wf"][:], t["wf"]), (c["bf"][:], t["bf"].to_broadcast([P, D])),
                                 (c["bo"][:], t["bo"].to_broadcast([P, D])), (c["negc"][:], t["negc"]),
                                 (c["wq2"][:], t["wq2"].rearrange("g e r -> e g r")),
                                 (c["wk2"][:], t["wk2"].rearrange("g e r -> e g r")),
                                 (c["wv2"][:], t["wv2"]), (c["wo2"][:], t["wo2"]),
                                 (c["ctx"][:], t["ctx"].rearrange("b m d -> m b d"))):
                    sp.dma_start(dst, src).then_inc(c_loaded, 16)
                for it in range(2, ITS):
                    sp.wait_ge(s_full, 3 * (it - 1))
                    sp.dma_start(wst[:, it % 2, :], t["wst"][it // 4 % HG]).then_inc(w_in[it % 2], 16)

            @block.gpsimd
            def _(pool):
                def weights(it):
                    g = (it >> 2) & 3
                    pool.wait_ge(s_g, 8 * it)
                    pool.wait_ge(s_gl, 4 * it)
                    for r in range(4):
                        b = slice(BAND * r, BAND * r + BAND)
                        pool.tensor_copy(wz[b, r, :, :], wpf[b, bass.ds(g, 1), :, :]
                                         .rearrange("p a v c -> p (a v) c")).then_inc(s_wz, 1)
                        pool.wait_ge(s_wz, 4 * it + r + 1)

                def values(it, par, first):
                    g, b = (it >> 2) & 3, it & 3
                    if not first:
                        pool.wait_ge(s_pv, 4 * (it - 1) + 1)
                    for j in range(QB):
                        src = v_all[:, bass.ds(4 * b + j, 1), bass.ds(BAND * g, BAND)]
                        pool.tensor_copy(vz[:, par, j, :, 0:HD],
                                         src.rearrange("p a (r d) -> p (a r) d", r=4)).then_inc(s_vz, 1)

                def table(it, par, r):
                    pool.wait_ge(s_rot, 8 * it + 2 * r + 2)
                    if r >= 2:
                        pool.wait_ge(s_gl, 4 * it + r - 1)
                    pool.tensor_tensor(gsum[:, r % 2, :], trig[:, r % 2, 0, :], trig[:, r % 2, 1, :],
                                       ALU.add).then_inc(s_gsum, 1)
                    pool.wait_ge(s_gh, 4 * it + r + 1)
                    pool.tensor_tensor(gl[:, par, r, 0:S], gsum[:, r % 2, :],
                                       gh[:, par, r, 0:S].bitcast(F32), ALU.subtract).then_inc(s_gl, 1)

                def prep(it, par, first=False):
                    if not first:
                        weights(it)
                    for r in range(4):
                        table(it, par, r)
                    values(it, par, first)

                pool.memset(gh[:, :, :, S:S + 2].bitcast(F32), 0.0).then_inc(zeroed, 1)
                pool.memset(gl[:, :, :, S:S + 2].bitcast(F32), 0.0).then_inc(zeroed, 1)
                pool.memset(vz[:], 0.0).then_inc(zeroed, 1)
                pool.wait_ge(zeroed, 4)
                prep(0, 0, True)
                with pool.Fori(0, ITS // 2 - 1) as p:
                    prep(2 * p + 1, 1)
                    prep(2 * p + 2, 0)
                prep(ITS - 1, 1)
                pool.wait_ge(c_loaded, 16 * 9)
                pool.tensor_tensor(xr[:], xr[:], c["bf"][:].rearrange("p (a d) -> p a d", a=1)
                                   .to_broadcast([P, NT, D]), ALU.add).then_inc(s_xbf, 1)
                pool.wait_ge(s_xbf, 1)

            @block.scalar
            def _(act):
                def full_queries(it, par, turn):
                    act.wait_ge(s_proj, 2 * it + 1)
                    act.wait_ge(s_bias, it + 1)
                    if turn is not None:
                        act.wait_ge(s_stack, NSTK * it)
                    for k in range(2):
                        act.activation(full[:, k, :], psG, ACT.Identity, bias=bias[:, par, k:k + 1],
                                       scale=SCALE).then_inc(s_full, 1)

                def full_keys(it, par, bank=psG):
                    act.wait_ge(s_proj, 2 * it + 2)
                    act.activation(full[:, 2, :], bank, ACT.Identity,
                                   bias=wst[:, par, 2 * P + 1:2 * P + 2]).then_inc(s_full, 1)

                def split(it, k):
                    act.wait_ge(s_full, 3 * it + 2 + k // 2)
                    act.activation(high[:, k, :], full[:, k, :], ACT.Copy).then_inc(s_high, 1)

                def one_head(it, par, r):
                    act.wait_ge(s_stack, NSTK * it + 3)
                    act.activation(qz[:, par, r, :], qs[:], ACT.Copy, scale=bandm[:, r:r + 1]).then_inc(s_qz, 1)

                def high_part(it, par, r):
                    act.wait_ge(s_gsum, 4 * it + r + 1)
                    act.activation(gh[:, par, r, 0:S], gsum[:, r % 2, :], ACT.Copy).then_inc(s_gh, 1)

                def exp(p, u):
                    act.wait_ge(s_max, UPP * p + u + 1)
                    if u >= 4 or not first(p):
                        act.wait_ge(s_tr, UPP * p + u - 3)
                    act.activation(prob[:, u % 4, :], psS[u % 4], ACT.Exp, bias=nmax[:, u % 4:u % 4 + 1],
                                   accum_out=rsum[:, u // 16, u % 16:u % 16 + 1]).then_inc(s_exp, 1)

                def evac(p, u):
                    blk = u // 4
                    act.wait_ge(s_tr, UPP * p + u + 1)
                    if blk >= 2 or not first(p):
                        act.wait_ge(s_pv, 8 * p + blk - 1)
                    act.activation(probT[:, blk % 2, u % 4, :, :], psT.rearrange("p (j i) -> p j i", j=QB),
                                   ACT.Copy).then_inc(s_evac, 1)

                def slot(p, s, prep=True):
                    nxt, par, q = 2 * p + s // 16 + 1, (s // 16 + 1) % 2, s % 16
                    if prep and q == 0:
                        full_queries(nxt, par, p)
                    if prep and q == 3:
                        full_keys(nxt, par)
                    if s:
                        evac(p, s - 1)
                    elif not first(p):
                        evac(p - 1, UPP - 1)
                    exp(p, s)
                    if not prep:
                        return
                    if q in (0, 3, 4):
                        split(nxt, {0: 1, 3: 2, 4: 0}[q])
                    if q in (7, 9, 12, 14):
                        high_part(nxt, par, (7, 9, 12, 14).index(q))
                    if q in (8, 10, 11, 13):
                        one_head(nxt, par, (8, 10, 11, 13).index(q))

                full_queries(0, 0, None)
                full_keys(0, 0, bank=psT)
                for k in (1, 2, 0):
                    split(0, k)
                for r in range(4):
                    one_head(0, 0, r)
                    high_part(0, 0, r)
                for s in range(LEAD):
                    slot(0, s)
                with act.Fori(0, ITS // 2 - 1) as p:
                    for s in range(LEAD, UPP):
                        slot(p, s)
                    for s in range(LEAD):
                        slot(p + 1, s)
                for s in range(LEAD, UPP):
                    slot(ITS // 2 - 1, s, prep=s < UPP // 2)
                evac(ITS // 2 - 1, UPP - 1)

            @block.vector
            def _(v):
                def biases(it, par, turn):
                    v.wait_ge(w_in[par], 16 * (turn + 1))
                    v.tensor_scalar(bias[:, par, :], wst[:, par, 2 * P + 2:2 * P + 4],
                                    wst[:, par, 2 * P:2 * P + 1], SCALE, ALU.add, ALU.mult).then_inc(s_bias, 1)

                def stack(it, dst, k, c, b=slice(0, P)):
                    v.wait_ge(s_high, 3 * it + SPLIT_AT[k])
                    v.scalar_tensor_tensor(dst, high[b, k, :].bitcast(F32), negc[b, c:c + 1],
                                           full[b, k, :], ALU.mult, ALU.add).then_inc(s_stack, 1)

                def rotate(it, par, h, bank=psG):
                    r, c = h // 2, slice(h % 2 * HS, h % 2 * HS + HS)
                    v.wait_ge(s_g, 8 * it + h + 1)
                    if r >= 2:
                        v.wait_ge(s_gsum, 4 * it + r - 1)
                    v.tensor_tensor(trig[:, r % 2, :, c], bank.rearrange("p (v j) -> p v j", v=2), cs[:, :, c],
                                    ALU.mult).then_inc(s_rot, 1)

                def neg_z(it, par, bank=psG):
                    v.wait_ge(s_z, it + 1)
                    v.tensor_scalar(negz[:, par, :], bank[:, 0:16], -1.0, None, ALU.mult).then_inc(s_negz, 1)

                def take_upper(p, u):
                    z0, _ = zone(u % 16 // 4)
                    v.reg_add(scored, scored, 1)
                    v.wait_ge(zeroed, 4)
                    v.wait_ge(s_score, scored)
                    v.copy_predicated(psS[u % 4][:, z0:S], maskU[:, 0:S - z0], psU[:, z0:S]).then_inc(s_pred, 1)

                def fix(p, u):
                    par, i, r = u // 16, u % 16 // 4, u % 4
                    z0, zw = zone(i)
                    sc = psS[u % 4][:, z0:z0 + zw]
                    if u % 16 == 0:
                        v.wait_ge(s_negz, 2 * p + par + 1)
                    v.wait_ge(s_pred, UPP * p + u + 1)
                    v.scalar_tensor_tensor(sc, maskS[:, 0:zw], negz[:, par, 4 * i + r:4 * i + r + 1], sc,
                                           ALU.mult, ALU.add).then_inc(s_zfix, 1)

                def maximum(p, u):
                    v.wait_ge(s_zfix, UPP * p + u + 1)
                    v.tensor_reduce(nmax[:, u % 4:u % 4 + 1], psS[u % 4], AX_X, ALU.max,
                                    negate=True).then_inc(s_max, 1)

                def out_T(p, blk):
                    v.wait_ge(s_pv, 8 * p + blk + 1)
                    v.tensor_copy(oT[:, blk % 2, :], psO[:, 0:P]).then_inc(s_oT, 1)

                def invert(p, blk):
                    par, i = blk // 4, blk % 4
                    v.wait_ge(s_exp, UPP * p + 4 * blk + 4)
                    v.reciprocal(rinv[:, blk % 2, :], rsum[:, par, 4 * i:4 * i + 4]).then_inc(s_rinv, 1)

                def norm(p, blk):
                    par, i = blk // 4, blk % 4
                    it = 2 * p + par
                    v.wait_ge(s_trO, 8 * p + blk + 1)
                    v.wait_ge(s_rinv, 8 * p + blk + 1)
                    dst = attn[:, bass.ds(4 * (it & 3) + i, 1), bass.ds(BAND * ((it >> 2) & 3), BAND)]
                    v.tensor_tensor(dst.rearrange("p a (r d) -> p (a r) d", r=4),
                                    psO[:, P:2 * P].rearrange("p (r c) -> p r c", r=4)[:, :, 0:HD],
                                    rinv[:, blk % 2, :].rearrange("p (r a) -> p r a", a=1)
                                    .to_broadcast([P, 4, HD]), ALU.mult).then_inc(s_norm, 1)

                scored = v.alloc_register("scored")
                v.reg_mov(scored, 0)
                biases(0, 0, 0)
                v.wait_ge(zeroed, 4)
                stack(0, qvs[:, 0, :], 1, 0)
                for h in range(8):
                    rotate(0, 0, h, bank=early[h % 2])
                    if h == 1:
                        stack(0, ks[:, 0, :], 2, 1)
                        stack(0, qs[:], 0, 0)
                neg_z(0, 0, bank=psO)

                def slot(p, s, prep=True):
                    nxt, par, q = 2 * p + s // 16 + 1, (s // 16 + 1) % 2, s % 16
                    if prep and q == 0:
                        biases(nxt, par, p + s // 16)
                    if prep and q in TURNS:
                        rotate(nxt, par, TURNS.index(q))
                    if prep and q == 5:
                        neg_z(nxt, par)
                    finish(p, s)
                    if s < LEAD and not first(p):
                        finish(p - 1, s + UPP)
                    take_upper(p, s)
                    if s:
                        maximum(p, s - 1)
                    elif not first(p):
                        maximum(p - 1, UPP - 1)
                    fix(p, s)
                    if prep and q == 2:
                        stack(nxt, qvs[:, par, :], 1, 0)
                    if prep and q == 5:
                        stack(nxt, ks[:, par, :], 2, 1)
                    if prep and q == 6:
                        v.wait_ge(s_qz, 4 * nxt)
                        stack(nxt, qs[:], 0, 0)

                def finish(p, s):
                    if s >= 8 and s % 4 == 0:
                        out_T(p, (s - 8) // 4)
                        invert(p, (s - 8) // 4)
                    if s >= 10 and s % 4 == 2:
                        norm(p, (s - 10) // 4)

                for s in range(LEAD):
                    slot(0, s)
                with v.Fori(0, ITS // 2 - 1) as p:
                    for s in range(LEAD, UPP):
                        slot(p, s)
                    for s in range(LEAD):
                        slot(p + 1, s)
                for s in range(LEAD, UPP):
                    slot(ITS // 2 - 1, s, prep=s < UPP // 2)
                maximum(ITS // 2 - 1, UPP - 1)
                for s in range(UPP, UPP + LEAD):
                    finish(ITS // 2 - 1, s)

            @block.tensor
            def _(pe):
                def project_q(it, par, turn):
                    pe.wait_ge(w_in[par], 16 if turn is None else 16 * (turn + 1))
                    if turn is not None:
                        pe.wait_ge(s_rot, 8 * it)
                    pe.matmul(psG, wst[:, par, 0:P], xnT[:, bass.ds(S * (it & 3), S)], start=True,
                              stop=True).then_inc(s_proj, 1)

                def project_k(it, par, bank=psG):
                    if bank is psG:
                        pe.wait_ge(s_full, 3 * it + 2)
                    pe.matmul(bank, wst[:, par, P:2 * P], xnT[:, bass.ds(S * (it & 3), S)], start=True,
                              stop=True).then_inc(s_proj, 1)

                def positions(it, par, h, bank=psG, others=0):
                    r, c = h // 2, slice(h % 2 * HS, h % 2 * HS + HS)
                    if h > others:
                        pe.wait_ge(s_rot, 8 * it + h - others)
                    elif others:
                        pe.wait_ge(s_stack, 1)
                        pe.wait_ge(s_full, 3)
                    else:
                        pe.wait_ge(s_negz, it + 1)
                    pe.wait_ge(s_wz, 4 * it + r + 1)
                    out = bank.rearrange("p (v j) -> p v j", v=2)
                    pe.matmul(out[:, 0, :], wz[:, r, 0, :], qvs[:, par, c], start=True, stop=True)
                    pe.matmul(out[:, 1, :], wz[:, r, 1, :], qvs[:, par, c], start=True,
                              stop=True).then_inc(s_g, 1)

                def beside(it, par, bank=psG):
                    pe.wait_ge(s_stack, NSTK * it + 1)
                    pe.wait_ge(s_full, 3 * it + 3)
                    g = (it >> 2) & 3
                    for i in range(QB):
                        last = pe.matmul(bank[:, 4 * i:4 * i + 4], qvs[:, par, i * P:(i + 1) * P],
                                         psz[:, bass.ds(g, 1), :].rearrange("p a r -> p (a r)"),
                                         start=True, stop=True)
                    last.then_inc(s_z, 1)

                def scores_lower(p, u):
                    par, i, r = u // 16, u % 16 // 4, u % 4
                    it = 2 * p + par
                    nl = sum(zone(i))
                    if i == 0:
                        pe.wait_ge(s_gl, 4 * it + r + 1)
                        pe.wait_ge(s_gh, 4 * it + r + 1)
                        pe.wait_ge(s_qz, 4 * it + r + 1)
                    if u >= 4 or not first(p):
                        pe.wait_ge(s_exp, UPP * p + u - 3)
                    g = gh[:, par, r, i * P:(i + 1) * P], gl[:, par, r, i * P:(i + 1) * P]
                    pe.matmul(psS[u % 4][:, 0:nl], qz[:, par, r, i * P:(i + 1) * P], ks[:, par, 0:nl],
                              start=True, stop=False)
                    for a, k in PASSES:
                        pe.matmul(psS[u % 4][:, 0:nl], g[a], tabs[:, 0, k, 0:nl], start=False, stop=a == 1)

                def scores_upper(p, u):
                    par, i, r = u // 16, u % 16 // 4, u % 4
                    z0, _ = zone(i)
                    if u or not first(p):
                        pe.wait_ge(s_pred, UPP * p + u)
                    g = gh[:, par, r, i * P + 1:(i + 1) * P + 1], gl[:, par, r, i * P + 1:(i + 1) * P + 1]
                    pe.matmul(psU[:, z0:S], qz[:, par, r, i * P:(i + 1) * P], ks[:, par, z0:S],
                              start=True, stop=False)
                    for a, k in PASSES:
                        last = pe.matmul(psU[:, z0:S], g[a], tabs[:, 1, k, z0:S], start=False, stop=a == 1)
                    last.then_inc(s_score, 1)

                def turn_probs(p, u):
                    pe.wait_ge(s_exp, UPP * p + u + 1)
                    if u or not first(p):
                        pe.wait_ge(s_evac, UPP * p + u)
                    for j in range(QB):
                        last = pe.transpose(psT[:, j * P:(j + 1) * P], prob[:, u % 4, j * P:(j + 1) * P],
                                            ident[:])
                    last.then_inc(s_tr, 1)

                def weigh(p, blk):
                    par = blk // 4
                    pe.wait_ge(s_evac, UPP * p + 4 * blk + 4)
                    if blk or not first(p):
                        pe.wait_ge(s_norm, 8 * p + blk)
                    if blk % 4 == 0:
                        pe.wait_ge(s_vz, 4 * (2 * p + par) + 4)
                    for j in range(QB):
                        for r in range(4):
                            last = pe.matmul(psO[BAND * r:BAND * r + BAND, 0:P], vz[:, par, j, r, :],
                                             probT[:, blk % 2, r, j, :], start=j == 0, stop=j == QB - 1)
                    last.then_inc(s_pv, 1)

                def turn_out(p, blk):
                    pe.wait_ge(s_oT, 8 * p + blk + 1)
                    pe.transpose(psO[:, P:2 * P], oT[:, blk % 2, :], ident[:]).then_inc(s_trO, 1)

                project_q(0, 0, None)
                project_k(0, 0, bank=psT)
                for h in range(8):
                    positions(0, 0, h, bank=early[h % 2], others=1)
                beside(0, 0, bank=psO)
                def finish(p, s):
                    if LAG <= s < UPP + LAG:
                        turn_probs(p, s - LAG)
                    if s >= 7 and s % 4 == 3:
                        weigh(p, (s - 7) // 4)
                    if s >= 9 and s % 4 == 1:
                        turn_out(p, (s - 9) // 4)

                def slot(p, s, prep=True):
                    scores_lower(p, s)
                    finish(p, s)
                    if s < LEAD and not first(p):
                        finish(p - 1, s + UPP)
                    nxt, par, q = 2 * p + s // 16 + 1, (s // 16 + 1) % 2, s % 16
                    if prep:
                        if q == 0:
                            project_q(nxt, par, p + s // 16)
                        if q == 4:
                            project_k(nxt, par)
                        if q in TURNS:
                            positions(nxt, par, TURNS.index(q))
                        if q == 5:
                            beside(nxt, par)
                    scores_upper(p, s)

                for s in range(LEAD):
                    slot(0, s)
                with pe.Fori(0, ITS // 2 - 1) as p:
                    for s in range(LEAD, UPP):
                        slot(p, s)
                    for s in range(LEAD):
                        slot(p + 1, s)
                for s in range(LEAD, UPP):
                    slot(ITS // 2 - 1, s, prep=s < UPP // 2)
                for s in range(UPP, UPP + LEAD):
                    finish(ITS // 2 - 1, s)


CU = 2 * QB
CLEAD = 5
HH = H // 2


def cross_attention(nc, t, ident, epsc, attn, xr, c, x2T, x2Th, x2Tl, w, psum):
    with ExitStack() as ctx:
        def sb(name, shape, dt=F32):
            return ctx.enter_context(nc.sbuf_tensor(name, shape, dt))

        T = QB
        wide = sb("attT", [P, B, S])
        y = sb("y1", [P, NT, D])
        st = sb("st2", [P, NT, 6])
        mv = sb("mv2", [P, NT, 2])
        rstd = sb("rstd2", [P, NT])
        x1 = sb("x1", [P, NT, D])
        x1T = x2T[:].rearrange("p (b i) -> p b i", b=B)
        cT = sb("cT", [P, B, M2])
        q2f = sb("q2f", [P, 2, S])
        q2h = sb("q2h", [P, 2, S], F32R)
        q2s = sb("q2s", [P, B, HG, S], F32R)
        q2w = sb("q2w", [P, 2, HG, P], F32R)
        k2f = sb("k2f", [P, HG, B, M2])
        k2h = sb("k2h", [P, HG, B, M2], F32R)
        k2s = k2h
        k2z = sb("k2z", [P, HG, B, 4, M2], F32R)
        v2o = sb("v2o", [M2, B, H, HD + 1])
        v2z = sb("v2z", [M2, 2, H, BAND])
        pr = sb("pr2", [P, 4, HH, M2])
        mx = sb("mx2", [P, 2, HH])
        pT = sb("pT2", [M2, 2, HH, P])
        o2T = sb("o2T", [P, 2, HG, P])
        rin = sb("rin2", [P, 2, H])
        at2 = attn
        x2 = y

        names = ["zeroed", "attT_ps", "attT", "y_ps", "res", "st", "mv", "sq", "rstd", "x1", "x1bo", "x1T_ps",
                 "x1T", "cT_ps", "cT", "k_ps", "k_full", "k_high", "k_stack", "k_band", "v_ps", "v2", "q_ps", "q_full",
                 "q_high0", "q_high1", "q_stack", "q_tile", "v_tile", "score", "max", "sub", "exp",
                 "turned", "pT", "pv", "oT", "oN_ps", "inv",
                 "at2", "at2T_ps", "at2T", "y2_ps", "res2", "st2", "mv2", "sq2", "rstd2", "x2", "x2T_ps", "x2T",
                 "x2T_high",
                 "x2T_low"]
        s = {n: ctx.enter_context(nc.semaphore("c_" + n)) for n in names}

        def scores_of(u):
            return psum[:, 2 * (u % 2):2 * (u % 2) + 2, 0:4 * M2].rearrange("p g (r m) -> p g r m", r=4)

        bankO, bankN = 6, 7

        with nc.Block() as block:
            @block.sync
            def _(sp):
                w.load_consts(sp, t)
                for e in range(2):
                    w.load(sp, t, e, e)

            @block.gpsimd
            def _(pool):
                pool.memset(k2z[:].bitcast(F32), 0.0).then_inc(s["zeroed"], 1)
                pool.memset(v2z[:], 0.0).then_inc(s["zeroed"], 1)
                pool.memset(v2o[:, :, :, HD:HD + 1], 1.0).then_inc(s["zeroed"], 1)
                pool.wait_ge(s["zeroed"], 3)
                pool.wait_ge(s["k_stack"], 1)
                for r in range(4):
                    rows = slice(BAND * r, BAND * r + BAND)
                    pool.tensor_copy(k2z[rows, :, :, r, :].rearrange("p g b m -> p (g b) m"),
                                     k2s[rows].rearrange("p g b m -> p (g b) m")).then_inc(s["k_band"], 1)
                    pool.wait_ge(s["k_band"], r + 1)

                def bring_q(b, k):
                    pool.wait_ge(s["zeroed"], 3)
                    if k >= 2 or not first(b):
                        pool.wait_ge(s["score"], CU * b + 2 * k - 2)
                    pool.tensor_copy(q2w[:, k % 2, :, :], q2s[:, bass.ds(b, 1), :, k * P:(k + 1) * P]
                                     .rearrange("p a g i -> p (a g) i")).then_inc(s["q_tile"], 1)

                def bring_v(b, k):
                    pool.wait_ge(s["zeroed"], 3)
                    if k >= 2 or not first(b):
                        pool.wait_ge(s["pv"], CU * b + 2 * k - 2)
                    pool.tensor_copy(v2z[:, k % 2, :, 0:HD + 1], v2o[:, bass.ds(b, 1), :, :]
                                     .rearrange("m a h d -> m (a h) d")).then_inc(s["v_tile"], 1)

                def residual(b):
                    pool.tensor_tensor(xr[:, T * b:T * b + T, :], x1[:, T * b:T * b + T, :],
                                       c["bo"][:].rearrange("p (a d) -> p a d", a=1).to_broadcast([P, T, D]),
                                       ALU.add).then_inc(s["x1bo"], 1)

                pool.wait_ge(s["v2"], B)
                pool.wait_ge(s["q_stack"], HG)
                pool.wait_ge(s["x1"], NT)
                bring_q(0, 0)
                for k in range(1, T):
                    bring_q(0, k)
                    bring_v(0, k - 1)
                    residual(k - 1)
                pool.wait_ge(s["q_stack"], B * HG)
                with pool.Fori(1, B) as b:
                    bring_q(b, 0)
                    bring_v(b - 1, T - 1)
                    for k in range(1, T):
                        bring_q(b, k)
                        bring_v(b, k - 1)
                bring_v(B - 1, T - 1)
                residual(B - 1)
                for e in range(2):
                    w.split(pool, e, e, 0)

            @block.scalar
            def _(act):
                act.wait_ge(s["cT_ps"], 1)
                act.activation(cT[:].rearrange("p b m -> p (b m)"), psum[:, 4, 0:B * M2],
                               ACT.Copy).then_inc(s["cT"], 1)
                for b in range(B):
                    act.wait_ge(s["attT_ps"], b + 1)
                    act.activation(wide[:, b, :], psum[:, b, :], ACT.Copy).then_inc(s["attT"], 1)
                act.wait_ge(s["k_ps"], 1)
                for dst, done in ((k2f, s["k_full"]), (k2h, s["k_high"])):
                    act.activation(dst[:].rearrange("p g b m -> p g (b m)"), psum[:, 4:8, 0:B * M2],
                                   ACT.Copy).then_inc(done, 1)
                act.wait_ge(s["mv"], NT)
                act.activation(rstd[:], mv[:, :, 1], ACT.Sqrt, bias=epsc[:, 0:1]).then_inc(s["sq"], 1)
                for b in range(B + 1):
                    if b < B:
                        act.wait_ge(s["x1T_ps"], b + 1)
                        act.activation(x1T[:, b, :], psum[:, b, :], ACT.Copy).then_inc(s["x1T"], 1)
                    for n in range(HG * (b - 1), HG * b) if b else ():
                        act.wait_ge(s["q_ps"], n + 1)
                        if n >= 2:
                            act.wait_ge(s["q_stack"], n - 1)
                        act.activation(q2f[:, n % 2, :], psum[:, 4 + n % HG, :], ACT.Copy,
                                       scale=SCALE2).then_inc(s["q_full"], 1)
                        if n % 2:
                            act.activation(q2h[:, n % 2, :], psum[:, 4 + n % HG, :], ACT.Copy,
                                           scale=SCALE2).then_inc(s["q_high1"], 1)

                def exp(b, u):
                    act.wait_ge(s["sub"], CU * b + u + 1)
                    act.activation(pr[:, u % 4, :, :], pr[:, u % 4, :, :], ACT.Exp).then_inc(s["exp"], 1)

                def evac(b, u):
                    if u >= 2 or not first(b):
                        act.wait_ge(s["pv"], CU * b + u - 1)
                    for a in range(2):
                        act.wait_ge(s["turned"], 2 * (CU * b + u) + a + 1)
                        act.activation(pT[:, u % 2, 4 * a:4 * a + 4, :],
                                       psum[0:M2, 4 + a, :].rearrange("m (r i) -> m r i", r=4),
                                       ACT.Copy).then_inc(s["pT"], 1)

                def out_T(b, k):
                    act.wait_ge(s["pv"], CU * b + 2 * k + 2)
                    if k >= 2 or not first(b):
                        act.wait_ge(s["oN_ps"], T * b + k - 1)
                    act.activation(o2T[:, k % 2, :, :], psum[:, bankO, :].rearrange("p (g i) -> p g i", g=HG),
                                   ACT.Copy).then_inc(s["oT"], 1)

                def finish(b, u):
                    if 1 <= u <= CU:
                        evac(b, u - 1)
                    if 3 <= u < CU + 3 and u % 2 == 1:
                        out_T(b, (u - 3) // 2)

                def slot(b, u):
                    exp(b, u)
                    finish(b, u)
                    if u < CLEAD and not first(b):
                        finish(b - 1, u + CU)

                for u in range(CLEAD):
                    slot(0, u)
                with act.Fori(0, B - 1) as b:
                    for u in range(CLEAD, CU):
                        slot(b, u)
                    for u in range(CLEAD):
                        slot(b + 1, u)
                for u in range(CLEAD, CU):
                    slot(B - 1, u)
                for u in range(CU, CU + CLEAD):
                    finish(B - 1, u)
                for b in range(B):
                    act.wait_ge(s["at2T_ps"], b + 1)
                    act.activation(wide[:, b, :], psum[:, b, :], ACT.Copy).then_inc(s["at2T"], 1)
                for b in range(B):
                    if b % 2 == 0:
                        part = slice(b * T, b * T + 2 * T)
                        act.wait_ge(s["mv2"], part.stop)
                        act.activation(rstd[:, part], mv[:, part, 1], ACT.Sqrt,
                                       bias=epsc[:, 0:1]).then_inc(s["sq2"], 1)
                    act.wait_ge(s["x2T_ps"], b + 1)
                    act.activation(x2T[:, S * b:S * b + S], psum[:, 4 + b, :], ACT.Copy).then_inc(s["x2T"], 1)
                    act.activation(x2Th[:, S * b:S * b + S], psum[:, 4 + b, :], ACT.Copy).then_inc(s["x2T_high"], 1)

            @block.vector
            def _(v):
                def residual_and_stats(batches, y_ps, res, stats, ready=None):
                    for b in batches:
                        v.wait_ge(y_ps, b + 1)
                        if ready is not None:
                            v.wait_ge(ready, b + 1)
                        v.tensor_tensor(y[:, T * b:T * b + T, :], psum[:, b, :].rearrange("p (t d) -> p t d", t=T),
                                        xr[:, T * b:T * b + T, :], ALU.add).then_inc(res, 1)
                        v.wait_ge(res, b + 1)
                        for i in range(T * b, T * b + T):
                            v.bn_stats(st[:, i, :], y[:, i, :]).then_inc(stats, 1)

                def means(tiles, stats, mean):
                    v.wait_ge(stats, tiles.stop)
                    for i in tiles:
                        v.bn_aggr(mv[:, i, :], st[:, i, :]).then_inc(mean, 1)

                def normalise(tiles, dst, sq, inv, done, n=1):
                    v.wait_ge(sq, n)
                    part = slice(tiles.start, tiles.stop)
                    v.reciprocal(rstd[:, part], rstd[:, part]).then_inc(inv, 1)
                    v.wait_ge(inv, n)
                    for i in tiles:
                        v.tensor_scalar(dst[:, i, :], y[:, i, :], mv[:, i, 0:1], rstd[:, i:i + 1],
                                        ALU.subtract, ALU.mult).then_inc(done, 1)

                v.wait_ge(s["v_ps"], 1)
                for b in range(B):
                    v.tensor_copy(v2o[:, b, :, 0:HD], psum[0:M2, 7, b * D:(b + 1) * D]
                                  .rearrange("m (h d) -> m h d", h=H)).then_inc(s["v2"], 1)
                residual_and_stats(range(B), s["y_ps"], s["res"], s["st"])
                means(range(NT), s["st"], s["mv"])
                v.wait_ge(s["k_high"], 1)
                v.scalar_tensor_tensor(k2s[:].rearrange("p g b m -> p (g b m)"),
                                       k2h[:].rearrange("p g b m -> p (g b m)").bitcast(F32),
                                       c["negc"][:, 1:2], k2f[:].rearrange("p g b m -> p (g b m)"),
                                       ALU.mult, ALU.add).then_inc(s["k_stack"], 1)
                normalise(range(NT), x1, s["sq"], s["rstd"], s["x1"])
                for n in range(B * HG):
                    if n % 2 == 0:
                        v.wait_ge(s["q_full"], n + 1)
                        v.tensor_copy(q2h[:, n % 2, :], q2f[:, n % 2, :]).then_inc(s["q_high0"], 1)
                        v.wait_ge(s["q_high0"], n // 2 + 1)
                    else:
                        v.wait_ge(s["q_high1"], n // 2 + 1)
                    v.scalar_tensor_tensor(q2s[:, n // HG, n % HG, :], q2h[:, n % 2, :].bitcast(F32),
                                           c["negc"][:, 0:1], q2f[:, n % 2, :], ALU.mult,
                                           ALU.add).then_inc(s["q_stack"], 1)

                def shift(b, u):
                    v.wait_ge(s["score"], CU * b + u + 1)
                    v.tensor_reduce(mx[:, u % 2, :].rearrange("p (g r) -> p g r", g=2), scores_of(u), AX_X,
                                    ALU.max).then_inc(s["max"], 1)
                    v.wait_ge(s["max"], CU * b + u + 1)
                    if u >= 4 or not first(b):
                        v.wait_ge(s["turned"], 2 * (CU * b + u - 3))
                    v.tensor_tensor(pr[:, u % 4, :, :].rearrange("p (g r) m -> p g r m", g=2), scores_of(u),
                                    mx[:, u % 2, :].rearrange("p (g r a) -> p g r a", g=2, a=1)
                                    .to_broadcast([P, 2, 4, M2]), ALU.subtract).then_inc(s["sub"], 1)

                def norm(b, k):
                    n = psum[:, bankN, :].rearrange("p (h c) -> p h c", h=H)
                    v.wait_ge(s["oN_ps"], T * b + k + 1)
                    v.reciprocal(rin[:, k % 2, :].rearrange("p (h a) -> p h a", a=1),
                                 n[:, :, HD:HD + 1]).then_inc(s["inv"], 1)
                    v.wait_ge(s["inv"], T * b + k + 1)
                    v.tensor_tensor(at2[:, bass.ds(T * b + k, 1), :].rearrange("p a (h d) -> p (a h) d", h=H),
                                    n[:, :, 0:HD], rin[:, k % 2, :].rearrange("p (h a) -> p h a", a=1)
                                    .to_broadcast([P, H, HD]), ALU.mult).then_inc(s["at2"], 1)

                def finish(b, u):
                    if u >= 6 and u % 2 == 0:
                        norm(b, (u - 6) // 2)

                def slot(b, u):
                    finish(b, u)
                    if u < CLEAD and not first(b):
                        finish(b - 1, u + CU)
                    shift(b, u)

                for u in range(CLEAD):
                    slot(0, u)
                with v.Fori(0, B - 1) as b:
                    for u in range(CLEAD, CU):
                        slot(b, u)
                    for u in range(CLEAD):
                        slot(b + 1, u)
                for u in range(CLEAD, CU):
                    slot(B - 1, u)
                for u in range(CU, CU + CLEAD):
                    finish(B - 1, u)
                def rows(*batches):
                    residual_and_stats(batches, s["y2_ps"], s["res2"], s["st2"], ready=s["x1bo"])

                halves = range(NT // 2), range(NT // 2, NT)
                rows(0, 1)
                means(halves[0], s["st2"], s["mv2"])
                rows(2)
                normalise(halves[0], x2, s["sq2"], s["rstd2"], s["x2"], 1)
                rows(3)
                means(halves[1], s["st2"], s["mv2"])
                normalise(halves[1], x2, s["sq2"], s["rstd2"], s["x2"], 2)
                for b in range(B):
                    v.wait_ge(s["x2T_high"], b + 1)
                    v.tensor_tensor(x2Tl[:, S * b:S * b + S], x2T[:, S * b:S * b + S],
                                    x2Th[:, S * b:S * b + S].bitcast(F32), ALU.subtract).then_inc(s["x2T_low"], 1)

            @block.tensor
            def _(pe):
                def turn(bank, src, b, done):
                    for k in range(T):
                        last = pe.transpose(psum[:, bank, k * P:(k + 1) * P], src[:, T * b + k, :], ident[:])
                    last.then_inc(done, 1)

                def times(bank, src, w, done):
                    for k in range(T):
                        last = pe.matmul(psum[:, bank, k * P:(k + 1) * P], src[:, k * P:(k + 1) * P], w,
                                         start=True, stop=True)
                    last.then_inc(done, 1)

                for b in range(B):
                    last = pe.transpose(psum[:, 4, b * M2:(b + 1) * M2], c["ctx"][:, b, :], ident[0:M2, 0:M2])
                last.then_inc(s["cT_ps"], 1)
                for b in range(B):
                    turn(b, attn, b, s["attT_ps"])
                pe.wait_ge(s["cT"], 1)
                for b in range(B):
                    last = pe.matmul(psum[0:M2, 7, b * D:(b + 1) * D], cT[:, b, :], c["wv2"][:], start=True,
                                     stop=True)
                last.then_inc(s["v_ps"], 1)
                for b in range(B):
                    pe.wait_ge(s["attT"], b + 1)
                    times(b, wide[:, b, :], c["wf"][:], s["y_ps"])
                pe.wait_ge(s["v2"], B)
                for g in range(HG):
                    last = pe.matmul(psum[:, 4 + g, 0:B * M2], c["wk2"][:, g, :],
                                     cT[:].rearrange("p b m -> p (b m)"), start=True, stop=True)
                last.then_inc(s["k_ps"], 1)
                for b in range(B + 1):
                    if b < B:
                        pe.wait_ge(s["x1"], T * (b + 1))
                        turn(b, x1, b, s["x1T_ps"])
                    if b == 1:
                        pe.wait_ge(s["k_high"], 1)
                    if b:
                        pe.wait_ge(s["x1T"], b)
                    for n in range(HG * (b - 1), HG * b) if b else ():
                        if n >= HG:
                            if n % 2:
                                pe.wait_ge(s["q_high1"], n // 2 - 1)
                            else:
                                pe.wait_ge(s["q_full"], n - HG + 1)
                        pe.matmul(psum[:, 4 + n % HG, :], c["wq2"][:, n % HG, :], x1T[:, b - 1, :], start=True,
                                  stop=True).then_inc(s["q_ps"], 1)

                def scores(b, u):
                    k, h = u // 2, u % 2
                    if u >= 2 or not first(b):
                        pe.wait_ge(s["sub"], CU * b + u - 1)
                    if h == 0:
                        pe.wait_ge(s["q_tile"], T * b + k + 1)
                    for a in range(2):
                        g = 2 * h + a
                        last = pe.matmul(psum[:, 2 * (u % 2) + a, 0:4 * M2], q2w[:, k % 2, g, :],
                                         k2z[:, g, bass.ds(b, 1), :, :].rearrange("p a r m -> p (a r m)"),
                                         start=True, stop=True)
                    last.then_inc(s["score"], 1)

                def turn_probs(b, u):
                    pe.wait_ge(s["exp"], CU * b + u + 1)
                    for a in range(2):
                        if u or not first(b):
                            pe.wait_ge(s["pT"], 2 * (CU * b + u) + a - 1)
                        for r in range(4):
                            last = pe.transpose(psum[0:M2, 4 + a, r * P:(r + 1) * P], pr[:, u % 4, 4 * a + r, :],
                                                ident[:])
                        last.then_inc(s["turned"], 1)

                def weigh(b, u):
                    k, h = u // 2, u % 2
                    pe.wait_ge(s["pT"], 2 * (CU * b + u + 1))
                    if h == 0:
                        pe.wait_ge(s["v_tile"], T * b + k + 1)
                    if h == 0 and (k or not first(b)):
                        pe.wait_ge(s["oT"], T * b + k)
                    for a in range(2):
                        g = 2 * h + a
                        for r in range(4):
                            last = pe.matmul(psum[BAND * r:BAND * r + BAND, bankO, g * P:(g + 1) * P],
                                             v2z[:, k % 2, 4 * g + r, :],
                                             pT[:, u % 2, 4 * a + r, :], start=True, stop=True)
                    last.then_inc(s["pv"], 1)

                def turn_out(b, k):
                    pe.wait_ge(s["oT"], T * b + k + 1)
                    if k or not first(b):
                        pe.wait_ge(s["at2"], T * b + k)
                    for g in range(HG):
                        last = pe.transpose(psum[:, bankN, g * P:(g + 1) * P], o2T[:, k % 2, g, :], ident[:])
                    last.then_inc(s["oN_ps"], 1)

                def finish(b, u):
                    if 2 <= u < CU + 2:
                        turn_probs(b, u - 2)
                    if 3 <= u < CU + 3:
                        weigh(b, u - 3)
                    if u >= 5 and u % 2 == 1:
                        turn_out(b, (u - 5) // 2)

                def slot(b, u):
                    scores(b, u)
                    finish(b, u)
                    if u < CLEAD and not first(b):
                        finish(b - 1, u + CU)

                pe.wait_ge(s["k_band"], 4)
                for u in range(CLEAD):
                    slot(0, u)
                with pe.Fori(0, B - 1) as b:
                    for u in range(CLEAD, CU):
                        slot(b, u)
                    for u in range(CLEAD):
                        slot(b + 1, u)
                for u in range(CLEAD, CU):
                    slot(B - 1, u)
                for u in range(CU, CU + CLEAD):
                    finish(B - 1, u)
                for b in range(B):
                    pe.wait_ge(s["at2"], T * (b + 1))
                    turn(b, at2, b, s["at2T_ps"])
                for b in range(B):
                    pe.wait_ge(s["at2T"], b + 1)
                    times(b, wide[:, b, :], c["wo2"][:], s["y2_ps"])
                pe.wait_ge(w.consts_in, 16 * 5)
                for b in range(B + 1):
                    if b < B:
                        pe.wait_ge(s["x2"], T * (b + 1))
                        turn(4 + b, x2, b, s["x2T_ps"])
                    if b:
                        pe.wait_ge(s["x2T"], b)
                    for i in range(T * (b - 1), T * b) if b else ():
                        last = pe.matmul(psum[:, 0, i * E:(i + 1) * E], x2T[:, i * P:(i + 1) * P], w.wg[:],
                                         start=True, stop=True)
                last.then_inc(w.logits, 1)


class ExpertWeights:

    def __init__(self, sb, sem):
        C = HID // P
        self.w1, self.w2 = sb("w1", [P, 2, HID]), sb("w2", [P, 2, C, D])
        self.w1h, self.w1l = sb("w1h", [P, 2, HID], F32R), sb("w1l", [P, 2, HID], F32R)
        self.w2h, self.w2l = sb("w2h", [P, 2, C, D], F32R), sb("w2l", [P, 2, C, D], F32R)
        self.b1 = sb("b1", [P, 2, C])
        self.b2 = sb("b2", [P, E])
        self.wg, self.bg = sb("wg", [P, E]), sb("bg", [P, E])
        self.order = sb("order", [P, E])
        self.pick = sb("pick", [P, E, P])
        self.pickw = sb("pickw", [P, 2, P], F32R)
        self.loaded = [sem("e_w_in0"), sem("e_w_in1")]
        self.consts_in, self.logits = sem("e_consts_in"), sem("e_logits")
        self.high, self.split_done, self.picked = sem("e_w_high"), sem("e_w_split"), sem("e_pick")

    def load_consts(self, sp, t):
        for dst, src in ((self.wg[:], t["wg"]), (self.bg[:], t["bg"].to_broadcast([P, E])),
                         (self.order[:], t["order"]), (self.b2[:], t["b2"]), (self.pick[:], t["pick"])):
            sp.dma_start(dst, src).then_inc(self.consts_in, 16)

    def load(self, sp, t, e, par):
        sp.dma_start(self.w1[:, par, :], t["w1"][bass.ds(e, 1)].rearrange("a p n -> p (a n)")
                     ).then_inc(self.loaded[par], 16)
        sp.dma_start(self.w2[:, par, :, :], t["w2"][bass.ds(e, 1)].rearrange("a (c p) n -> p (a c) n", p=P)
                     ).then_inc(self.loaded[par], 16)
        sp.dma_start(self.b1[:, par, :], t["b1"][bass.ds(e, 1)].rearrange("a p c -> p (a c)")
                     ).then_inc(self.loaded[par], 16)

    def split(self, pool, e, par, turn, used=None):
        pool.wait_ge(self.consts_in, 16 * 5)
        pool.wait_ge(self.loaded[par], 48 * (turn + 1))
        if used is not None:
            pool.wait_ge(used, B * (e - 1))
        pool.tensor_copy(self.pickw[:, par, :], self.pick[:, bass.ds(e, 1), :].rearrange("p a j -> p (a j)")
                         ).then_inc(self.picked, 1)
        pool.tensor_copy(self.w1h[:, par, :], self.w1[:, par, :]).then_inc(self.high, 1)
        pool.wait_ge(self.high, 2 * e + 1)
        pool.tensor_tensor(self.w1l[:, par, :], self.w1[:, par, :], self.w1h[:, par, :].bitcast(F32),
                           ALU.subtract).then_inc(self.split_done, 1)
        pool.tensor_copy(self.w2h[:, par, :, :], self.w2[:, par, :, :]).then_inc(self.high, 1)
        pool.wait_ge(self.high, 2 * e + 2)
        pool.tensor_tensor(self.w2l[:, par, :, :], self.w2[:, par, :, :], self.w2h[:, par, :, :].bitcast(F32),
                           ALU.subtract).then_inc(self.split_done, 1)


def experts(nc, t, ident, epsc, x2T, x2Th, x2Tl, w, psum, out):
    with ExitStack() as ctx:
        def sb(name, shape, dt=F32):
            return ctx.enter_context(nc.sbuf_tensor(name, shape, dt))

        def sem(name):
            return ctx.enter_context(nc.semaphore(name))

        C = HID // P
        STEPS = 2 * B
        HEAD = 3
        pr = sb("gate_p", [P, NT, E])
        left = sb("gate_left", [P, NT, E])
        hit = sb("gate_hit", [P, NT, E])
        sel = sb("gate_sel", [P, NT, E])
        selh = sb("gate_selh", [P, NT, E], F32R)
        selp = sb("gate_selp", [P, NT, 2 * E])
        m = sb("gate_m", [P, NT])
        selS = sb("selS", [P, B * S], F32R)
        accT = x2T[:].rearrange("p (b i) -> p b i", b=B)
        part = sb("part", [P, 2, S])
        share = sb("share", [P, 2, S])
        hf = sb("hf", [P, C, S])
        hh = sb("hh", [P, 2, C, S], F32R)
        hl = sb("hl", [P, 2, C, S], F32R)
        fin = sb("final", [P, NT, D])
        st = sb("st3", [P, NT, 6])
        mv = sb("mv3", [P, NT, 2])
        rstd = sb("rstd3", [P, NT])

        names = ["zeroed", "gate_step", "gate_exp", "sel_ps", "selS", "share_ps", "share",
                 "hidden_ps", "gelu", "gelu_high", "gelu_low", "out_ps", "weighted",
                 "acc", "accT_ps", "st", "mv", "sq", "rstd", "final", "stored"]
        s = {n: ctx.enter_context(nc.semaphore("e_" + n)) for n in names}
        bankY, bankW = 4, 6
        PAIRS = E // 2

        weight = psum[:, bankW:bankW + 2, :]

        with nc.Block() as block:
            @block.sync
            def _(sp):
                with sp.Fori(1, PAIRS) as p:
                    for par in range(2):
                        sp.wait_ge(w.loaded[par], 48)
                        sp.wait_ge(s["gelu_high"], B * C * (2 * p + par - 1))
                        w.load(sp, t, 2 * p + par, par)
                for b in range(B):
                    sp.wait_ge(s["final"], QB * (b + 1))
                    sp.dma_start(out[b].rearrange("(t p) d -> p t d", p=P),
                                 fin[:, QB * b:QB * b + QB, :]).then_inc(s["stored"], 16)
                sp.wait_ge(s["stored"], 16 * B)

            @block.gpsimd
            def _(pool):
                pool.memset(selS[:].bitcast(F32), 0.0).then_inc(s["zeroed"], 1)
                with pool.Fori(1, PAIRS) as p:
                    for par in range(2):
                        w.split(pool, 2 * p + par, par, p, used=s["out_ps"])

            @block.scalar
            def _(act):
                act.wait_ge(s["gate_step"], 3)
                act.activation(pr[:], pr[:], ACT.Exp).then_inc(s["gate_exp"], 1)

                def hidden(p, k):
                    par = k // B
                    if k % B == 0:
                        act.wait_ge(w.loaded[par], 48 * (p + 1))
                    for c in range(C):
                        n = C * (STEPS * p + k) + c
                        act.wait_ge(s["hidden_ps"], n + 1)
                        if k or not first(p):
                            act.wait_ge(s["gelu_low"], n + 1 - C)
                        act.activation(hf[:, c, :], psum[:, c, :], ACT.Gelu_apprx_tanh,
                                       bias=w.b1[:, par, c:c + 1]).then_inc(s["gelu"], 1)
                        if c == 0 and (k >= 2 or not first(p)):
                            act.wait_ge(s["out_ps"], STEPS * p + k - 1)
                        act.activation(hh[:, k % 2, c, :], psum[:, c, :], ACT.Gelu_apprx_tanh,
                                       bias=w.b1[:, par, c:c + 1]).then_inc(s["gelu_high"], 1)

                hidden(0, 0)
                hidden(0, 1)
                act.wait_ge(s["zeroed"], 1)
                for b in range(B):
                    act.wait_ge(s["sel_ps"], b + 1)
                    act.activation(selS[0:2 * E, b * S:(b + 1) * S], psum[0:2 * E, SEL_BANK[b], :],
                                   ACT.Copy).then_inc(s["selS"], 1)
                for k in range(2, HEAD):
                    hidden(0, k)
                with act.Fori(0, PAIRS - 1) as p:
                    for k in range(HEAD, STEPS):
                        hidden(p, k)
                    for k in range(HEAD):
                        hidden(p + 1, k)
                for k in range(HEAD, STEPS):
                    hidden(PAIRS - 1, k)
                for part in (slice(0, NT - QB), slice(NT - QB, NT)):
                    act.wait_ge(s["mv"], part.stop)
                    act.activation(rstd[:, part], mv[:, part, 1], ACT.Sqrt, bias=epsc[:, 0:1]).then_inc(s["sq"], 1)

            @block.vector
            def _(v):
                step = [0]

                def link(ins):
                    step[0] += 1
                    ins.then_inc(s["gate_step"], 1)
                    if step[0] in MEANWHILE:
                        low_chunk(0, 0, MEANWHILE.index(step[0]))
                    v.wait_ge(s["gate_step"], step[0])

                def per_tile(a):
                    return a.rearrange("p (t a) -> p t a", a=1).to_broadcast([P, NT, E])

                def all_tiles(a):
                    return a.rearrange("p (a e) -> p a e", a=1).to_broadcast([P, NT, E])

                def low_chunk(p, k, c):
                    v.wait_ge(s["gelu_high"], C * (STEPS * p + k) + c + 1)
                    v.tensor_tensor(hl[:, k % 2, c, :], hf[:, c, :], hh[:, k % 2, c, :].bitcast(F32),
                                    ALU.subtract).then_inc(s["gelu_low"], 1)

                def low(p, k):
                    for c in range(C):
                        low_chunk(p, k, c)

                v.wait_ge(w.consts_in, 16 * 5)
                v.wait_ge(w.logits, 1)
                link(v.tensor_tensor(pr[:], psum[:, 0, 0:NT * E].rearrange("p (t e) -> p t e", e=E),
                                     all_tiles(w.bg[:]), ALU.add))
                link(v.tensor_reduce(m[:], pr[:], AX_X, ALU.max))
                link(v.tensor_tensor(pr[:], pr[:], per_tile(m[:]), ALU.subtract))
                choose(v, link, s["gate_exp"], pr, left, hit, sel, m, w.order, per_tile, all_tiles)
                link(v.tensor_copy(selh[:], sel[:]))
                link(v.tensor_copy(selp[:, :, 0:E], selh[:].bitcast(F32)))
                link(v.tensor_tensor(selp[:, :, E:2 * E], sel[:], selh[:].bitcast(F32), ALU.subtract))

                def add(p, k):
                    b = k % B
                    v.wait_ge(s["out_ps"], STEPS * p + k + 1)
                    v.wait_ge(s["share"], STEPS * p + k + 1)
                    v.scalar_tensor_tensor(part[:, k % 2, :], psum[:, bankY + k % 2, :],
                                           w.b2[:, bass.ds(2 * p + k // B, 1)], share[:, k % 2, :],
                                           ALU.add, ALU.mult).then_inc(s["weighted"], 1)
                    v.wait_ge(s["weighted"], STEPS * p + k + 1)
                    v.tensor_tensor(accT[:, b, :], accT[:, b, :], part[:, k % 2, :], ALU.add).then_inc(s["acc"], 1)

                def bring(p, k):
                    v.wait_ge(s["share_ps"], STEPS * p + k + 1)
                    v.tensor_copy(share[:, k % 2, :], weight[:, k % 2, :]).then_inc(s["share"], 1)

                def slot(p, k):
                    low(p, k)
                    if k:
                        bring(p, k - 1)
                        add(p, k - 1)
                    elif not first(p):
                        bring(p - 1, STEPS - 1)
                        add(p - 1, STEPS - 1)

                for k in range(1, HEAD):
                    slot(0, k)
                with v.Fori(0, PAIRS - 1) as p:
                    for k in range(HEAD, STEPS):
                        slot(p, k)
                    for k in range(HEAD):
                        slot(p + 1, k)
                for k in range(HEAD, STEPS):
                    slot(PAIRS - 1, k)

                def stats(b):
                    v.wait_ge(s["accT_ps"], b + 1)
                    for i in range(QB * b, QB * b + QB):
                        v.bn_stats(st[:, i, :], psum[:, b, i % QB * P:(i % QB + 1) * P]).then_inc(s["st"], 1)

                def means(tiles):
                    v.wait_ge(s["st"], tiles.stop)
                    for i in range(tiles.start, tiles.stop):
                        v.bn_aggr(mv[:, i, :], st[:, i, :]).then_inc(s["mv"], 1)

                def normalise(n, tiles):
                    v.wait_ge(s["sq"], n)
                    v.reciprocal(rstd[:, tiles], rstd[:, tiles]).then_inc(s["rstd"], 1)
                    v.wait_ge(s["rstd"], n)
                    for i in range(tiles.start, tiles.stop):
                        v.tensor_scalar(fin[:, i, :], psum[:, i // QB, i % QB * P:(i % QB + 1) * P],
                                        mv[:, i, 0:1], rstd[:, i:i + 1], ALU.subtract,
                                        ALU.mult).then_inc(s["final"], 1)

                others, last = slice(0, NT - QB), slice(NT - QB, NT)
                for b in range(B - 1):
                    stats(b)
                means(others)
                bring(PAIRS - 1, STEPS - 1)
                add(PAIRS - 1, STEPS - 1)
                normalise(1, others)
                stats(B - 1)
                means(last)
                normalise(2, last)

            @block.tensor
            def _(pe):
                def hidden(p, k, c):
                    par, b = k // B, k % B
                    n = C * (STEPS * p + k) + c
                    if b == 0 and c == 0:
                        pe.wait_ge(w.split_done, 2 * (2 * p + par) + 1)
                    if k or not first(p):
                        pe.wait_ge(s["gelu_high"], n + 1 - C)
                    parts = (w.w1h, w.w1l), (x2Th, x2Tl)
                    for a, x in PASSES:
                        last = pe.matmul(psum[:, c, :], parts[0][a][:, par, c * P:(c + 1) * P],
                                         parts[1][x][:, b * S:(b + 1) * S], start=(a, x) == PASSES[0],
                                         stop=(a, x) == PASSES[-1])
                    last.then_inc(s["hidden_ps"], 1)

                def down(p, k, c):
                    par, b = k // B, k % B
                    n = C * (STEPS * p + k) + c
                    if c == 0:
                        if b == 0:
                            pe.wait_ge(w.split_done, 2 * (2 * p + par) + 2)
                        if k >= 2 or not first(p):
                            pe.wait_ge(s["weighted"], STEPS * p + k - 1)
                    if c == C - 1:
                        if b == 0:
                            pe.wait_ge(w.picked, 2 * p + par + 1)
                        pe.matmul(weight[:, k % 2, :], w.pickw[:, par, :], selS[:, b * S:(b + 1) * S],
                                  start=True, stop=True).then_inc(s["share_ps"], 1)
                    pe.wait_ge(s["gelu_low"], n + 1)
                    parts = (w.w2h, w.w2l), (hh, hl)
                    for a, x in PASSES:
                        last = pe.matmul(psum[:, bankY + k % 2, :], parts[0][a][:, par, c, :],
                                         parts[1][x][:, k % 2, c, :], start=c == 0 and (a, x) == PASSES[0],
                                         stop=c == C - 1 and (a, x) == PASSES[-1])
                    if c == C - 1:
                        last.then_inc(s["out_ps"], 1)

                pe.wait_ge(s["gate_step"], 1)
                for c in range(C):
                    hidden(0, 0, c)

                def turn_sel():
                    pe.wait_ge(s["gate_step"], GATE_STEPS)
                    for b in range(B):
                        if b == 3:
                            pe.wait_ge(s["selS"], 1)
                        for q in range(QB):
                            last = pe.transpose(psum[0:2 * E, SEL_BANK[b], q * P:(q + 1) * P],
                                                selp[:, QB * b + q, :], ident[:])
                        last.then_inc(s["sel_ps"], 1)
                    pe.wait_ge(s["selS"], B)

                def slot(p, k):
                    for c in range(C):
                        hidden(p, k, c)
                        if k:
                            down(p, k - 1, c)
                        elif not first(p):
                            down(p - 1, STEPS - 1, c)

                for c in range(C):
                    hidden(0, 1, c)
                    if c == C - 1:
                        turn_sel()
                    down(0, 0, c)
                for k in range(2, HEAD):
                    slot(0, k)
                with pe.Fori(0, PAIRS - 1) as p:
                    for k in range(HEAD, STEPS):
                        slot(p, k)
                    for k in range(HEAD):
                        slot(p + 1, k)
                for k in range(HEAD, STEPS):
                    slot(PAIRS - 1, k)
                def turn_sum(b):
                    pe.wait_ge(s["acc"], E * B - B + b + 1)
                    pe.wait_ge(s["gelu_high"], C * (E * B - 1) + b + 1)
                    for q in range(QB):
                        last = pe.transpose(psum[:, b, q * P:(q + 1) * P], accT[:, b, q * P:(q + 1) * P], ident[:])
                    last.then_inc(s["accT_ps"], 1)

                for c in range(C):
                    down(PAIRS - 1, STEPS - 1, c)
                    if c < B - 1:
                        turn_sum(c)
                turn_sum(B - 1)


GATE_STEPS = 28
MEANWHILE = 14, 18, 22, 26
SEL_BANK = 5, 6, 7, 5


def choose(v, link, gexp, pr, left, hit, sel, m, order, per_tile, all_tiles):
    v.wait_ge(gexp, 1)
    link(v.tensor_reduce(m[:], pr[:], AX_X, ALU.add))
    link(v.reciprocal(m[:], m[:]))
    link(v.tensor_tensor(pr[:], pr[:], per_tile(m[:]), ALU.mult))
    link(v.tensor_copy(left[:], pr[:]))
    for n in range(2):
        link(v.tensor_reduce(m[:], left[:], AX_X, ALU.max))
        link(v.tensor_tensor(hit[:], left[:], per_tile(m[:]), ALU.is_ge))
        link(v.tensor_tensor(hit[:], hit[:], all_tiles(order[:]), ALU.mult))
        link(v.tensor_reduce(m[:], hit[:], AX_X, ALU.max))
        link(v.tensor_tensor(hit[:], all_tiles(order[:]), per_tile(m[:]), ALU.is_equal))
        link(v.scalar_tensor_tensor(left[:], hit[:], -2.0, left[:], ALU.mult, ALU.add))
    link(v.tensor_scalar(hit[:], left[:], 0.0, None, ALU.is_lt))
    link(v.tensor_tensor(sel[:], pr[:], hit[:], ALU.mult))
    link(v.tensor_reduce(m[:], sel[:], AX_X, ALU.add))
    link(v.tensor_scalar(m[:], m[:], 1e-8, None, ALU.add))
    link(v.reciprocal(m[:], m[:]))
    link(v.tensor_tensor(sel[:], sel[:], per_tile(m[:]), ALU.mult))


def in_bands(a):
    a = np.asarray(a)
    out = np.zeros(a.shape[:-1] + (HG, 4, BAND), a.dtype)
    src = a.reshape(a.shape[:-1] + (HG, 4, HD))
    for k in range(3):
        out[..., k * HD:(k + 1) * HD] = src
    return out.reshape(a.shape[:-1] + (HG, P))


def shape_constants():
    f32 = np.float32
    inv = f32(1.0) / np.power(f32(10000.0), np.arange(0, D, 2, dtype=f32) / f32(D))
    w = np.repeat(inv.astype(f32).astype(np.float64), 2)[:, None]
    odd = (np.arange(D) % 2 == 1)[:, None]
    j = np.arange(S)[None, :]

    def table(pos):
        return np.where(odd, np.cos(pos * w), np.sin(pos * w))
    turn = (S - 1 - j) * w
    tabs = np.stack([table(j), table(j - S)], axis=1)
    cs = np.stack([np.cos(turn), np.where(odd, np.sin(turn), -np.sin(turn))], axis=1)
    row = np.arange(P)[:, None]
    in_band = row % BAND // HD
    negc = np.concatenate([-(in_band == 2).astype(f32), -(in_band == 1).astype(f32)], axis=1)
    col = np.arange(S)[None, :]
    return {
        "ident": np.eye(P, dtype=f32), "negc": negc, "tabs": tabs.astype(f32), "cs": cs.astype(f32),
        "peS": table(np.array([[S]])).astype(f32), "bandm": (row // BAND == np.arange(4)[None, :]).astype(f32),
        "maskU": (col >= row + 2).astype(np.uint32), "maskS": (col == row + 1)[:, 0:ZONE].astype(f32),
        "pick": np.where((row < 2 * E)[:, :, None] & (row % E == np.arange(E)[None, :])[:, :, None],
                         np.ones((1, 1, P), f32), f32(0)),
        "order": np.tile(np.arange(E, 0, -1, dtype=f32), (P, 1)),
    }


def kernel(x, ctx_1024, L0_attn_Wq, L0_attn_bq, L0_attn_Wk, L0_attn_bk, L0_attn_Wv, L0_attn_bv, L0_attn_Wpos,
           L0_attn_Wf, L0_attn_bf, L0_attn_u, L0_attn_v, L0_attn_gamma, L0_attn_beta, L0_xattn_wq, L0_xattn_wk,
           L0_xattn_wv, L0_xattn_wo, L0_xattn_bo, L0_ffn_Wg, L0_ffn_bg, L0_ffn_W1, L0_ffn_b1, L0_ffn_W2,
           L0_ffn_b2):
    import concourse.bacc as bacc
    from concourse.bass_utils import run_bass_kernel_spmd

    A = np.asarray
    wq, wk = (in_bands(w).transpose(1, 0, 2) for w in (L0_attn_Wq, L0_attn_Wk))
    cols = [in_bands(A(c).reshape(D))[:, :, None] for c in (L0_attn_bq, L0_attn_bk, L0_attn_u, L0_attn_v)]
    posC = in_bands(L0_attn_Wpos).transpose(1, 0, 2)
    posT = posC.transpose(0, 2, 1)
    swapped = posT.reshape(HG, P, D // 2, 2)[..., ::-1].reshape(HG, P, D)
    arrays = {
        "x": x, "ctx": ctx_1024, "wst": np.concatenate([wq, wk] + cols, axis=2),
        "wposT": np.stack([posT, swapped], axis=1), "wposC": posC,
        "gb": np.stack([A(L0_attn_gamma), A(L0_attn_beta)], axis=1),
        "wv": L0_attn_Wv, "bv": A(L0_attn_bv).reshape(1, D), "wf": L0_attn_Wf, "bf": A(L0_attn_bf).reshape(1, D),
        "wq2": in_bands(A(L0_xattn_wq).T).transpose(1, 0, 2), "wk2": in_bands(A(L0_xattn_wk).T).transpose(1, 0, 2),
        "wv2": A(L0_xattn_wv).T, "wo2": A(L0_xattn_wo).T, "bo": A(L0_xattn_bo).reshape(1, D),
        "wg": L0_ffn_Wg, "bg": A(L0_ffn_bg).reshape(1, E), "w1": L0_ffn_W1,
        "b1": A(L0_ffn_b1).reshape(E, HID // P, P).transpose(0, 2, 1), "w2": L0_ffn_W2, "b2": A(L0_ffn_b2).T,
    }
    arrays.update(shape_constants())
    nc = bacc.Bacc("TRN2", target_bir_lowering=False, num_devices=1)
    feed, t = {}, {}
    for name, a in arrays.items():
        a = np.ascontiguousarray(a)
        feed[f"in_{name}"] = a
        t[name] = nc.dram_tensor(f"in_{name}", a.shape, mybir.dt.from_np(a.dtype), kind="ExternalInput").ap()
    out = nc.dram_tensor("out_0", (B, S, D), F32, kind="ExternalOutput").ap()
    decoder_kernel(nc, t, out)
    r = run_bass_kernel_spmd(nc, [feed], core_ids=[0])
    return r.results[0]["out_0"]
```
